# Optimizing a Trainium2 kernel written in Bass

```python
import numpy as np
import jax
import jax.numpy as jnp

def _softmax(x, axis=-1):
    return jax.nn.softmax(x, axis=axis)

def _gelu(x):
    return jax.nn.gelu(x, approximate=True)

def _silu(x):
    return jax.nn.silu(x)

def _sigmoid(x):
    return jax.nn.sigmoid(x)

def _layernorm(x, axis=-1, eps=1e-05):
    m = jnp.mean(x, axis=axis, keepdims=True)
    v = jnp.var(x, axis=axis, keepdims=True)
    return (x - m) / jnp.sqrt(v + eps)

def _scatter_add(tgt, idx, src, axis=0):
    return tgt.at[idx].add(src)

def _segment_sum(src, seg, n):
    return jax.ops.segment_sum(src, seg, n)
kernel_name = 'mk_sandwich_d1_jaxref_r4_19a851'

def setup_inputs(seed: int=0):
    np.random.seed(seed)
    _w = jnp.asarray

    def _L0_attn_setup():
        import jax, jax.numpy as jnp
        import numpy as np
        B, T, C = (8, 256, 512)
        NEG_BIG = -1e+38

        def rwkv_linear_attention(time_decay, time_first, k, v):
            w = -jnp.exp(time_decay)
            u = time_first
            num0 = jnp.zeros(k.shape[::2], dtype=jnp.float32)
            den0 = jnp.zeros_like(num0)
            max0 = jnp.full_like(num0, NEG_BIG)

            def step(carry, kv_t):
                num, den, mx = carry
                kt, vt = kv_t
                mo = jnp.maximum(mx, kt + u)
                e1 = jnp.exp(mx - mo)
                e2 = jnp.exp(kt + u - mo)
                out = (e1 * num + e2 * vt) / (e1 * den + e2)
                ms = jnp.maximum(mx + w, kt)
                e1s = jnp.exp(mx + w - ms)
                e2s = jnp.exp(kt - ms)
                return ((e1s * num + e2s * vt, e1s * den + e2s, ms), out)
            kT = jnp.swapaxes(k, 0, 1).astype(jnp.float32)
            vT = jnp.swapaxes(v, 0, 1).astype(jnp.float32)
            _, outT = jax.lax.scan(step, (num0, den0, max0), (kT, vT))
            return jnp.swapaxes(outT, 0, 1).astype(k.dtype)
        key = jax.random.key(seed)
        ks = jax.random.split(key, 10)
        s = 0.02
        return {'x': jax.random.normal(ks[0], (B, T, C), dtype=jnp.float32), 'time_decay': jax.random.normal(ks[1], (C,), dtype=jnp.float32) * 0.5, 'time_first': jax.random.normal(ks[2], (C,), dtype=jnp.float32) * 0.5, 'time_mix_k': jax.random.uniform(ks[3], (1, 1, C), dtype=jnp.float32), 'time_mix_v': jax.random.uniform(ks[4], (1, 1, C), dtype=jnp.float32), 'time_mix_r': jax.random.uniform(ks[5], (1, 1, C), dtype=jnp.float32), 'Wk': jax.random.normal(ks[6], (C, C), dtype=jnp.float32) * s, 'Wv': jax.random.normal(ks[7], (C, C), dtype=jnp.float32) * s, 'Wr': jax.random.normal(ks[8], (C, C), dtype=jnp.float32) * s, 'Wo': jax.random.normal(ks[9], (C, C), dtype=jnp.float32) * s}
    _L0_attn_in = _L0_attn_setup()

    def _L0_ffn_setup():
        import jax, jax.numpy as jnp
        import numpy as np
        E = 64
        K = 6
        NG = 8
        TKG = 4
        SCALE = 2.5
        CAP = 128

        def _router(x, gate_w, e_bias):
            logits = x.astype(jnp.float32) @ gate_w.T
            scores = jax.nn.sigmoid(logits)
            sc = scores + e_bias[None, :]
            T = x.shape[0]
            gs = sc.reshape(T, NG, E // NG)
            grp_score = jax.lax.top_k(gs, 2)[0].sum(-1)
            _, gidx = jax.lax.top_k(grp_score, TKG)
            gmask = jax.nn.one_hot(gidx, NG, dtype=sc.dtype).sum(1)
            emask = jnp.repeat(gmask, E // NG, axis=1)
            masked = jnp.where(emask > 0, sc, -jnp.inf)
            _, idx = jax.lax.top_k(masked, K)
            w = jnp.take_along_axis(scores, idx, axis=1)
            w = w / (w.sum(-1, keepdims=True) + 1e-20) * SCALE
            return (idx, w)

        def _relu2(h):
            return jnp.square(jax.nn.relu(h))

        def _moe(x, idx, w, w1, w2):
            T, D = x.shape
            e_flat = idx.reshape(-1)
            tok = jnp.repeat(jnp.arange(T), K)
            oh = jax.nn.one_hot(e_flat, E, dtype=jnp.float32)
            pos = jnp.cumsum(oh, axis=0) - oh
            pos = (pos * oh).sum(-1).astype(jnp.int32)
            keep = pos < CAP
            slot = jnp.where(keep, pos, CAP)
            xd = jnp.zeros((E, CAP + 1, D), x.dtype).at[e_flat, slot].set(x[tok])
            h = _relu2(jnp.einsum('ecd,eid->eci', xd, w1))
            yd = jnp.einsum('eci,edi->ecd', h, w2)
            gate = w.reshape(-1)[:, None] * keep[:, None].astype(x.dtype)
            y_assign = yd[e_flat, slot] * gate
            return jnp.zeros((T, D), x.dtype).at[tok].add(y_assign)
        key = jax.random.key(seed)
        ks = jax.random.split(key, 6)
        D, I, SH, T = (512, 256, 1024, 512)
        x = jax.random.normal(ks[0], (1, T, D), jnp.float32)
        gate_w = jax.random.normal(ks[1], (E, D), jnp.float32) * D ** (-0.5)
        e_bias = jnp.zeros((E,), jnp.float32)
        w1 = jax.random.normal(ks[2], (E, I, D), jnp.float32) * D ** (-0.5)
        w2 = jax.random.normal(ks[3], (E, D, I), jnp.float32) * I ** (-0.5)
        su = jax.random.normal(ks[4], (SH, D), jnp.float32) * D ** (-0.5)
        sd = jax.random.normal(ks[5], (D, SH), jnp.float32) * SH ** (-0.5)
        return {'hidden_states': x, 'gate_w': gate_w, 'e_bias': e_bias, 'w1': w1, 'w2': w2, 'shared_up_w': su, 'shared_down_w': sd}
    _L0_ffn_in = _L0_ffn_setup()
    _d = {'L0_attn_x': _L0_attn_in['x'], 'L0_attn_time_decay': _L0_attn_in['time_decay'], 'L0_attn_time_first': _L0_attn_in['time_first'], 'L0_attn_time_mix_k': _L0_attn_in['time_mix_k'], 'L0_attn_time_mix_v': _L0_attn_in['time_mix_v'], 'L0_attn_time_mix_r': _L0_attn_in['time_mix_r'], 'L0_attn_Wk': _L0_attn_in['Wk'], 'L0_attn_Wv': _L0_attn_in['Wv'], 'L0_attn_Wr': _L0_attn_in['Wr'], 'L0_attn_Wo': _L0_attn_in['Wo'], 'L0_ffn_gate_w': _L0_ffn_in['gate_w'], 'L0_ffn_e_bias': _L0_ffn_in['e_bias'], 'L0_ffn_w1': _L0_ffn_in['w1'], 'L0_ffn_w2': _L0_ffn_in['w2'], 'L0_ffn_shared_up_w': _L0_ffn_in['shared_up_w'], 'L0_ffn_shared_down_w': _L0_ffn_in['shared_down_w']}
    _x0 = _d['L0_attn_x']
    _d['L0_attn_x'] = jax.random.normal(jax.random.fold_in(jax.random.key(seed), 1), (4, 1024, 512), dtype=_x0.dtype)
    del _x0
    return _d

def reference(L0_attn_x, L0_attn_time_decay, L0_attn_time_first, L0_attn_time_mix_k, L0_attn_time_mix_v, L0_attn_time_mix_r, L0_attn_Wk, L0_attn_Wv, L0_attn_Wr, L0_attn_Wo, L0_ffn_gate_w, L0_ffn_e_bias, L0_ffn_w1, L0_ffn_w2, L0_ffn_shared_up_w, L0_ffn_shared_down_w):

    def _L0_attn_ref(x, time_decay, time_first, time_mix_k, time_mix_v, time_mix_r, Wk, Wv, Wr, Wo):
        import jax, jax.numpy as jnp
        import numpy as np
        B, T, C = (8, 256, 512)
        NEG_BIG = -1e+38

        def rwkv_linear_attention(time_decay, time_first, k, v):
            w = -jnp.exp(time_decay)
            u = time_first
            num0 = jnp.zeros(k.shape[::2], dtype=jnp.float32)
            den0 = jnp.zeros_like(num0)
            max0 = jnp.full_like(num0, NEG_BIG)

            def step(carry, kv_t):
                num, den, mx = carry
                kt, vt = kv_t
                mo = jnp.maximum(mx, kt + u)
                e1 = jnp.exp(mx - mo)
                e2 = jnp.exp(kt + u - mo)
                out = (e1 * num + e2 * vt) / (e1 * den + e2)
                ms = jnp.maximum(mx + w, kt)
                e1s = jnp.exp(mx + w - ms)
                e2s = jnp.exp(kt - ms)
                return ((e1s * num + e2s * vt, e1s * den + e2s, ms), out)
            kT = jnp.swapaxes(k, 0, 1).astype(jnp.float32)
            vT = jnp.swapaxes(v, 0, 1).astype(jnp.float32)
            _, outT = jax.lax.scan(step, (num0, den0, max0), (kT, vT))
            return jnp.swapaxes(outT, 0, 1).astype(k.dtype)
        shifted = jnp.pad(x, ((0, 0), (1, 0), (0, 0)))[:, :-1]
        xk = x * time_mix_k + shifted * (1 - time_mix_k)
        xv = x * time_mix_v + shifted * (1 - time_mix_v)
        xr = x * time_mix_r + shifted * (1 - time_mix_r)
        k = jnp.einsum('btc,dc->btd', xk, Wk)
        v = jnp.einsum('btc,dc->btd', xv, Wv)
        r = jnp.einsum('btc,dc->btd', xr, Wr)
        sr = jax.nn.sigmoid(r)
        rwkv = sr * rwkv_linear_attention(time_decay, time_first, k, v)
        return jnp.einsum('btd,cd->btc', rwkv, Wo)

    def _L0_ffn_ref(hidden_states, gate_w, e_bias, w1, w2, shared_up_w, shared_down_w):
        import jax, jax.numpy as jnp
        import numpy as np
        E = 64
        K = 6
        NG = 8
        TKG = 4
        SCALE = 2.5
        CAP = 128

        def _router(x, gate_w, e_bias):
            logits = x.astype(jnp.float32) @ gate_w.T
            scores = jax.nn.sigmoid(logits)
            sc = scores + e_bias[None, :]
            T = x.shape[0]
            gs = sc.reshape(T, NG, E // NG)
            grp_score = jax.lax.top_k(gs, 2)[0].sum(-1)
            _, gidx = jax.lax.top_k(grp_score, TKG)
            gmask = jax.nn.one_hot(gidx, NG, dtype=sc.dtype).sum(1)
            emask = jnp.repeat(gmask, E // NG, axis=1)
            masked = jnp.where(emask > 0, sc, -jnp.inf)
            _, idx = jax.lax.top_k(masked, K)
            w = jnp.take_along_axis(scores, idx, axis=1)
            w = w / (w.sum(-1, keepdims=True) + 1e-20) * SCALE
            return (idx, w)

        def _relu2(h):
            return jnp.square(jax.nn.relu(h))

        def _moe(x, idx, w, w1, w2):
            T, D = x.shape
            e_flat = idx.reshape(-1)
            tok = jnp.repeat(jnp.arange(T), K)
            oh = jax.nn.one_hot(e_flat, E, dtype=jnp.float32)
            pos = jnp.cumsum(oh, axis=0) - oh
            pos = (pos * oh).sum(-1).astype(jnp.int32)
            keep = pos < CAP
            slot = jnp.where(keep, pos, CAP)
            xd = jnp.zeros((E, CAP + 1, D), x.dtype).at[e_flat, slot].set(x[tok])
            h = _relu2(jnp.einsum('ecd,eid->eci', xd, w1))
            yd = jnp.einsum('eci,edi->ecd', h, w2)
            gate = w.reshape(-1)[:, None] * keep[:, None].astype(x.dtype)
            y_assign = yd[e_flat, slot] * gate
            return jnp.zeros((T, D), x.dtype).at[tok].add(y_assign)
        orig = hidden_states.shape
        x = hidden_states.reshape(-1, orig[-1])
        idx, wts = _router(x, gate_w, e_bias)
        shared = _relu2(x @ shared_up_w.T) @ shared_down_w.T
        routed = _moe(x, idx, wts.astype(x.dtype), w1, w2)
        return (shared + routed).reshape(orig)
    x = L0_attn_x
    x = x + _layernorm(_L0_attn_ref(_layernorm(x, axis=-1), L0_attn_time_decay, L0_attn_time_first, L0_attn_time_mix_k, L0_attn_time_mix_v, L0_attn_time_mix_r, L0_attn_Wk, L0_attn_Wv, L0_attn_Wr, L0_attn_Wo), axis=-1)
    x = x + _layernorm(_L0_ffn_ref(_layernorm(x, axis=-1), L0_ffn_gate_w, L0_ffn_e_bias, L0_ffn_w1, L0_ffn_w2, L0_ffn_shared_up_w, L0_ffn_shared_down_w), axis=-1)
    return x

_drawn_inputs = setup_inputs


def setup_inputs(seed=0):
    import zlib

    import numpy as np

    out = dict(_drawn_inputs(seed))
    spreads = {'L0_ffn_e_bias': (0.0, 0.1)}
    factors = {}
    for name, (base, spread) in spreads.items():
        noise = np.random.default_rng([zlib.crc32(name.encode()), seed]).standard_normal(out[name].shape)
        drawn = base * np.exp(spread * noise) if base else spread * noise
        out[name] = jnp.asarray(drawn.astype(out[name].dtype))
    for name, factor in factors.items():
        out[name] = (out[name] * factor).astype(out[name].dtype)
    return out
```

```python
import concourse.bass as bass
from concourse import mybir
from contextlib import ExitStack

F32 = mybir.dt.float32
F32R = mybir.dt.float32r
BF16 = mybir.dt.bfloat16
I32 = mybir.dt.int32
U32 = mybir.dt.uint32
ALU = mybir.AluOpType
ACT = mybir.ActivationFunctionType
AX = mybir.AxisListType

P = 128
C = 512
CK = C // P
B, T = 4, 1024
N = B * T
TT = 512
ST = TT // P
NT = N // TT
EPS = 1e-5
NEG_BIG = -1e38
E, GROUPS, TOPG, TOPK = 64, 8, 4, 6
EG = E // GROUPS
CAP = 128
HID = 256
SH = 1024
SJ = SH // P
IK = HID // P
ROUTE_SCALE = 2.5
ROW = C + 2
GATE, TOKEN = C, C + 1
FAR = 1e6
LOWEST = 3e38
KJ, VJ, RJ = range(3)


def sandwich(nc, t):
    ctx = ExitStack()
    with ctx:
        def sb(name, shape, dt=F32):
            return ctx.enter_context(nc.sbuf_tensor(name, shape, dt))

        def sem(name):
            return ctx.enter_context(nc.semaphore(name))

        weights = sb("weights", [P, 8, CK * C], F32R)
        mix_hi = sb("mix_hi", [P, 3, TT], F32R)
        mix_lo = sb("mix_lo", [P, 3, TT], F32R)
        rw_hi = sb("rw_hi", [P, CK, TT], F32R)
        rw_lo = sb("rw_lo", [P, CK, TT], F32R)
        xin = sb("xin", [P, ST, C])
        xres = sb("xres", [P, ST, C])
        xnd = sb("xnd", [P, CK, TT])
        xnT = sb("xnT", [P, CK, TT + 1])
        mixf = sb("mixf", [P, 2, TT])
        k_sb = sb("k_sb", [P, 2, CK, TT])
        v_sb = sb("v_sb", [P, CK, TT])
        sr = sb("sr", [P, CK, TT])
        hb = sb("hb", [P, ST, C])
        run_max = sb("run_max", [P, 2, TT + 1])
        state = sb("state", [P, 2, 2, TT + 1])
        wkv = sb("wkv", [P, max(12 * TT, 2 * TOPK * ROW)])

        def unit_pairs(n):
            return wkv[:, 4 * TT * n:4 * TT * (n + 1)].rearrange("p (b e t) -> p b e t", b=2, e=2)

        above = unit_pairs(0)
        below = unit_pairs(1)
        vexp = unit_pairs(2)
        gate_w = sb("gate_w", [P, 2, CK * E], F32R)
        carry = sb("carry", [P, CK, 3])
        vecs = sb("vecs", [P, 8, CK])
        stats = sb("stats", [P, ST, 6])
        mv = sb("mv", [P, 4, ST, 2])
        rstd = sb("rstd", [P, 4, ST])
        neg_half = sb("neg_half", [P, ST])
        ident = sb("ident", [P, P])
        TD, TF, MK, MV, MR, DECAY, NEGW, _ = range(8)

        banks = [ctx.enter_context(nc.psum_tensor(f"bank{g}", [P, 4, 512], F32)) for g in range(2)]

        names = """w_loaded0 w_loaded1 vec_loaded x_loaded xres_loaded x1_stored h_stored
        w_hi w_split decay_ready ident_ready half_ready
        ln1_stats ln1_moments ln1_rstd xn_ready turned xnT_ready shift_ready diff_ready mixed mix_hi_ready mix_lo_ready mix_used
        k_ready v_ready r_ready out_used y_ready
        seeded max_scanned gap_ready clamped carried exped vexped scanned scaled nd_ready recip_ln recip_ready ns_ready a_ready
        resid_ready rw_ready rw_hi_ready rw_lo_ready
        ln2_stats ln2_moments ln2_rstd yn_ready x1_ready ln3_stats ln3_moments ln3_rstd h_ready
        dve_step pool_step
        blank_ready dummy_blank xd_blank ysh_blank
        raw0_loaded raw1_loaded ffn_hi ffn_split gate_loaded gate_hi gate_split bias_loaded
        number_made number_ready causal_ready ones_ready seen_ready token_ready
        h_loaded h_turned h_hi_ready h_lo_ready up_done relu_ready square_ready s_hi_ready s_lo_ready down_done
        yout_ready ysh_stored logits_done score_ready sel_ready pos_ready route_step rows_loaded0 rows_loaded1
        slots_ready scattered0 scattered1
        w1_loaded0 w1_loaded1 w2_loaded0 w2_loaded1 xd_loaded0 xd_loaded1
        xd_turned xdT_ready e_up e_relu e_square e_down e_gated e_index added
        ysh_loaded0 ysh_loaded1 x1_loaded0 x1_loaded1 ln4_stats ln4_moments ln4_rstd o_normed o_ready out_stored""".split()
        S = {n: sem(n) for n in names}

        def W(j, part):
            return weights[:, 2 * j + part, :].rearrange("p (k d) -> p k d", k=CK)

        stage = [hb, sr]

        def flat(tile):
            return tile[:, :, :].rearrange("p a b -> p (a b)")

        su_hi, su_lo, sd_hi, sd_lo = (weights[:, 2 * n:2 * n + 2, :].rearrange("p a b -> p (a b)") for n in range(4))
        su = [w.rearrange("p (k d) -> p k d", k=CK) for w in (su_hi, su_lo)]
        sd = [w.rearrange("p (j c) -> p j c", j=SJ) for w in (sd_hi, sd_lo)]
        gate = [gate_w[:, n, :].rearrange("p (k e) -> p k e", k=CK) for n in range(2)]
        hT_hi, hT_lo, s_hi, s_lo = rw_hi, rw_lo, mix_hi, mix_lo
        relu = k_sb[:, 0, 0:2, :]
        square = k_sb[:, 1, 0:2, :]
        yout = v_sb
        rows = wkv[:, 0:2 * TOPK * ROW].rearrange("p (b k w) -> p b k w", b=2, k=TOPK)
        consts = flat(run_max)
        bias_row = consts[:, 0:E]
        number = consts[:, E:2 * E]
        causal = consts[:, 128:192].bitcast(BF16)
        ones = consts[:, 192:256].bitcast(BF16)
        sel = consts[:, 256:288].bitcast(BF16)
        seen = consts[:, 288:320].bitcast(BF16)
        token = consts[:, 320:321]
        number_i = consts[:, 384:448].bitcast(I32)
        token_i = consts[:, 448:449].bitcast(I32)
        e_token = consts[:, 452:456].bitcast(U32)
        e_gates = consts[:, 456:460]
        scratch = flat(xnd)
        at = [0]

        def carve(*shape, dt=F32):
            n = 1
            for k in shape:
                n *= k
            v = scratch[:, at[0]:at[0] + n]
            at[0] += n
            if dt is not F32:
                v = v.bitcast(dt)
            return v.rearrange("p (a b) -> p a b", a=shape[0]) if len(shape) == 2 else v

        score = carve(2, E)
        biased = carve(E)
        group_top = carve(GROUPS, 8)
        group_score = carve(GROUPS)
        group_best = carve(8)
        group_index = carve(8, dt=U32)
        group_number = carve(8)
        group_hot = carve(TOPG, GROUPS)
        group_mask = carve(GROUPS)
        group_floor = carve(GROUPS)
        masked = carve(E)
        expert_best = carve(8)
        expert_index = carve(8, dt=U32)
        expert_number = carve(8)
        hot = carve(TOPK, E)
        product = carve(TOPK, E)
        sel_f = carve(E)
        weight = carve(TOPK)
        weight_sum = carve(1)
        place = carve(TOPK)
        over = carve(TOPK)
        slot_f = carve(TOPK)
        slot = carve(2, TOPK, dt=U32)

        w1_sb = [hb[:, 2 * b:2 * b + 2, :].rearrange("p a b -> p (a b)").rearrange("p (k i) -> p k i", k=CK) for b in range(2)]
        w2_sb = [sr[:, 2 * b:2 * b + 2, :].rearrange("p a b -> p (a b)").rearrange("p (k c) -> p k c", k=IK) for b in range(2)]
        xd_sb = [flat(xres)[:, b * ROW:(b + 1) * ROW] for b in range(2)]
        xdT = [flat(xnT)[:, b * C:(b + 1) * C].rearrange("p (k n) -> p k n", k=CK) for b in range(2)]
        state_flat = state[:, :, :, :].rearrange("p a b c -> p (a b c)")
        e_hidden = [state_flat[:, b * HID:(b + 1) * HID] for b in range(2)]
        e_act = [state_flat[:, (2 + b) * HID:(3 + b) * HID].rearrange("p (k n) -> p k n", k=IK) for b in range(2)]
        e_out = [mixf[:, b, :] for b in range(2)]
        o_y = [xin, v_sb]
        o_x = [k_sb[:, b, :, :] for b in range(2)]
        x_by_tile = t["x"].rearrange("(t s p) c -> t p s c", s=ST, p=P)
        x1_by_tile = t["x1"].rearrange("(t s p) c -> t p s c", s=ST, p=P)
        h_by_tile = t["h"].rearrange("(t s p) c -> t p s c", s=ST, p=P)

        ysh_by_tile = t["ysh"][0:N, :].rearrange("(t s p) c -> t p s c", s=ST, p=P)
        out_by_tile = t["out"].rearrange("(t s p) c -> t p s c", s=ST, p=P)
        xd_by_expert = t["xd"].rearrange("(e c) w -> e c w", c=CAP)

        def tile_of(ap, tau):
            return ap[bass.ds(tau, 1)].rearrange("o p s c -> p (o s) c")

        def periods(eng, period):
            period(0, 0)
            with eng.Fori(0, (NT - 4) // 2) as i:
                period(2 * i + 1, 1)
                period(2 * i + 2, 0)
            for tau in range(NT - 3, NT):
                period(tau, tau % 2)

        def tiles(eng, tile):
            tile(0)
            with eng.Fori(0, NT - 2) as i:
                tile(i + 1)
            tile(NT - 1)

        def experts(eng, expert):
            for e in range(4):
                expert(e, e, e // 2)
            with eng.Fori(0, (E - 8) // 4) as i:
                for q in range(4):
                    expert(4 * i + 4 + q, q, 2 * i + 2 + q // 2)
            for e in range(E - 4, E):
                expert(e, e % 4, e // 2)

        def finals(eng, final):
            for k in range(2):
                final(k, k, 0)
            with eng.Fori(0, NT // 2 - 1) as i:
                for b in range(2):
                    final(2 * i + 2 + b, b, i + 1)

        def first(n):
            return isinstance(n, int) and n == 0

        def has(tau, ahead):
            return not (isinstance(tau, int) and tau + ahead >= NT)

        def back(tau):
            return not (isinstance(tau, int) and tau == 0)

        def after(eng, sm, value):
            eng.wait_ge(S[sm], value)
            eng.sem_inc(S["dve_step" if eng is dve_engine[0] else "pool_step"], 1)

        dve_engine = [None]
        block = ctx.enter_context(nc.Block())

        @block.sync
        def _(sp):
            for j, name in enumerate(("Wk", "Wv", "Wr", "Wo")):
                if j >= 2:
                    sp.wait_ge(S["w_split"], j - 1)
                sp.dma_start(stage[j % 2][:, :, :], t[name]).then_inc(S[f"w_loaded{j % 2}"], 16)
                if j == 0:
                    sp.dma_start(vecs[:, 0:5, :], t["vecs"]).then_inc(S["vec_loaded"], 16)
                    sp.dma_start(xin[:, :, :], x_by_tile[0]).then_inc(S["x_loaded"], 16)
            sp.wait_ge(S["xn_ready"], ST)
            sp.dma_start(xin[:, :, :], x_by_tile[1]).then_inc(S["x_loaded"], 16)

            def period(tau, par):
                if has(tau, 2):
                    sp.wait_ge(S["xn_ready"], ST * (tau + 2))
                    sp.dma_start(xin[:, :, :], tile_of(x_by_tile, tau + 2)).then_inc(S["x_loaded"], 16)
                if back(tau):
                    store_tail(tau - 1)
                    sp.wait_ge(S["x1_stored"], 16 * tau)
                sp.dma_start(xres[:, :, :], tile_of(x_by_tile, tau)).then_inc(S["xres_loaded"], 16)

            def load_expert(e, b):
                if isinstance(e, int):
                    e1, e2 = t["w1"][e], t["w2"][e]
                else:
                    e1, e2 = (t[w][bass.ds(e, 1)].rearrange("o p k -> p (o k)") for w in ("w1", "w2"))
                sp.dma_start(w1_sb[b].rearrange("p k i -> p (k i)"), e1).then_inc(S[f"w1_loaded{b}"], 16)
                sp.dma_start(w2_sb[b].rearrange("p k i -> p (k i)"), e2).then_inc(S[f"w2_loaded{b}"], 16)

            def store_tail(tau):
                sp.wait_ge(S["h_ready"], ST * (tau + 1))
                sp.dma_start(tile_of(x1_by_tile, tau), xres[:, :, :]).then_inc(S["x1_stored"], 16)
                sp.dma_start(tile_of(h_by_tile, tau), hb[:, :, :]).then_inc(S["h_stored"], 16)

            sp.wait_ge(S["blank_ready"], 2)
            blank = flat(hb)[:, 0:ROW]
            sp.dma_start(t["xd"].rearrange("(e c) w -> c e w", c=CAP),
                         blank.rearrange("p (o w) -> p o w", o=1).to_broadcast([P, E, ROW])).then_inc(S["xd_blank"], 16)
            sp.dma_start(t["ysh"][N:N + P, :], blank[:, 0:C]).then_inc(S["ysh_blank"], 16)

            periods(sp, period)

            raw = [flat(xin), flat(xnd)]
            sp.wait_ge(S["mix_used"], 12 * NT)
            sp.wait_ge(S["mixed"], 12 * NT)
            for q in range(4):
                if q >= 2:
                    sp.wait_ge(S["ffn_split"], q - 1)
                src = t["su"] if q < 2 else t["sd"]
                sp.dma_start(raw[q % 2], src[:, q % 2, :]).then_inc(S[f"raw{q % 2}_loaded"], 16)
                if q == 1:
                    sp.wait_ge(S["carried"], 2 * CK * NT)
                    sp.dma_start(bias_row, t["e_bias"].to_broadcast([P, E])).then_inc(S["bias_loaded"], 16)
                    sp.wait_ge(S["k_ready"], CK * NT)
                    sp.wait_ge(S["gap_ready"], CK * NT)
                    sp.dma_start(flat(k_sb[:, 0, :, :])[:, 0:CK * E], t["gate"]).then_inc(S["gate_loaded"], 16)
            store_tail(NT - 1)
            sp.wait_ge(S["x1_stored"], 16 * NT)
            sp.wait_ge(S["h_stored"], 16 * NT)
            sp.wait_ge(S["rw_lo_ready"], CK * NT)
            sp.wait_ge(S["ffn_split"], 4)
            sp.dma_start(xin[:, :, :], h_by_tile[0]).then_inc(S["h_loaded"], 16)
            for b in range(2):
                load_expert(b, b)
            sp.wait_ge(S["xd_blank"], 16)
            sp.wait_ge(S["ysh_blank"], 16)

            def tile(k):
                if has(k, 1):
                    sp.wait_ge(S["h_turned"], CK * (k + 1))
                    sp.dma_start(xin[:, :, :], tile_of(h_by_tile, k + 1)).then_inc(S["h_loaded"], 16)
                for s in range(ST):
                    if not (first(k) and s < 2):
                        sp.wait_ge(S[f"scattered{s % 2}"], 16 * TOPK * (2 * k + s // 2))
                    src = t["h"].rearrange("(g p) (o c) -> g p o c", p=P, o=1)[bass.ds(ST * k + s, 1)].rearrange("g p o c -> p (g o) c")
                    sp.dma_start(rows[:, s % 2, :, 0:C], src.to_broadcast([P, TOPK, C])).then_inc(S[f"rows_loaded{s % 2}"], 16)
                sp.wait_ge(S["yout_ready"], ST * (k + 1))
                sp.dma_start(tile_of(ysh_by_tile, k), yout[:, :, :]).then_inc(S["ysh_stored"], 16)

            tiles(sp, tile)
            for b in range(2):
                sp.wait_ge(S[f"scattered{b}"], 16 * TOPK * ST * NT // 2)
            sp.wait_ge(S["ysh_stored"], 16 * NT)
            for b in range(2):
                sp.dma_start(xd_sb[b], xd_by_expert[b]).then_inc(S[f"xd_loaded{b}"], 16)

            def expert(e, q, m):
                b = q % 2
                if not (isinstance(e, int) and e + 2 >= E):
                    sp.wait_ge(S["xd_turned"], e + 1)
                    sp.wait_ge(S["e_index"], 2 * e + 2)
                    sp.dma_start(xd_sb[b], xd_by_expert[bass.ds(e + 2, 1)].rearrange("o p w -> p (o w)")).then_inc(S[f"xd_loaded{b}"], 16)
                    sp.wait_ge(S["e_up"], e + 1)
                    sp.wait_ge(S["e_down"], e + 1)
                    load_expert(e + 2, b)

            experts(sp, expert)
            sp.wait_ge(S["added"], 16 * E)

            def load_final(k, b):
                sp.dma_start(o_y[b][:, :, :], tile_of(ysh_by_tile, k)).then_inc(S[f"ysh_loaded{b}"], 16)
                sp.dma_start(o_x[b], tile_of(x1_by_tile, k)).then_inc(S[f"x1_loaded{b}"], 16)

            for b in range(2):
                load_final(b, b)

            def final(k, b, m):
                sp.wait_ge(S["o_ready"], ST * (k + 1))
                sp.dma_start(tile_of(out_by_tile, k), o_y[b][:, :, :]).then_inc(S["out_stored"], 16)
                if not (isinstance(k, int) and k + 2 >= NT):
                    sp.wait_ge(S["out_stored"], 16 * (k + 1))
                    load_final(k + 2, b)

            for k in range(2):
                final(k, k, 0)
            with sp.Fori(0, NT // 2 - 2) as i:
                for b in range(2):
                    final(2 * i + 2 + b, b, i + 1)
            for k in range(NT - 2, NT):
                final(k, k % 2, k // 2)
            sp.wait_ge(S["out_stored"], 16 * NT)

        @block.tensor
        def _(pe):
            def group(tau, job):
                return banks[(1 + tau + job) % 2]

            def transposes(bank, tau):
                pe.wait_ge(S["xn_ready"], ST * (tau + 1))
                for c in range(CK):
                    for s in range(ST):
                        mm = pe.transpose(bank[:, c, s * P:(s + 1) * P], xnd[:, s, c * P:(c + 1) * P], ident[:, :])
                    mm.then_inc(S["turned"], 1)

            def project(bank, tau, j):
                for ck in range(CK):
                    pe.wait_ge(S["mix_lo_ready"], 12 * tau + 4 * j + ck + 1)
                    slot = (4 * j + ck) % 3
                    for d in range(CK):
                        hi = W(j, 0)[:, ck, d * P:(d + 1) * P]
                        lo = W(j, 1)[:, ck, d * P:(d + 1) * P]
                        pe.matmul(bank[:, d, :], hi, mix_hi[:, slot, :], start=(ck == 0), stop=False)
                        pe.matmul(bank[:, d, :], hi, mix_lo[:, slot, :], start=False, stop=False)
                        mm = pe.matmul(bank[:, d, :], lo, mix_hi[:, slot, :], start=False, stop=(ck == CK - 1))
                    mm.then_inc(S["mix_used"], 1)

            def output(bank, tau):
                for ck in range(CK):
                    pe.wait_ge(S["rw_lo_ready"], 4 * tau + ck + 1)
                    for s in range(ST):
                        hi = rw_hi[:, ck, s * P:(s + 1) * P]
                        lo = rw_lo[:, ck, s * P:(s + 1) * P]
                        pe.matmul(bank[:, s, :], hi, W(3, 0)[:, ck, :], start=(ck == 0), stop=False)
                        pe.matmul(bank[:, s, :], hi, W(3, 1)[:, ck, :], start=False, stop=False)
                        mm = pe.matmul(bank[:, s, :], lo, W(3, 0)[:, ck, :], start=False, stop=(ck == CK - 1))
                    mm.then_inc(S["out_used"], 1)

            pe.wait_ge(S["ident_ready"], 2)
            transposes(banks[0], 0)
            pe.wait_ge(S["w_split"], 1)
            project(banks[1], 0, KJ)
            pe.wait_ge(S["xnT_ready"], 4)
            pe.wait_ge(S["w_split"], 2)
            project(banks[0], 0, VJ)
            pe.wait_ge(S["k_ready"], 4)
            pe.wait_ge(S["w_split"], 3)
            project(banks[1], 0, RJ)
            pe.wait_ge(S["v_ready"], 4)
            transposes(banks[0], 1)
            pe.wait_ge(S["w_split"], 4)

            def period(tau, par):
                if has(tau, 1):
                    if back(tau):
                        pe.wait_ge(S["xnT_ready"], 4 * (tau + 2))
                    else:
                        pe.wait_ge(S["r_ready"], 4)
                    project(group(par, 0), tau + 1, KJ)
                    if back(tau):
                        pe.wait_ge(S["y_ready"], 4 * tau)
                    else:
                        pe.wait_ge(S["xnT_ready"], 8)
                    project(group(par, 1), tau + 1, VJ)
                    pe.wait_ge(S["k_ready"], 4 * (tau + 2))
                    project(group(par, 2), tau + 1, RJ)
                if has(tau, 2):
                    pe.wait_ge(S["v_ready"], 4 * (tau + 2))
                    transposes(group(par, 3), tau + 2)
                if has(tau, 1):
                    pe.wait_ge(S["r_ready"], 4 * (tau + 2))
                output(group(par, 4), tau)

            periods(pe, period)

            y_bank, (up_bank, turn_bank, route_bank) = banks[0], (banks[1][:, 0:2, :], banks[1][:, 2, :], banks[1][:, 3, :])

            def h_transpose(k, c):
                if c == 0:
                    pe.wait_ge(S["h_loaded"], 16 * (k + 1))
                    if not first(k):
                        pe.wait_ge(S["score_ready"], ST * k)
                if not (first(k) and c == 0):
                    pe.wait_ge(S["h_lo_ready"], CK * k + c)
                for s in range(ST):
                    mm = pe.transpose(turn_bank[:, s * P:(s + 1) * P], xin[:, s, c * P:(c + 1) * P], ident[:, :])
                mm.then_inc(S["h_turned"], 1)

            def logits(k, s):
                if s == 0:
                    pe.wait_ge(S["h_lo_ready"], CK * (k + 1))
                if not (first(k) and s == 0):
                    pe.wait_ge(S["score_ready"], ST * k + s)
                out = turn_bank[:, 0:E]
                for ck in range(CK):
                    hi, lo = (x[:, ck, s * P:(s + 1) * P] for x in (hT_hi, hT_lo))
                    pe.matmul(out, hi, gate[0][:, ck, :], start=(ck == 0), stop=False)
                    pe.matmul(out, hi, gate[1][:, ck, :], start=False, stop=False)
                    mm = pe.matmul(out, lo, gate[0][:, ck, :], start=False, stop=(ck == CK - 1))
                mm.then_inc(S["logits_done"], 1)

            def places(k, s):
                g = ST * k + s
                pe.wait_ge(S["sel_ready"], g + 1)
                pe.wait_ge(S["seen_ready"], g + 1)
                out = route_bank[:, 0:E]
                pe.matmul(out, causal, sel, start=True, stop=False)
                pe.matmul(out, ones, seen, start=False, stop=True).then_inc(S["pos_ready"], 1)

            def up(k, j):
                if not (first(k) and j < 2):
                    pe.wait_ge(S["relu_ready"], SJ * k + j - 1)
                for ck in range(CK):
                    hi, lo = (x[:, ck, j * P:(j + 1) * P] for x in su)
                    pe.matmul(up_bank[:, j % 2, :], hi, hT_hi[:, ck, :], start=(ck == 0), stop=False)
                    pe.matmul(up_bank[:, j % 2, :], hi, hT_lo[:, ck, :], start=False, stop=False)
                    mm = pe.matmul(up_bank[:, j % 2, :], lo, hT_hi[:, ck, :], start=False, stop=(ck == CK - 1))
                mm.then_inc(S["up_done"], 1)

            def down(k, j):
                pe.wait_ge(S["s_lo_ready"], SJ * k + j + 1)
                if j == 0 and not first(k):
                    pe.wait_ge(S["yout_ready"], ST * k)
                for s in range(ST):
                    hi, lo = (x[:, j % 3, s * P:(s + 1) * P] for x in (s_hi, s_lo))
                    pe.matmul(y_bank[:, s, :], hi, sd[0][:, j, :], start=(j == 0), stop=False)
                    pe.matmul(y_bank[:, s, :], hi, sd[1][:, j, :], start=False, stop=False)
                    mm = pe.matmul(y_bank[:, s, :], lo, sd[0][:, j, :], start=False, stop=(j == SJ - 1))
                mm.then_inc(S["down_done"], 1)

            pe.wait_ge(S["y_ready"], ST * NT)
            pe.wait_ge(S["r_ready"], ST * NT)
            for c in range(CK):
                h_transpose(0, c)
            pe.wait_ge(S["gate_split"], 1)
            pe.wait_ge(S["ffn_split"], 4)
            pe.wait_ge(S["causal_ready"], 2)
            pe.wait_ge(S["ones_ready"], 1)

            def tile(k):
                for j in range(SJ):
                    if j % 2 == 0:
                        logits(k, j // 2)
                    if j == 2 and not first(k):
                        places(k - 1, 3)
                    if j in (4, 6):
                        places(k, j // 2 - 2)
                    up(k, j)
                    if j >= 2:
                        down(k, j - 2)
                if has(k, 1):
                    h_transpose(k + 1, 0)
                down(k, SJ - 2)
                if has(k, 1):
                    h_transpose(k + 1, 1)
                down(k, SJ - 1)
                if has(k, 1):
                    for c in range(2, CK):
                        h_transpose(k + 1, c)
                places(k, 2)

            tiles(pe, tile)
            places(NT - 1, 3)

            def xd_transpose(e, b, m):
                pe.wait_ge(S[f"xd_loaded{b}"], 16 * (m + 1))
                if not (isinstance(e, int) and e < 2):
                    pe.wait_ge(S["xdT_ready"], e - 1)
                for c in range(CK):
                    mm = pe.transpose(banks[0][:, b, c * P:(c + 1) * P], xd_sb[b][:, c * P:(c + 1) * P], ident[:, :])
                mm.then_inc(S["xd_turned"], 1)

            def e_first(e, b, m):
                pe.wait_ge(S[f"w1_loaded{b}"], 16 * (m + 1))
                pe.wait_ge(S["xdT_ready"], e + 1)
                if not (isinstance(e, int) and e < 2):
                    pe.wait_ge(S["e_relu"], e - 1)
                for i in range(IK):
                    for ck in range(CK):
                        mm = pe.matmul(banks[0][:, 2 + b, i * CAP:(i + 1) * CAP], w1_sb[b][:, ck, i * P:(i + 1) * P], xdT[b][:, ck, :],
                                       start=(ck == 0), stop=(ck == CK - 1))
                mm.then_inc(S["e_up"], 1)

            def e_second(e, b, m):
                pe.wait_ge(S[f"w2_loaded{b}"], 16 * (m + 1))
                pe.wait_ge(S["e_square"], e + 1)
                if not (isinstance(e, int) and e < 2):
                    pe.wait_ge(S["e_gated"], e - 1)
                for i in range(IK):
                    mm = pe.matmul(banks[1][:, b, :], e_act[b][:, i, :], w2_sb[b][:, i, :], start=(i == 0), stop=(i == IK - 1))
                mm.then_inc(S["e_down"], 1)

            pe.wait_ge(S["yout_ready"], ST * NT)
            pe.wait_ge(S["relu_ready"], SJ * NT)
            for b in range(2):
                xd_transpose(b, b, 0)
            e_first(0, 0, 0)

            def expert(e, q, m):
                b = q % 2
                if not (isinstance(e, int) and e + 2 >= E):
                    xd_transpose(e + 2, b, m + 1)
                if not (isinstance(e, int) and e + 1 >= E):
                    e_first(e + 1, 1 - b, m + b)
                e_second(e, b, m)

            experts(pe, expert)

        @block.scalar
        def _(act):
            def group(tau, job):
                return banks[(1 + tau + job) % 2]

            for j in range(4):
                act.wait_ge(S[f"w_loaded{j % 2}"], 16 * (j // 2 + 1))
                act.activation(W(j, 0), stage[j % 2][:, :, :], ACT.Copy, scale=-1.0 if j == 3 else 1.0).then_inc(S["w_hi"], 1)
                if j == 0:
                    act.wait_ge(S["vec_loaded"], 16)
                    act.activation(vecs[:, DECAY, :], vecs[:, TD, :], ACT.Exp).then_inc(S["decay_ready"], 1)

            def xnT_read(bank, tau):
                act.wait_ge(S["shift_ready"], tau + 1)
                for c in range(CK):
                    act.wait_ge(S["turned"], 4 * tau + c + 1)
                    act.activation(xnT[:, c, 1:TT + 1], bank[:, c, :], ACT.Copy).then_inc(S["xnT_ready"], 1)

            def round_mix(tau, j, ck):
                n = 4 * j + ck
                act.wait_ge(S["mixed"], 12 * tau + n + 1)
                if not (isinstance(tau, int) and 12 * tau + n < 3):
                    act.wait_ge(S["mix_used"], 12 * tau + n - 2)
                act.activation(mix_hi[:, n % 3, :], mixf[:, n % 2, :], ACT.Copy).then_inc(S["mix_hi_ready"], 1)

            def k_read(bank, tau, par):
                for c in range(CK):
                    act.wait_ge(S["mix_used"], 12 * tau + 4 * KJ + 4)
                    if not (isinstance(tau, int) and tau < 2):
                        act.wait_ge(S["gap_ready"], 4 * (tau - 2) + c + 1)
                    act.activation(k_sb[:, par, c, :], bank[:, c, :], ACT.Copy).then_inc(S["k_ready"], 1)

            def v_read(bank, tau, c):
                act.wait_ge(S["mix_used"], 12 * tau + 4 * VJ + 4)
                if not (isinstance(tau, int) and tau < 1):
                    act.wait_ge(S["vexped"], 4 * (tau - 1) + c + 1)
                act.activation(v_sb[:, c, :], bank[:, c, :], ACT.Copy).then_inc(S["v_ready"], 1)

            def r_read(bank, tau, c):
                act.wait_ge(S["mix_used"], 12 * tau + 4 * RJ + 4)
                if not (isinstance(tau, int) and tau < 1):
                    act.wait_ge(S["ns_ready"], 4 * (tau - 1) + c + 1)
                else:
                    act.wait_ge(S["w_split"], 4)
                act.activation(sr[:, c, :], bank[:, c, :], ACT.Sigmoid).then_inc(S["r_ready"], 1)

            def exps(tau, c):
                act.wait_ge(S["clamped"], 16 * tau + 4 * c + 4)
                act.activation(above[:, c % 2, :, :], above[:, c % 2, :, :], ACT.Exp, scale=-1.0).then_inc(S["exped"], 1)
                act.activation(below[:, c % 2, :, :], below[:, c % 2, :, :], ACT.Exp).then_inc(S["exped"], 1)

            def recip(tau, c):
                act.wait_ge(S["nd_ready"], 8 * tau + 2 * c + 2)
                act.activation(vexp[:, c % 2, 0, :], above[:, c % 2, 0, :], ACT.Ln).then_inc(S["recip_ln"], 1)
                act.wait_ge(S["recip_ln"], 4 * tau + c + 1)
                act.activation(vexp[:, c % 2, 0, :], vexp[:, c % 2, 0, :], ACT.Exp, scale=-1.0).then_inc(S["recip_ready"], 1)

            def rw_round(tau, c):
                act.wait_ge(S["rw_ready"], 4 * tau + c + 1)
                if back(tau):
                    act.wait_ge(S["out_used"], 4 * (tau - 1) + c + 1)
                act.activation(rw_hi[:, c, :], above[:, c % 2, 1, :], ACT.Copy).then_inc(S["rw_hi_ready"], 1)

            def y_read(bank, tau):
                if not (isinstance(tau, int) and tau < 1):
                    act.wait_ge(S["h_stored"], 16 * tau)
                for s in range(ST):
                    act.wait_ge(S["out_used"], 4 * tau + 4)
                    act.activation(hb[:, s, :], bank[:, s, :], ACT.Copy).then_inc(S["y_ready"], 1)

            def exp_table():
                act.preload_act_table_set("natural_log_exp_and_others")

            xnT_read(banks[0], 0)
            for j in range(3):
                for ck in range(CK):
                    round_mix(0, j, ck)
                if j == KJ:
                    k_read(banks[1], 0, 0)
                if j == VJ:
                    for c in range(CK):
                        v_read(banks[0], 0, c)
            for c in range(CK):
                r_read(banks[1], 0, c)
            xnT_read(banks[0], 1)
            exp_table()

            def period(tau, par):
                g = 1 if back(tau) else 0
                if back(tau):
                    y_read(group(par - 1, 4), tau - 1)
                exps(tau, 0)
                if has(tau, 1):
                    for ck in range(CK):
                        round_mix(tau + 1, KJ, ck)
                recip(tau, 0)
                exps(tau, 1)
                if has(tau, 1):
                    for ck in range(CK):
                        round_mix(tau + 1, VJ, ck)
                    k_read(group(par, 0), tau + 1, 1 - par)
                rw_round(tau, 0)
                recip(tau, 1)
                exps(tau, 2)
                if has(tau, 1):
                    for c in range(2):
                        v_read(group(par, 1), tau + 1, c)
                    for ck in range(CK):
                        round_mix(tau + 1, RJ, ck)
                rw_round(tau, 1)
                recip(tau, 2)
                exps(tau, 3)
                if has(tau, 1):
                    for c in range(2, 4):
                        v_read(group(par, 1), tau + 1, c)
                rw_round(tau, 2)
                recip(tau, 3)
                if has(tau, 2):
                    xnT_read(group(par, 3), tau + 2)
                rw_round(tau, 3)
                if has(tau, 1):
                    for c in range(CK):
                        r_read(group(par, 2), tau + 1, c)
                    exp_table()

            periods(act, period)
            y_read(group(1, 4), NT - 1)

            raw = [flat(xin), flat(xnd)]
            act.wait_ge(S["out_used"], CK * NT)
            for q in range(4):
                act.wait_ge(S[f"raw{q % 2}_loaded"], 16 * (q // 2 + 1))
                act.activation((su_hi if q < 2 else sd_hi)[:, (q % 2) * 2048:(q % 2 + 1) * 2048], raw[q % 2], ACT.Copy).then_inc(S["ffn_hi"], 1)
            act.wait_ge(S["gate_loaded"], 16)
            act.activation(gate_w[:, 0, :], flat(k_sb[:, 0, :, :])[:, 0:CK * E], ACT.Copy).then_inc(S["gate_hi"], 1)

            y_bank, (up_bank, turn_bank, route_bank) = banks[0], (banks[1][:, 0:2, :], banks[1][:, 2, :], banks[1][:, 3, :])

            def h_hi(k, c):
                if not first(k):
                    act.wait_ge(S["up_done"], SJ * k)
                    act.wait_ge(S["logits_done"], ST * k)
                act.wait_ge(S["h_turned"], CK * k + c + 1)
                act.activation(hT_hi[:, c, :], turn_bank, ACT.Copy).then_inc(S["h_hi_ready"], 1)

            def scores(k, s):
                act.wait_ge(S["logits_done"], ST * k + s + 1)
                if not (first(k) and s < 2):
                    act.wait_ge(S["slots_ready"], ST * k + s - 1)
                act.activation(score[:, s % 2, :], turn_bank[:, 0:E], ACT.Sigmoid).then_inc(S["score_ready"], 1)

            def hidden(k, j):
                act.wait_ge(S["up_done"], SJ * k + j + 1)
                if not (first(k) and j < 2):
                    act.wait_ge(S["square_ready"], SJ * k + j - 1)
                act.activation(relu[:, j % 2, :], up_bank[:, j % 2, :], ACT.Relu).then_inc(S["relu_ready"], 1)
                act.wait_ge(S["relu_ready"], SJ * k + j + 1)
                if not (first(k) and j < 3):
                    act.wait_ge(S["down_done"], SJ * k + j - (2 if j < 2 else 3) + 1)
                act.activation(s_hi[:, j % 3, :], relu[:, j % 2, :], ACT.Square).then_inc(S["s_hi_ready"], 1)

            def yout_read(k):
                act.wait_ge(S["down_done"], SJ * (k + 1))
                if not first(k):
                    act.wait_ge(S["ysh_stored"], 16 * k)
                for s in range(ST):
                    act.activation(yout[:, s, :], y_bank[:, s, :], ACT.Copy).then_inc(S["yout_ready"], 1)

            for c in range(CK):
                h_hi(0, c)
            act.wait_ge(S["gate_split"], 1)

            def tile(k):
                for j in range(SJ):
                    if j % 2 == 0:
                        scores(k, j // 2)
                    hidden(k, j)
                if has(k, 1):
                    for c in range(CK):
                        h_hi(k + 1, c)
                yout_read(k)

            tiles(act, tile)

            def xdT_read(e, b, m):
                act.wait_ge(S["xd_turned"], e + 1)
                if not (isinstance(e, int) and e < 2):
                    act.wait_ge(S["e_up"], e - 1)
                act.activation(xdT[b].rearrange("p k n -> p (k n)"), banks[0][:, b, :], ACT.Copy).then_inc(S["xdT_ready"], 1)

            def e_relu(e, b, m):
                act.wait_ge(S["e_up"], e + 1)
                if not (isinstance(e, int) and e < 2):
                    act.wait_ge(S["e_square"], e - 1)
                act.activation(e_hidden[b], banks[0][:, 2 + b, 0:HID], ACT.Relu).then_inc(S["e_relu"], 1)

            def e_gate(e, q, m):
                b = q % 2
                """The expert's output, times the gate of each slot."""
                act.wait_ge(S["e_down"], e + 1)
                act.wait_ge(S["e_index"], 2 * e + 2)
                if not (isinstance(e, int) and e < 2):
                    act.wait_ge(S["added"], 16 * (e - 1))
                act.activation(e_out[b], banks[1][:, b, :], ACT.Copy, scale=e_gates[:, q:q + 1]).then_inc(S["e_gated"], 1)

            for b in range(2):
                xdT_read(b, b, 0)
            e_relu(0, 0, 0)

            def expert(e, q, m):
                b = q % 2
                if not (isinstance(e, int) and e + 2 >= E):
                    xdT_read(e + 2, b, m + 1)
                if not (isinstance(e, int) and e + 1 >= E):
                    e_relu(e + 1, 1 - b, m + b)
                e_gate(e, q, m)

            experts(act, expert)

        @block.gpsimd
        def _(pool):
            pool.memset(ident[:, :], 0.0).then_inc(S["ident_ready"], 1)
            pool.memset(neg_half[:, :], -0.5).then_inc(S["half_ready"], 1)
            pool.wait_ge(S["ident_ready"], 1)
            pool.affine_select(out=ident[:, :], in_=ident[:, :], compare_op=ALU.not_equal, fill=1.0, base=0,
                               pattern=[[-1, P]], channel_multiplier=1).then_inc(S["ident_ready"], 1)
            pool.wait_ge(S["half_ready"], 1)

            def inv_std(ln, tau):
                pool.wait_ge(S[f"ln{ln}_moments"], ST * (tau + 1))
                pool.sem_inc(S["pool_step"], 1)
                pool.tensor_scalar(rstd[:, ln - 1, :], mv[:, ln - 1, :, 1], EPS, None, ALU.add).then_inc(S[f"ln{ln}_rstd"], 1)
                pool.wait_ge(S[f"ln{ln}_rstd"], 2 * tau + 1)
                pool.tensor_tensor(rstd[:, ln - 1, :], rstd[:, ln - 1, :], neg_half[:, :], ALU.pow).then_inc(S[f"ln{ln}_rstd"], 1)

            def mix_rest(tau, j, ck):
                n = 4 * j + ck
                pool.wait_ge(S["mix_hi_ready"], 12 * tau + n + 1)
                pool.tensor_tensor(mix_lo[:, n % 3, :], mixf[:, n % 2, :], mix_hi[:, n % 3, :].bitcast(F32),
                                   ALU.subtract).then_inc(S["mix_lo_ready"], 1)

            def times_v(tau, c):
                pool.wait_ge(S["exped"], 8 * tau + 2 * c + 2)
                pool.wait_ge(S["v_ready"], 4 * tau + c + 1)
                for e in range(2):
                    ins = pool.tensor_tensor(vexp[:, c % 2, e, :], below[:, c % 2, e, :], v_sb[:, c, :], ALU.mult)
                ins.then_inc(S["vexped"], 1)

            def gated_num(tau, c):
                pool.wait_ge(S["nd_ready"], 8 * tau + 2 * c + 2)
                pool.wait_ge(S["r_ready"], 4 * tau + c + 1)
                pool.tensor_tensor(vexp[:, c % 2, 1, :], above[:, c % 2, 1, :], sr[:, c, :], ALU.mult).then_inc(S["ns_ready"], 1)
                pool.wait_ge(S["ns_ready"], 4 * tau + c + 1)
                pool.wait_ge(S["recip_ready"], 4 * tau + c + 1)
                pool.tensor_tensor(vexp[:, c % 2, 1, :], vexp[:, c % 2, 1, :], vexp[:, c % 2, 0, :], ALU.mult).then_inc(S["a_ready"], 1)

            def rw_rest(tau, c):
                pool.wait_ge(S["rw_hi_ready"], 4 * tau + c + 1)
                pool.tensor_tensor(rw_lo[:, c, :], above[:, c % 2, 1, :], rw_hi[:, c, :].bitcast(F32),
                                   ALU.subtract).then_inc(S["rw_lo_ready"], 1)

            def residual(tau):
                pool.wait_ge(S["xres_loaded"], 16 * (tau + 1))
                for s in range(ST):
                    pool.wait_ge(S["yn_ready"], ST * tau + s + 1)
                    pool.tensor_tensor(xres[:, s, :], xres[:, s, :], hb[:, s, :], ALU.add).then_inc(S["x1_ready"], 1)

            inv_std(1, 0)
            pool.wait_ge(S["w_split"], 3)
            blank = flat(hb)[:, 0:ROW]
            pool.memset(blank[:, 0:TOKEN], 0.0).then_inc(S["blank_ready"], 1)
            pool.iota(blank[:, TOKEN:ROW], pattern=[[0, 1]], base=N, channel_multiplier=1,
                      allow_small_or_imprecise_dtypes=True).then_inc(S["blank_ready"], 1)
            for j in range(3):
                for ck in range(CK):
                    mix_rest(0, j, ck)
            inv_std(1, 1)

            def period(tau, par):
                times_v(tau, 0)
                if has(tau, 1):
                    for ck in range(CK):
                        mix_rest(tau + 1, KJ, ck)
                gated_num(tau, 0)
                times_v(tau, 1)
                if has(tau, 1):
                    for ck in range(CK):
                        mix_rest(tau + 1, VJ, ck)
                rw_rest(tau, 0)
                gated_num(tau, 1)
                times_v(tau, 2)
                if back(tau):
                    inv_std(2, tau - 1)
                    residual(tau - 1)
                if has(tau, 1):
                    for ck in range(CK):
                        mix_rest(tau + 1, RJ, ck)
                rw_rest(tau, 1)
                gated_num(tau, 2)
                times_v(tau, 3)
                if has(tau, 2):
                    inv_std(1, tau + 2)
                rw_rest(tau, 2)
                if back(tau):
                    inv_std(3, tau - 1)
                gated_num(tau, 3)
                rw_rest(tau, 3)

            periods(pool, period)
            inv_std(2, NT - 1)
            residual(NT - 1)
            inv_std(3, NT - 1)

            pool.wait_ge(S["carried"], 2 * CK * NT)
            pool.iota(number_i, pattern=[[1, E]], base=0, channel_multiplier=0).then_inc(S["number_made"], 1)
            pool.iota(token_i, pattern=[[0, 1]], base=0, channel_multiplier=1).then_inc(S["number_made"], 1)
            pool.memset(ones, 1.0).then_inc(S["ones_ready"], 1)
            pool.memset(causal, 1.0).then_inc(S["causal_ready"], 1)
            pool.memset(seen, 0.0).then_inc(S["seen_ready"], 1)
            pool.wait_ge(S["causal_ready"], 1)
            pool.affine_select(out=causal, in_=causal, compare_op=ALU.is_gt, fill=0.0, base=0,
                               pattern=[[1, P]], channel_multiplier=-1).then_inc(S["causal_ready"], 1)
            pool.wait_ge(S["xd_blank"], 16)

            def tile(k):
                for s in range(ST):
                    pool.wait_ge(S[f"rows_loaded{s % 2}"], 16 * (2 * k + s // 2 + 1))
                    pool.wait_ge(S["slots_ready"], ST * k + s + 1)
                    pool.sem_inc(S["pool_step"], 1)
                    for c in range(TOPK):
                        pool.indirect_dma_start(t["xd"], bass.IndirectOffsetOnAxis(ap=slot[:, s % 2, c:c + 1], axis=0), rows[:, s % 2, c, :], None,
                                                bounds_check=E * CAP - 1, oob_is_err=False).then_inc(S[f"scattered{s % 2}"], 16)

            tiles(pool, tile)
            pool.wait_ge(S["ysh_stored"], 16 * NT)
            pool.wait_ge(S["ysh_blank"], 16)

            def expert(e, q, m):
                b = q % 2
                pool.wait_ge(S["e_gated"], e + 1)
                pool.wait_ge(S["e_index"], 2 * e + 2)
                if not first(e):
                    pool.wait_ge(S["added"], 16 * e)
                pool.sem_inc(S["pool_step"], 1)
                pool.indirect_dma_start(t["ysh"], bass.IndirectOffsetOnAxis(ap=e_token[:, q:q + 1], axis=0), e_out[b], None,
                                        compute_op=ALU.add).then_inc(S["added"], 16)

            experts(pool, expert)

            def final(k, b, m):
                inv_std(4, k)

            finals(pool, final)

        @block.vector
        def _(dve):
            dve_engine[0] = dve
            for j in range(4):
                dve.wait_ge(S["w_hi"], j + 1)
                hi = W(j, 0).bitcast(F32)
                if j == 3:
                    dve.scalar_tensor_tensor(out=W(j, 1), in0=stage[j % 2][:, :, :], scalar=-1.0, in1=hi,
                                             op0=ALU.mult, op1=ALU.subtract).then_inc(S["w_split"], 1)
                else:
                    dve.tensor_tensor(W(j, 1), stage[j % 2][:, :, :], hi, ALU.subtract).then_inc(S["w_split"], 1)
                if j == 0:
                    dve.wait_ge(S["decay_ready"], 1)
                    dve.tensor_scalar(vecs[:, NEGW, :], vecs[:, DECAY, :], -1.0, None, ALU.mult).then_inc(S["decay_ready"], 1)

            def moments(ln, src, tau):
                for s in range(ST):
                    dve.bn_stats(stats[:, s, :], src[:, s, :]).then_inc(S[f"ln{ln}_stats"], 1)
                after(dve, f"ln{ln}_stats", ST * (tau + 1))
                for s in range(ST):
                    dve.bn_aggr(mv[:, ln - 1, s, :], stats[:, s, :]).then_inc(S[f"ln{ln}_moments"], 1)

            def normalise(ln, dst, src, tau, done):
                dve.wait_ge(S[f"ln{ln}_rstd"], 2 * tau + 2)
                for s in range(ST):
                    dve.tensor_scalar(dst[:, s, :], src[:, s, :], mv[:, ln - 1, s, 0:1], rstd[:, ln - 1, s:s + 1],
                                      ALU.subtract, ALU.mult).then_inc(S[done], 1)

            def ln1_moments(tau):
                dve.wait_ge(S["x_loaded"], 16 * (tau + 1))
                moments(1, xin, tau)

            def ln1_normalise(tau):
                if not (isinstance(tau, int) and tau < 1):
                    dve.wait_ge(S["mixed"], 12 * tau)
                normalise(1, xnd, xin, tau, "xn_ready")

            def shift(tau, par):
                if par == 0:
                    if not (isinstance(tau, int) and tau < 1):
                        dve.wait_ge(S["mixed"], 12 * tau)
                    dve.memset(xnT[:, :, 0:1], 0.0).then_inc(S["shift_ready"], 1)
                else:
                    dve.wait_ge(S["xnT_ready"], 4 * tau)
                    dve.tensor_copy(xnT[:, :, 0:1], xnT[:, :, TT:TT + 1]).then_inc(S["shift_ready"], 1)

            def diff(tau, ck):
                dve.wait_ge(S["xnT_ready"], 4 * tau + ck + 1)
                if ck == 0:
                    dve.wait_ge(S["turned"], 4 * tau + 4)
                dve.tensor_tensor(xnd[:, ck, :], xnT[:, ck, 1:TT + 1], xnT[:, ck, 0:TT],
                                  ALU.subtract).then_inc(S["diff_ready"], 1)

            def mix(tau, j, ck):
                n = 4 * j + ck
                if j == KJ:
                    dve.wait_ge(S["diff_ready"], 4 * tau + ck + 1)
                if not (isinstance(tau, int) and 12 * tau + n < 2):
                    dve.wait_ge(S["mix_lo_ready"], 12 * tau + n - 1)
                dve.scalar_tensor_tensor(out=mixf[:, n % 2, :], in0=xnd[:, ck, :], scalar=vecs[:, MK + j, ck:ck + 1],
                                         in1=xnT[:, ck, 0:TT], op0=ALU.mult, op1=ALU.add).then_inc(S["mixed"], 1)

            def gaps(tau, par, c):
                b = c % 2
                u = 4 * tau + c
                if par == 0:
                    dve.memset(run_max[:, b, 0:1], NEG_BIG).then_inc(S["seeded"], 1)
                    dve.memset(state[:, b, :, 0:1], 0.0).then_inc(S["seeded"], 1)
                else:
                    dve.wait_ge(S["carried"], 2 * (u - CK) + 2)
                    dve.tensor_copy(run_max[:, b, 0:1], carry[:, c, 0:1]).then_inc(S["seeded"], 1)
                    dve.tensor_copy(state[:, b, :, 0:1], carry[:, c, 1:3].rearrange("p (a o) -> p a o", o=1)).then_inc(S["seeded"], 1)
                dve.wait_ge(S["seeded"], 2 * u + 2)
                dve.wait_ge(S["k_ready"], u + 1)
                dve.tensor_tensor_scan(run_max[:, b, 1:TT + 1], vecs[:, NEGW, c:c + 1].to_broadcast([P, TT]), k_sb[:, par, c, :],
                                       run_max[:, b, 0:1], ALU.add, ALU.max).then_inc(S["max_scanned"], 1)
                dve.wait_ge(S["max_scanned"], u + 1)
                if not (isinstance(tau, int) and 4 * tau + c < 2):
                    dve.wait_ge(S["rw_lo_ready"], u - 1)
                dve.tensor_tensor(below[:, b, 1, :], k_sb[:, par, c, :], run_max[:, b, 0:TT], ALU.subtract).then_inc(S["gap_ready"], 1)
                dve.tensor_copy(carry[:, c, 0:1], run_max[:, b, TT:TT + 1]).then_inc(S["carried"], 1)
                dve.wait_ge(S["gap_ready"], u + 1)
                for dst, op in ((above, ALU.max), (below, ALU.min)):
                    for e, shift_by in enumerate((TF, DECAY)):
                        dve.tensor_scalar(dst[:, b, e, :], below[:, b, 1, :], vecs[:, shift_by, c:c + 1], 0.0,
                                          ALU.add, op).then_inc(S["clamped"], 1)

            def scans(tau, c):
                b = c % 2
                u = 4 * tau + c
                dve.wait_ge(S["vexped"], u + 1)
                for e, add in ((0, vexp[:, b, 1, :]), (1, below[:, b, 1, :])):
                    dve.tensor_tensor_scan(state[:, b, e, 1:TT + 1], above[:, b, 1, :], add, state[:, b, e, 0:1],
                                           ALU.mult, ALU.add).then_inc(S["scanned"], 1)
                dve.wait_ge(S["scanned"], 2 * u + 2)
                dve.tensor_tensor(above[:, b, 1, :], above[:, b, 0, :], state[:, b, 0, 0:TT], ALU.mult).then_inc(S["scaled"], 1)
                dve.tensor_copy(carry[:, c, 1:3].rearrange("p (a o) -> p a o", o=1), state[:, b, :, TT:TT + 1]).then_inc(S["carried"], 1)
                dve.wait_ge(S["scaled"], 2 * u + 1)
                dve.tensor_tensor(above[:, b, 0, :], above[:, b, 0, :], state[:, b, 1, 0:TT], ALU.mult).then_inc(S["scaled"], 1)
                dve.tensor_tensor(above[:, b, 1, :], above[:, b, 1, :], vexp[:, b, 0, :], ALU.add).then_inc(S["nd_ready"], 1)
                dve.wait_ge(S["scaled"], 2 * u + 2)
                dve.tensor_tensor(above[:, b, 0, :], above[:, b, 0, :], below[:, b, 0, :], ALU.add).then_inc(S["nd_ready"], 1)

            def refine(tau, c):
                b = c % 2
                u = 4 * tau + c
                dve.wait_ge(S["recip_ready"], u + 1)
                dve.tensor_tensor(above[:, b, 0, :], above[:, b, 0, :], vexp[:, b, 0, :], ALU.mult).then_inc(S["resid_ready"], 1)
                dve.wait_ge(S["resid_ready"], u + 1)
                dve.wait_ge(S["a_ready"], u + 1)
                dve.scalar_tensor_tensor(out=above[:, b, 1, :], in0=above[:, b, 0, :], scalar=2.0, in1=vexp[:, b, 1, :],
                                         op0=ALU.subtract, op1=ALU.mult).then_inc(S["rw_ready"], 1)

            def ln2(tau):
                dve.wait_ge(S["y_ready"], ST * (tau + 1))
                moments(2, hb, tau)

            def ln2_normalise(tau):
                normalise(2, hb, hb, tau, "yn_ready")

            def ln3(tau):
                dve.wait_ge(S["x1_ready"], ST * (tau + 1))
                moments(3, xres, tau)

            def ln3_normalise(tau):
                normalise(3, hb, xres, tau, "h_ready")

            ln1_moments(0)
            ln1_normalise(0)
            shift(0, 0)
            for j in range(3):
                for ck in range(CK):
                    if j == KJ:
                        diff(0, ck)
                    mix(0, j, ck)
            ln1_moments(1)
            ln1_normalise(1)
            shift(1, 1)

            def period(tau, par):
                gaps(tau, par, 0)
                if has(tau, 1):
                    for ck in range(CK):
                        diff(tau + 1, ck)
                        mix(tau + 1, KJ, ck)
                scans(tau, 0)
                gaps(tau, par, 1)
                if has(tau, 1):
                    for ck in range(CK):
                        mix(tau + 1, VJ, ck)
                refine(tau, 0)
                scans(tau, 1)
                if back(tau):
                    ln2(tau - 1)
                gaps(tau, par, 2)
                if back(tau):
                    ln2_normalise(tau - 1)
                if has(tau, 1):
                    for ck in range(CK):
                        mix(tau + 1, RJ, ck)
                refine(tau, 1)
                scans(tau, 2)
                if has(tau, 2):
                    ln1_moments(tau + 2)
                gaps(tau, par, 3)
                if has(tau, 2):
                    ln1_normalise(tau + 2)
                    shift(tau + 2, par)
                refine(tau, 2)
                if back(tau):
                    ln3(tau - 1)
                scans(tau, 3)
                if back(tau):
                    ln3_normalise(tau - 1)
                refine(tau, 3)

            periods(dve, period)
            ln2(NT - 1)
            ln2_normalise(NT - 1)
            ln3(NT - 1)
            ln3_normalise(NT - 1)

            raw = [flat(xin), flat(xnd)]
            for q in range(4):
                dve.wait_ge(S["ffn_hi"], q + 1)
                part = slice((q % 2) * 2048, (q % 2 + 1) * 2048)
                hi, lo = (su_hi, su_lo) if q < 2 else (sd_hi, sd_lo)
                dve.tensor_tensor(lo[:, part], raw[q % 2], hi[:, part].bitcast(F32), ALU.subtract).then_inc(S["ffn_split"], 1)
            dve.wait_ge(S["gate_hi"], 1)
            dve.tensor_tensor(gate_w[:, 1, :], flat(k_sb[:, 0, :, :])[:, 0:CK * E], gate_w[:, 0, :].bitcast(F32),
                              ALU.subtract).then_inc(S["gate_split"], 1)
            dve.wait_ge(S["number_made"], 2)
            dve.tensor_copy(number, number_i).then_inc(S["number_ready"], 1)
            dve.tensor_copy(token, token_i).then_inc(S["token_ready"], 1)
            dve.wait_ge(S["ffn_split"], 4)
            dve.wait_ge(S["number_ready"], 1)
            dve.wait_ge(S["token_ready"], 1)
            dve.wait_ge(S["bias_loaded"], 16)

            turn_bank, route_bank = banks[1][:, 2, :], banks[1][:, 3, :]

            def h_rest(k, c):
                dve.wait_ge(S["h_hi_ready"], CK * k + c + 1)
                dve.tensor_tensor(hT_lo[:, c, :], turn_bank, hT_hi[:, c, :].bitcast(F32), ALU.subtract).then_inc(S["h_lo_ready"], 1)

            def split(k, j):
                dve.wait_ge(S["relu_ready"], SJ * k + j + 1)
                dve.tensor_tensor(square[:, j % 2, :], relu[:, j % 2, :], relu[:, j % 2, :], ALU.mult).then_inc(S["square_ready"], 1)
                dve.wait_ge(S["square_ready"], SJ * k + j + 1)
                dve.wait_ge(S["s_hi_ready"], SJ * k + j + 1)
                dve.tensor_tensor(s_lo[:, j % 3, :], square[:, j % 2, :], s_hi[:, j % 3, :].bitcast(F32), ALU.subtract).then_inc(S["s_lo_ready"], 1)

            STEPS = 36
            count = [0]

            def route(k, s):
                base = STEPS * (ST * k + s)

                def step(ins):
                    ins.then_inc(S["route_step"], 1)
                    count[0] += 1

                def settled(own=False):
                    dve.wait_ge(S["route_step"], base + count[0])
                    if own:
                        dve.sem_inc(S["dve_step"], 1)

                return step, settled

            def choose(k, s):
                count[0] = 0
                step, settled = route(k, s)
                by_group = biased.rearrange("p (g e) -> p g e", g=GROUPS)
                sc = score[:, s % 2, :]
                dve.wait_ge(S["score_ready"], ST * k + s + 1)
                step(dve.tensor_tensor(biased, sc, bias_row, ALU.add))
                settled(own=True)
                for g in range(GROUPS):
                    step(dve.max(group_top[:, g, :], by_group[:, g, :]))
                settled()
                step(dve.tensor_tensor(group_score, group_top[:, :, 0], group_top[:, :, 1], ALU.add))
                settled(own=True)
                step(dve.max(group_best, group_score))
                settled(own=True)
                step(dve.max_index(group_index, group_best, group_score))
                settled()
                step(dve.tensor_copy(group_number, group_index))
                settled()
                step(dve.tensor_tensor(group_hot, number[:, 0:GROUPS].rearrange("p (o g) -> p o g", o=1).to_broadcast([P, TOPG, GROUPS]),
                                       group_number[:, 0:TOPG].rearrange("p (g o) -> p g o", o=1).to_broadcast([P, TOPG, GROUPS]), ALU.is_equal))
                settled()
                step(dve.tensor_reduce(group_mask, group_hot.rearrange("p k g -> p g k"), AX.X, ALU.add))
                settled()
                step(dve.tensor_scalar(group_floor, group_mask, 1.0, LOWEST, ALU.subtract, ALU.mult))
                over_experts = [m.rearrange("p (g o) -> p g o", o=1).to_broadcast([P, GROUPS, EG]) for m in (group_mask, group_floor)]
                masked_g = masked.rearrange("p (g e) -> p g e", g=GROUPS)
                step(dve.tensor_tensor(masked_g, by_group, over_experts[0], ALU.mult))
                settled()
                step(dve.tensor_tensor(masked_g, masked_g, over_experts[1], ALU.add))
                settled(own=True)
                step(dve.max(expert_best, masked))
                settled(own=True)
                step(dve.max_index(expert_index, expert_best, masked))
                settled()
                step(dve.tensor_copy(expert_number, expert_index))
                settled()
                step(dve.tensor_tensor(hot, number.rearrange("p (o e) -> p o e", o=1).to_broadcast([P, TOPK, E]),
                                       expert_number[:, 0:TOPK].rearrange("p (k o) -> p k o", o=1).to_broadcast([P, TOPK, E]), ALU.is_equal))
                settled()
                step(dve.tensor_reduce(sel_f, hot.rearrange("p k e -> p e k"), AX.X, ALU.add))
                settled()
                dve.tensor_copy(sel, sel_f).then_inc(S["sel_ready"], 1)
                step(dve.tensor_tensor(product, hot, sc.rearrange("p (o e) -> p o e", o=1).to_broadcast([P, TOPK, E]), ALU.mult))
                settled()
                step(dve.tensor_reduce(weight, product, AX.X, ALU.add))
                settled()
                step(dve.tensor_reduce(weight_sum, weight, AX.X, ALU.add))
                settled()
                step(dve.tensor_scalar(weight_sum, weight_sum, 1e-20, None, ALU.add))
                settled()
                step(dve.reciprocal(weight_sum, weight_sum))
                settled()
                dve.wait_ge(S[f"rows_loaded{s % 2}"], 16 * (2 * k + s // 2 + 1))
                step(dve.tensor_scalar(rows[:, s % 2, :, GATE], weight, weight_sum, ROUTE_SCALE, ALU.mult, ALU.mult))
                step(dve.tensor_copy(rows[:, s % 2, :, TOKEN], token.to_broadcast([P, TOPK])))

            def dispatch(k, s):
                step, settled = route(k, s)
                dve.wait_ge(S["pos_ready"], ST * k + s + 1)
                pos = route_bank[:, 0:E].rearrange("p (o e) -> p o e", o=1).to_broadcast([P, TOPK, E])
                settled()
                step(dve.tensor_tensor(product, hot, pos, ALU.mult))
                settled()
                step(dve.tensor_reduce(place, product, AX.X, ALU.add))
                dve.wait_ge(S["sel_ready"], ST * k + s + 1)
                dve.tensor_tensor(seen, seen, sel, ALU.add).then_inc(S["seen_ready"], 1)
                settled()
                step(dve.tensor_scalar(over, place, float(CAP), FAR, ALU.is_ge, ALU.mult))
                step(dve.scalar_tensor_tensor(out=slot_f, in0=expert_number[:, 0:TOPK], scalar=float(CAP), in1=place, op0=ALU.mult, op1=ALU.add))
                settled()
                step(dve.tensor_tensor(slot_f, slot_f, over, ALU.add))
                settled()
                dve.tensor_copy(slot[:, s % 2, :], slot_f).then_inc(S["slots_ready"], 1)
                step(dve.tensor_scalar(token, token, float(P), None, ALU.add))
                assert count[0] == STEPS, count[0]

            for c in range(CK):
                h_rest(0, c)

            def tile(k):
                for j in range(SJ):
                    split(k, j)
                    if j == 1 and not first(k):
                        dispatch(k - 1, 3)
                    if j in (3, 5):
                        dispatch(k, j // 2 - 1)
                    if j in (1, 3, 5):
                        choose(k, j // 2)
                if has(k, 1):
                    for c in range(CK):
                        h_rest(k + 1, c)
                dispatch(k, 2)
                choose(k, 3)

            tiles(dve, tile)
            dispatch(NT - 1, 3)

            def e_index(e, q, m):
                b = q % 2
                dve.wait_ge(S[f"xd_loaded{b}"], 16 * (m + 1))
                if not (isinstance(e, int) and e < 4):
                    dve.wait_ge(S["added"], 16 * (e - 3))
                dve.tensor_copy(e_token[:, q:q + 1], xd_sb[b][:, TOKEN:ROW]).then_inc(S["e_index"], 1)
                dve.tensor_copy(e_gates[:, q:q + 1], xd_sb[b][:, GATE:GATE + 1]).then_inc(S["e_index"], 1)

            def e_square(e, b, m):
                dve.wait_ge(S["e_relu"], e + 1)
                if not (isinstance(e, int) and e < 2):
                    dve.wait_ge(S["e_down"], e - 1)
                dve.tensor_tensor(e_act[b].rearrange("p k n -> p (k n)"), e_hidden[b], e_hidden[b], ALU.mult).then_inc(S["e_square"], 1)

            e_index(0, 0, 0)
            e_index(1, 1, 0)
            e_square(0, 0, 0)

            def expert(e, q, m):
                b = q % 2
                if not (isinstance(e, int) and e + 1 >= E):
                    e_square(e + 1, 1 - b, m + b)
                if not (isinstance(e, int) and e + 2 >= E):
                    e_index(e + 2, (q + 2) % 4, m + 1)

            experts(dve, expert)

            def final(k, b, m):
                dve.wait_ge(S[f"ysh_loaded{b}"], 16 * (m + 1))
                moments(4, o_y[b], k)
                normalise(4, o_y[b], o_y[b], k, "o_normed")
                dve.wait_ge(S[f"x1_loaded{b}"], 16 * (m + 1))
                for s in range(ST):
                    dve.wait_ge(S["o_normed"], ST * k + s + 1)
                    dve.tensor_tensor(o_y[b][:, s, :], o_y[b][:, s, :], o_x[b][:, s, :], ALU.add).then_inc(S["o_ready"], 1)

            finals(dve, final)


def kernel(**inputs):
    import numpy as _np
    import concourse.bacc as _bacc
    from concourse import mybir as _mybir
    from concourse.bass_utils import run_bass_kernel_spmd as _run

    def by_partition(w, chunks):
        return _np.ascontiguousarray(w.reshape(chunks, P, -1).transpose(1, 0, 2))

    g = {n: _np.asarray(a) for n, a in inputs.items()}
    vecs = [g["L0_attn_time_decay"], g["L0_attn_time_first"], g["L0_attn_time_mix_k"], g["L0_attn_time_mix_v"], g["L0_attn_time_mix_r"]]
    arrays = {
        "x": _np.ascontiguousarray(g["L0_attn_x"].reshape(N, C)),
        "vecs": _np.ascontiguousarray(_np.stack([v.reshape(CK, P).T for v in vecs], axis=1)),
        "Wk": by_partition(g["L0_attn_Wk"].T, CK),
        "Wv": by_partition(g["L0_attn_Wv"].T, CK),
        "Wr": by_partition(g["L0_attn_Wr"].T, CK),
        "Wo": by_partition(g["L0_attn_Wo"].T, CK),
        "gate": by_partition(g["L0_ffn_gate_w"].T, CK).reshape(P, CK * E),
        "e_bias": g["L0_ffn_e_bias"].reshape(1, E),
        "su": by_partition(g["L0_ffn_shared_up_w"].T, CK).reshape(P, 2, -1),
        "sd": by_partition(g["L0_ffn_shared_down_w"].T, SJ).reshape(P, 2, -1),
        "w1": _np.ascontiguousarray(g["L0_ffn_w1"].transpose(0, 2, 1).reshape(E, CK, P, HID).transpose(0, 2, 1, 3)).reshape(E, P, CK * HID),
        "w2": _np.ascontiguousarray(g["L0_ffn_w2"].transpose(0, 2, 1).reshape(E, IK, P, C).transpose(0, 2, 1, 3)).reshape(E, P, IK * C),
    }
    nc = _bacc.Bacc("TRN2", target_bir_lowering=False, num_devices=1)
    aps = {n: nc.dram_tensor(f"in_{n}", a.shape, _mybir.dt.from_np(a.dtype), kind="ExternalInput").ap() for n, a in arrays.items()}
    scratch = {"x1": (N, C), "h": (N, C), "ysh": (N + P, C), "xd": (E * CAP, ROW)}
    aps.update({n: nc.dram_tensor(n, shape, F32, kind="Internal").ap() for n, shape in scratch.items()})
    aps["out"] = nc.dram_tensor("out", (N, C), F32, kind="ExternalOutput").ap()
    sandwich(nc, aps)
    r = _run(nc, [{f"in_{n}": a for n, a in arrays.items()}], core_ids=[0])
    return r.results[0]["out"].reshape(B, T, C)
```

```python
import concourse.bass as bass
from concourse import mybir
from contextlib import ExitStack

F32 = mybir.dt.float32
F32R = mybir.dt.float32r
BF16 = mybir.dt.bfloat16
I32 = mybir.dt.int32
U32 = mybir.dt.uint32
ALU = mybir.AluOpType
ACT = mybir.ActivationFunctionType
AX = mybir.AxisListType

P = 128
C = 512
CK = C // P
B, T = 4, 1024
N = B * T
TT = 512
ST = TT // P
NT = N // TT
EPS = 1e-5
NEG_BIG = -1e38
E, GROUPS, TOPG, TOPK = 64, 8, 4, 6
EG = E // GROUPS
CAP = 128
HID = 256
SH = 1024
SJ = SH // P
IK = HID // P
ROUTE_SCALE = 2.5
GATE, TOKEN = range(2)
EB = 4
FB = 4
LOWEST = 3e38
KJ, VJ, RJ = range(3)


def sandwich(nc, t):
    ctx = ExitStack()
    with ctx:
        def sb(name, shape, dt=F32):
            return ctx.enter_context(nc.sbuf_tensor(name, shape, dt))

        def sem(name):
            return ctx.enter_context(nc.semaphore(name))

        weights = sb("weights", [P, 8, CK * C], F32R)
        mix_hi = sb("mix_hi", [P, 3, TT], F32R)
        mix_lo = sb("mix_lo", [P, 3, TT], F32R)
        rw_hi = sb("rw_hi", [P, CK, TT], F32R)
        rw_lo = sb("rw_lo", [P, CK, TT], F32R)
        xin = sb("xin", [P, ST, C])
        xres = sb("xres", [P, ST, C])
        xnd = sb("xnd", [P, CK, TT])
        xnT = sb("xnT", [P, CK, TT + 1])
        mixf = sb("mixf", [P, 2, TT])
        k_sb = sb("k_sb", [P, 2, CK, TT])
        v_sb = sb("v_sb", [P, CK, TT])
        sr = sb("sr", [P, CK, TT])
        hb = sb("hb", [P, ST, C])
        run_max = sb("run_max", [P, 2, TT + 1])
        state = sb("state", [P, 2, 2, TT + 1])
        wkv = sb("wkv", [P, 12 * TT])

        def unit_pairs(n):
            return wkv[:, 4 * TT * n:4 * TT * (n + 1)].rearrange("p (b e t) -> p b e t", b=2, e=2)

        above = unit_pairs(0)
        below = unit_pairs(1)
        vexp = unit_pairs(2)
        gate_w = sb("gate_w", [P, 2, CK * E], F32R)
        carry = sb("carry", [P, CK, 3])
        vecs = sb("vecs", [P, 8, CK])
        stats = sb("stats", [P, ST, 6])
        mv = sb("mv", [P, 4, ST, 2])
        rstd = sb("rstd", [P, 4, ST])
        neg_half = sb("neg_half", [P, ST])
        ident = sb("ident", [P, P])
        TD, TF, MK, MV, MR, DECAY, NEGW, _ = range(8)

        banks = [ctx.enter_context(nc.psum_tensor(f"bank{g}", [P, 4, 512], F32)) for g in range(2)]

        names = """w_loaded0 w_loaded1 vec_loaded x_loaded xres_loaded x1_stored h_stored
        w_hi w_split decay_ready ident_ready half_ready
        ln1_stats ln1_moments ln1_rstd xn_ready turned xnT_ready shift_ready diff_ready mixed mix_hi_ready mix_lo_ready mix_used
        k_ready v_ready r_ready out_used y_ready
        seeded max_scanned gap_ready clamped carried exped vexped scanned scaled nd_ready recip_ln recip_ready ns_ready a_ready
        resid_ready rw_ready rw_hi_ready rw_lo_ready
        ln2_stats ln2_moments ln2_rstd yn_ready x1_ready ln3_stats ln3_moments ln3_rstd h_ready
        dve_step pool_step
        blank_ready slots_blank h_blank ysh_blank
        raw_loaded0 raw_loaded1 ffn_hi ffn_split gate_loaded gate_hi gate_split bias_loaded
        number_made number_ready causal_ready ones_ready seen_ready token_ready
        h_loaded h_turned h_hi_ready h_lo_ready up_done relu_ready square_ready s_hi_ready s_lo_ready down_done
        yout_ready ysh_stored logits_done score_ready sel_ready pos_ready route_step
        slots_ready scattered0 scattered1
        table_loaded gather_index scatter_index xd_turned xdT_ready e_up e_relu e_square e_down e_gated added
        ln4_stats ln4_moments ln4_rstd o_normed o_ready""".split()
        names += [f"{n}{q}" for n in ("w1_loaded", "w2_loaded", "xd_loaded") for q in range(EB)]
        names += [f"{n}{q}" for n in ("ysh_loaded", "x1_loaded", "out_stored") for q in range(FB)]
        S = {n: sem(n) for n in names}

        def W(j, part):
            return weights[:, 2 * j + part, :].rearrange("p (k d) -> p k d", k=CK)

        stage = [hb, sr]
        blank_slots = hb[:, 0, 0:2 * E].rearrange("p (e w) -> p e w", w=2)

        def flat(tile):
            return tile[:, :, :].rearrange("p a b -> p (a b)")

        su_hi, su_lo, sd_hi, sd_lo = (weights[:, 2 * n:2 * n + 2, :].rearrange("p a b -> p (a b)") for n in range(4))
        su = [w.rearrange("p (k d) -> p k d", k=CK) for w in (su_hi, su_lo)]
        sd = [w.rearrange("p (j c) -> p j c", j=SJ) for w in (sd_hi, sd_lo)]
        gate = [gate_w[:, n, :].rearrange("p (k e) -> p k e", k=CK) for n in range(2)]
        hT_hi, hT_lo, s_hi, s_lo = rw_hi, rw_lo, mix_hi, mix_lo
        relu = k_sb[:, 0, 0:2, :]
        square = k_sb[:, 1, 0:2, :]
        yout = v_sb
        choice = wkv[:, 8 * TT:8 * TT + 2 * TOPK * 2].rearrange("p (b k w) -> p b k w", b=2, k=TOPK)
        table = wkv[:, 9 * TT:9 * TT + E * 2].rearrange("p (e w) -> p e w", w=2)
        consts = flat(run_max)
        bias_row = consts[:, 0:E]
        number = consts[:, E:2 * E]
        causal = consts[:, 128:192].bitcast(BF16)
        ones = consts[:, 192:256].bitcast(BF16)
        sel = consts[:, 256:288].bitcast(BF16)
        seen = consts[:, 288:320].bitcast(BF16)
        token = consts[:, 320:321]
        number_i = consts[:, 384:448].bitcast(I32)
        token_i = consts[:, 448:449].bitcast(I32)
        gather_token = consts[:, 452:452 + EB].bitcast(U32)
        scatter_token = consts[:, 456:456 + EB].bitcast(U32)
        e_gates = consts[:, 460:460 + EB]
        scratch = flat(xnd)
        at = [0]

        def carve(*shape, dt=F32):
            n = 1
            for k in shape:
                n *= k
            v = scratch[:, at[0]:at[0] + n]
            at[0] += n
            if dt is not F32:
                v = v.bitcast(dt)
            return v.rearrange("p (a b) -> p a b", a=shape[0]) if len(shape) == 2 else v

        score = carve(2, E)
        biased = carve(E)
        group_top = carve(GROUPS, 8)
        group_score = carve(GROUPS)
        group_best = carve(8)
        group_index = carve(8, dt=U32)
        group_number = carve(8)
        group_hot = carve(TOPG, GROUPS)
        group_mask = carve(GROUPS)
        group_floor = carve(GROUPS)
        masked = carve(E)
        expert_best = carve(8)
        expert_index = carve(8, dt=U32)
        expert_number = carve(8)
        hot = carve(TOPK, E)
        product = carve(TOPK, E)
        sel_f = carve(E)
        weight = carve(TOPK)
        weight_sum = carve(1)
        place = carve(TOPK)
        slot_f = carve(TOPK)
        slot = carve(2, TOPK, dt=U32)

        halves = [flat(m)[:, b * CK * HID:(b + 1) * CK * HID] for m in (hb, sr) for b in range(2)] + \
                 [wkv[:, b * CK * HID:(b + 1) * CK * HID] for b in range(4)]
        w1_sb = [w.rearrange("p (k i) -> p k i", k=CK) for w in halves[0::2]]
        w2_sb = [w.rearrange("p (k c) -> p k c", k=IK) for w in halves[1::2]]
        xd_sb = [xres[:, q, :] for q in range(EB)]
        xdT = [flat(xnT)[:, q * C:(q + 1) * C].rearrange("p (k n) -> p k n", k=CK) for q in range(EB)]
        state_flat = state[:, :, :, :].rearrange("p a b c -> p (a b c)")
        e_hidden = [state_flat[:, b * HID:(b + 1) * HID] for b in range(2)]
        e_act = [state_flat[:, (2 + b) * HID:(3 + b) * HID].rearrange("p (k n) -> p k n", k=IK) for b in range(2)]
        e_out = [mixf[:, b, :] for b in range(2)]
        o_y = [xin[:, :, :], v_sb[:, :, :], k_sb[:, 0, :, :], k_sb[:, 1, :, :]]
        o_x = [weights[:, n, :].bitcast(F32).rearrange("p (s c) -> p s c", s=ST) for n in range(FB)]
        x_by_tile = t["x"].rearrange("(t s p) c -> t p s c", s=ST, p=P)
        x1_by_tile = t["x1"].rearrange("(t s p) c -> t p s c", s=ST, p=P)
        h_by_tile = t["h"][0:N, :].rearrange("(t s p) c -> t p s c", s=ST, p=P)

        ysh_by_tile = t["ysh"][0:N, :].rearrange("(t s p) c -> t p s c", s=ST, p=P)
        out_by_tile = t["out"].rearrange("(t s p) c -> t p s c", s=ST, p=P)
        slots_by_place = t["slots"].rearrange("(c e) w -> c e w", e=E)

        def tile_of(ap, tau):
            return ap[bass.ds(tau, 1)].rearrange("o p s c -> p (o s) c")

        def periods(eng, period):
            period(0, 0)
            with eng.Fori(0, (NT - 4) // 2) as i:
                period(2 * i + 1, 1)
                period(2 * i + 2, 0)
            for tau in range(NT - 3, NT):
                period(tau, tau % 2)

        def tiles(eng, tile):
            tile(0)
            with eng.Fori(0, NT - 2) as i:
                tile(i + 1)
            tile(NT - 1)

        def experts(eng, expert):
            for e in range(EB):
                expert(e, e, 0)
            with eng.Fori(0, E // EB - 2) as i:
                for q in range(EB):
                    expert(EB * i + EB + q, q, i + 1)
            for e in range(E - EB, E):
                expert(e, e % EB, e // EB)

        def within(e, ahead):
            return not (isinstance(e, int) and e + ahead >= E)

        def finals(eng, final):
            with eng.Fori(0, NT // FB) as i:
                for q in range(FB):
                    final(FB * i + q, q, i)

        def first(n):
            return isinstance(n, int) and n == 0

        def has(tau, ahead):
            return not (isinstance(tau, int) and tau + ahead >= NT)

        def back(tau):
            return not (isinstance(tau, int) and tau == 0)

        def after(eng, sm, value):
            eng.wait_ge(S[sm], value)
            eng.sem_inc(S["dve_step" if eng is dve_engine[0] else "pool_step"], 1)

        dve_engine = [None]
        block = ctx.enter_context(nc.Block())

        @block.sync
        def _(sp):
            for j, name in enumerate(("Wk", "Wv", "Wr", "Wo")):
                if j >= 2:
                    sp.wait_ge(S["w_split"], j - 1)
                sp.dma_start(stage[j % 2][:, :, :], t[name]).then_inc(S[f"w_loaded{j % 2}"], 16)
                if j == 0:
                    sp.dma_start(vecs[:, 0:5, :], t["vecs"]).then_inc(S["vec_loaded"], 16)
                    sp.dma_start(xin[:, :, :], x_by_tile[0]).then_inc(S["x_loaded"], 16)
            sp.wait_ge(S["xn_ready"], ST)
            sp.dma_start(xin[:, :, :], x_by_tile[1]).then_inc(S["x_loaded"], 16)

            def period(tau, par):
                if has(tau, 2):
                    sp.wait_ge(S["xn_ready"], ST * (tau + 2))
                    sp.dma_start(xin[:, :, :], tile_of(x_by_tile, tau + 2)).then_inc(S["x_loaded"], 16)
                if back(tau):
                    store_tail(tau - 1)
                    sp.wait_ge(S["x1_stored"], 16 * tau)
                sp.dma_start(xres[:, :, :], tile_of(x_by_tile, tau)).then_inc(S["xres_loaded"], 16)

            def load_expert(e, q):
                if isinstance(e, int):
                    e1, e2 = t["w1"][e], t["w2"][e]
                else:
                    e1, e2 = (t[w][bass.ds(e, 1)].rearrange("o p k -> p (o k)") for w in ("w1", "w2"))
                sp.dma_start(w1_sb[q].rearrange("p k i -> p (k i)"), e1).then_inc(S[f"w1_loaded{q}"], 16)
                sp.dma_start(w2_sb[q].rearrange("p k i -> p (k i)"), e2).then_inc(S[f"w2_loaded{q}"], 16)

            def store_tail(tau):
                sp.wait_ge(S["h_ready"], ST * (tau + 1))
                sp.dma_start(tile_of(x1_by_tile, tau), xres[:, :, :]).then_inc(S["x1_stored"], 16)
                sp.dma_start(tile_of(h_by_tile, tau), hb[:, :, :]).then_inc(S["h_stored"], 16)

            sp.wait_ge(S["blank_ready"], 2)
            sp.dma_start(slots_by_place, blank_slots).then_inc(S["slots_blank"], 16)
            sp.dma_start(t["h"][N:N + P, :], hb[:, 1, :]).then_inc(S["h_blank"], 16)
            sp.dma_start(t["ysh"][N:N + P, :], hb[:, 1, :]).then_inc(S["ysh_blank"], 16)

            periods(sp, period)

            raw = [flat(xin), flat(xnd)]
            sp.wait_ge(S["mix_used"], 12 * NT)
            sp.wait_ge(S["mixed"], 12 * NT)
            for q in range(4):
                if q >= 2:
                    sp.wait_ge(S["ffn_split"], q - 1)
                src = t["su"] if q < 2 else t["sd"]
                sp.dma_start(raw[q % 2], src[:, q % 2, :]).then_inc(S[f"raw_loaded{q % 2}"], 16)
                if q == 1:
                    sp.wait_ge(S["carried"], 2 * CK * NT)
                    sp.dma_start(bias_row, t["e_bias"].to_broadcast([P, E])).then_inc(S["bias_loaded"], 16)
                    sp.wait_ge(S["k_ready"], CK * NT)
                    sp.wait_ge(S["gap_ready"], CK * NT)
                    sp.dma_start(flat(k_sb[:, 0, :, :])[:, 0:CK * E], t["gate"]).then_inc(S["gate_loaded"], 16)
            store_tail(NT - 1)
            sp.wait_ge(S["x1_stored"], 16 * NT)
            sp.wait_ge(S["h_stored"], 16 * NT)
            sp.wait_ge(S["rw_lo_ready"], CK * NT)
            sp.wait_ge(S["ffn_split"], 4)
            sp.dma_start(xin[:, :, :], h_by_tile[0]).then_inc(S["h_loaded"], 16)
            sp.wait_ge(S["h_blank"], 16)
            sp.wait_ge(S["ysh_blank"], 16)
            for q in range(EB):
                load_expert(q, q)

            def tile(k):
                if has(k, 1):
                    sp.wait_ge(S["h_turned"], CK * (k + 1))
                    sp.dma_start(xin[:, :, :], tile_of(h_by_tile, k + 1)).then_inc(S["h_loaded"], 16)
                sp.wait_ge(S["yout_ready"], ST * (k + 1))
                sp.dma_start(tile_of(ysh_by_tile, k), yout[:, :, :]).then_inc(S["ysh_stored"], 16)

            tiles(sp, tile)
            for b in range(2):
                sp.wait_ge(S[f"scattered{b}"], 16 * TOPK * ST * NT // 2)
            sp.dma_start(table, slots_by_place).then_inc(S["table_loaded"], 16)

            def load_x1(k, q):
                sp.dma_start(o_x[q], tile_of(x1_by_tile, k)).then_inc(S[f"x1_loaded{q}"], 16)

            sp.wait_ge(S["down_done"], SJ * NT)
            for q in range(FB):
                load_x1(q, q)
            sp.wait_ge(S["ysh_stored"], 16 * NT)

            def expert(e, q, m):
                if within(e, EB):
                    sp.wait_ge(S["e_up"], e + 1)
                    sp.wait_ge(S["e_down"], e + 1)
                    load_expert(e + EB, q)

            experts(sp, expert)
            sp.wait_ge(S["added"], 16 * E)

            def load_ysh(k, q):
                sp.dma_start(o_y[q], tile_of(ysh_by_tile, k)).then_inc(S[f"ysh_loaded{q}"], 16)

            def store_out(k, q):
                sp.wait_ge(S["o_ready"], ST * (k + 1))
                sp.dma_start(tile_of(out_by_tile, k), o_y[q]).then_inc(S[f"out_stored{q}"], 16)

            for q in range(FB):
                load_ysh(q, q)
            for k in range(FB):
                store_out(k, k)
                load_x1(k + FB, k)
                sp.wait_ge(S[f"out_stored{k}"], 16)
                load_ysh(k + FB, k)
            for k in range(FB, NT):
                store_out(k, k % FB)
            for q in range(FB):
                sp.wait_ge(S[f"out_stored{q}"], 16 * NT // FB)

        @block.tensor
        def _(pe):
            def group(tau, job):
                return banks[(1 + tau + job) % 2]

            def transposes(bank, tau):
                pe.wait_ge(S["xn_ready"], ST * (tau + 1))
                for c in range(CK):
                    for s in range(ST):
                        mm = pe.transpose(bank[:, c, s * P:(s + 1) * P], xnd[:, s, c * P:(c + 1) * P], ident[:, :])
                    mm.then_inc(S["turned"], 1)

            def project(bank, tau, j):
                for ck in range(CK):
                    pe.wait_ge(S["mix_lo_ready"], 12 * tau + 4 * j + ck + 1)
                    slot = (4 * j + ck) % 3
                    for d in range(CK):
                        hi = W(j, 0)[:, ck, d * P:(d + 1) * P]
                        lo = W(j, 1)[:, ck, d * P:(d + 1) * P]
                        pe.matmul(bank[:, d, :], hi, mix_hi[:, slot, :], start=(ck == 0), stop=False)
                        pe.matmul(bank[:, d, :], hi, mix_lo[:, slot, :], start=False, stop=False)
                        mm = pe.matmul(bank[:, d, :], lo, mix_hi[:, slot, :], start=False, stop=(ck == CK - 1))
                    mm.then_inc(S["mix_used"], 1)

            def output(bank, tau):
                for ck in range(CK):
                    pe.wait_ge(S["rw_lo_ready"], 4 * tau + ck + 1)
                    for s in range(ST):
                        hi = rw_hi[:, ck, s * P:(s + 1) * P]
                        lo = rw_lo[:, ck, s * P:(s + 1) * P]
                        pe.matmul(bank[:, s, :], hi, W(3, 0)[:, ck, :], start=(ck == 0), stop=False)
                        pe.matmul(bank[:, s, :], hi, W(3, 1)[:, ck, :], start=False, stop=False)
                        mm = pe.matmul(bank[:, s, :], lo, W(3, 0)[:, ck, :], start=False, stop=(ck == CK - 1))
                    mm.then_inc(S["out_used"], 1)

            pe.wait_ge(S["ident_ready"], 2)
            transposes(banks[0], 0)
            pe.wait_ge(S["w_split"], 1)
            project(banks[1], 0, KJ)
            pe.wait_ge(S["xnT_ready"], 4)
            pe.wait_ge(S["w_split"], 2)
            project(banks[0], 0, VJ)
            pe.wait_ge(S["k_ready"], 4)
            pe.wait_ge(S["w_split"], 3)
            project(banks[1], 0, RJ)
            pe.wait_ge(S["v_ready"], 4)
            transposes(banks[0], 1)
            pe.wait_ge(S["w_split"], 4)

            def period(tau, par):
                if has(tau, 1):
                    if back(tau):
                        pe.wait_ge(S["xnT_ready"], 4 * (tau + 2))
                    else:
                        pe.wait_ge(S["r_ready"], 4)
                    project(group(par, 0), tau + 1, KJ)
                    if back(tau):
                        pe.wait_ge(S["y_ready"], 4 * tau)
                    else:
                        pe.wait_ge(S["xnT_ready"], 8)
                    project(group(par, 1), tau + 1, VJ)
                    pe.wait_ge(S["k_ready"], 4 * (tau + 2))
                    project(group(par, 2), tau + 1, RJ)
                if has(tau, 2):
                    pe.wait_ge(S["v_ready"], 4 * (tau + 2))
                    transposes(group(par, 3), tau + 2)
                if has(tau, 1):
                    pe.wait_ge(S["r_ready"], 4 * (tau + 2))
                output(group(par, 4), tau)

            periods(pe, period)

            y_bank, (up_bank, turn_bank, route_bank) = banks[0], (banks[1][:, 0:2, :], banks[1][:, 2, :], banks[1][:, 3, :])

            def h_transpose(k, c):
                if c == 0:
                    pe.wait_ge(S["h_loaded"], 16 * (k + 1))
                    if not first(k):
                        pe.wait_ge(S["score_ready"], ST * k)
                if not (first(k) and c == 0):
                    pe.wait_ge(S["h_lo_ready"], CK * k + c)
                for s in range(ST):
                    mm = pe.transpose(turn_bank[:, s * P:(s + 1) * P], xin[:, s, c * P:(c + 1) * P], ident[:, :])
                mm.then_inc(S["h_turned"], 1)

            def logits(k, s):
                if s == 0:
                    pe.wait_ge(S["h_lo_ready"], CK * (k + 1))
                if not (first(k) and s == 0):
                    pe.wait_ge(S["score_ready"], ST * k + s)
                out = turn_bank[:, 0:E]
                for ck in range(CK):
                    hi, lo = (x[:, ck, s * P:(s + 1) * P] for x in (hT_hi, hT_lo))
                    pe.matmul(out, hi, gate[0][:, ck, :], start=(ck == 0), stop=False)
                    pe.matmul(out, hi, gate[1][:, ck, :], start=False, stop=False)
                    mm = pe.matmul(out, lo, gate[0][:, ck, :], start=False, stop=(ck == CK - 1))
                mm.then_inc(S["logits_done"], 1)

            def places(k, s):
                g = ST * k + s
                pe.wait_ge(S["sel_ready"], g + 1)
                pe.wait_ge(S["seen_ready"], g + 1)
                out = route_bank[:, 0:E]
                pe.matmul(out, causal, sel, start=True, stop=False)
                pe.matmul(out, ones, seen, start=False, stop=True).then_inc(S["pos_ready"], 1)

            def up(k, j):
                if not (first(k) and j < 2):
                    pe.wait_ge(S["relu_ready"], SJ * k + j - 1)
                for ck in range(CK):
                    hi, lo = (x[:, ck, j * P:(j + 1) * P] for x in su)
                    pe.matmul(up_bank[:, j % 2, :], hi, hT_hi[:, ck, :], start=(ck == 0), stop=False)
                    pe.matmul(up_bank[:, j % 2, :], hi, hT_lo[:, ck, :], start=False, stop=False)
                    mm = pe.matmul(up_bank[:, j % 2, :], lo, hT_hi[:, ck, :], start=False, stop=(ck == CK - 1))
                mm.then_inc(S["up_done"], 1)

            def down(k, j):
                pe.wait_ge(S["s_lo_ready"], SJ * k + j + 1)
                if j == 0 and not first(k):
                    pe.wait_ge(S["yout_ready"], ST * k)
                for s in range(ST):
                    hi, lo = (x[:, j % 3, s * P:(s + 1) * P] for x in (s_hi, s_lo))
                    pe.matmul(y_bank[:, s, :], hi, sd[0][:, j, :], start=(j == 0), stop=False)
                    pe.matmul(y_bank[:, s, :], hi, sd[1][:, j, :], start=False, stop=False)
                    mm = pe.matmul(y_bank[:, s, :], lo, sd[0][:, j, :], start=False, stop=(j == SJ - 1))
                mm.then_inc(S["down_done"], 1)

            pe.wait_ge(S["y_ready"], ST * NT)
            pe.wait_ge(S["r_ready"], ST * NT)
            for c in range(CK):
                h_transpose(0, c)
            pe.wait_ge(S["gate_split"], 1)
            pe.wait_ge(S["ffn_split"], 4)
            pe.wait_ge(S["causal_ready"], 2)
            pe.wait_ge(S["ones_ready"], 1)

            def tile(k):
                for j in range(SJ):
                    if j % 2 == 0:
                        logits(k, j // 2)
                    if j == 2 and not first(k):
                        places(k - 1, 3)
                    if j in (4, 6):
                        places(k, j // 2 - 2)
                    up(k, j)
                    if j >= 2:
                        down(k, j - 2)
                if has(k, 1):
                    h_transpose(k + 1, 0)
                down(k, SJ - 2)
                if has(k, 1):
                    h_transpose(k + 1, 1)
                down(k, SJ - 1)
                if has(k, 1):
                    for c in range(2, CK):
                        h_transpose(k + 1, c)
                places(k, 2)

            tiles(pe, tile)
            places(NT - 1, 3)

            def xd_transpose(e, q, m):
                b = q % 2
                pe.wait_ge(S[f"xd_loaded{q}"], 16 * (m + 1))
                if not (isinstance(e, int) and e < 2):
                    pe.wait_ge(S["xdT_ready"], e - 1)
                for c in range(CK):
                    mm = pe.transpose(banks[0][:, b, c * P:(c + 1) * P], xd_sb[q][:, c * P:(c + 1) * P], ident[:, :])
                mm.then_inc(S["xd_turned"], 1)

            def e_first(e, q, m):
                b = q % 2
                pe.wait_ge(S[f"w1_loaded{q}"], 16 * (m + 1))
                pe.wait_ge(S["xdT_ready"], e + 1)
                if not (isinstance(e, int) and e < 2):
                    pe.wait_ge(S["e_relu"], e - 1)
                for i in range(IK):
                    for ck in range(CK):
                        mm = pe.matmul(banks[0][:, 2 + b, i * CAP:(i + 1) * CAP], w1_sb[q][:, ck, i * P:(i + 1) * P], xdT[q][:, ck, :],
                                       start=(ck == 0), stop=(ck == CK - 1))
                mm.then_inc(S["e_up"], 1)

            def e_second(e, q, m):
                b = q % 2
                pe.wait_ge(S[f"w2_loaded{q}"], 16 * (m + 1))
                pe.wait_ge(S["e_square"], e + 1)
                if not (isinstance(e, int) and e < 2):
                    pe.wait_ge(S["e_gated"], e - 1)
                for i in range(IK):
                    mm = pe.matmul(banks[1][:, b, :], e_act[b][:, i, :], w2_sb[q][:, i, :], start=(i == 0), stop=(i == IK - 1))
                mm.then_inc(S["e_down"], 1)

            pe.wait_ge(S["yout_ready"], ST * NT)
            pe.wait_ge(S["relu_ready"], SJ * NT)
            for e in range(2):
                xd_transpose(e, e, 0)
            e_first(0, 0, 0)

            def expert(e, q, m):
                if within(e, 2):
                    xd_transpose(e + 2, (q + 2) % EB, m + (q + 2) // EB)
                if within(e, 1):
                    e_first(e + 1, (q + 1) % EB, m + (q + 1) // EB)
                e_second(e, q, m)

            experts(pe, expert)

        @block.scalar
        def _(act):
            def group(tau, job):
                return banks[(1 + tau + job) % 2]

            for j in range(4):
                act.wait_ge(S[f"w_loaded{j % 2}"], 16 * (j // 2 + 1))
                act.activation(W(j, 0), stage[j % 2][:, :, :], ACT.Copy, scale=-1.0 if j == 3 else 1.0).then_inc(S["w_hi"], 1)
                if j == 0:
                    act.wait_ge(S["vec_loaded"], 16)
                    act.activation(vecs[:, DECAY, :], vecs[:, TD, :], ACT.Exp).then_inc(S["decay_ready"], 1)

            def xnT_read(bank, tau):
                act.wait_ge(S["shift_ready"], tau + 1)
                for c in range(CK):
                    act.wait_ge(S["turned"], 4 * tau + c + 1)
                    act.activation(xnT[:, c, 1:TT + 1], bank[:, c, :], ACT.Copy).then_inc(S["xnT_ready"], 1)

            def round_mix(tau, j, ck):
                n = 4 * j + ck
                act.wait_ge(S["mixed"], 12 * tau + n + 1)
                if not (isinstance(tau, int) and 12 * tau + n < 3):
                    act.wait_ge(S["mix_used"], 12 * tau + n - 2)
                act.activation(mix_hi[:, n % 3, :], mixf[:, n % 2, :], ACT.Copy).then_inc(S["mix_hi_ready"], 1)

            def k_read(bank, tau, par):
                for c in range(CK):
                    act.wait_ge(S["mix_used"], 12 * tau + 4 * KJ + 4)
                    if not (isinstance(tau, int) and tau < 2):
                        act.wait_ge(S["gap_ready"], 4 * (tau - 2) + c + 1)
                    act.activation(k_sb[:, par, c, :], bank[:, c, :], ACT.Copy).then_inc(S["k_ready"], 1)

            def v_read(bank, tau, c):
                act.wait_ge(S["mix_used"], 12 * tau + 4 * VJ + 4)
                if not (isinstance(tau, int) and tau < 1):
                    act.wait_ge(S["vexped"], 4 * (tau - 1) + c + 1)
                act.activation(v_sb[:, c, :], bank[:, c, :], ACT.Copy).then_inc(S["v_ready"], 1)

            def r_read(bank, tau, c):
                act.wait_ge(S["mix_used"], 12 * tau + 4 * RJ + 4)
                if not (isinstance(tau, int) and tau < 1):
                    act.wait_ge(S["ns_ready"], 4 * (tau - 1) + c + 1)
                else:
                    act.wait_ge(S["w_split"], 4)
                act.activation(sr[:, c, :], bank[:, c, :], ACT.Sigmoid).then_inc(S["r_ready"], 1)

            def exps(tau, c):
                act.wait_ge(S["clamped"], 16 * tau + 4 * c + 4)
                act.activation(above[:, c % 2, :, :], above[:, c % 2, :, :], ACT.Exp, scale=-1.0).then_inc(S["exped"], 1)
                act.activation(below[:, c % 2, :, :], below[:, c % 2, :, :], ACT.Exp).then_inc(S["exped"], 1)

            def recip(tau, c):
                act.wait_ge(S["nd_ready"], 8 * tau + 2 * c + 2)
                act.activation(vexp[:, c % 2, 0, :], above[:, c % 2, 0, :], ACT.Ln).then_inc(S["recip_ln"], 1)
                act.wait_ge(S["recip_ln"], 4 * tau + c + 1)
                act.activation(vexp[:, c % 2, 0, :], vexp[:, c % 2, 0, :], ACT.Exp, scale=-1.0).then_inc(S["recip_ready"], 1)

            def rw_round(tau, c):
                act.wait_ge(S["rw_ready"], 4 * tau + c + 1)
                if back(tau):
                    act.wait_ge(S["out_used"], 4 * (tau - 1) + c + 1)
                act.activation(rw_hi[:, c, :], above[:, c % 2, 1, :], ACT.Copy).then_inc(S["rw_hi_ready"], 1)

            def y_read(bank, tau):
                if not (isinstance(tau, int) and tau < 1):
                    act.wait_ge(S["h_stored"], 16 * tau)
                for s in range(ST):
                    act.wait_ge(S["out_used"], 4 * tau + 4)
                    act.activation(hb[:, s, :], bank[:, s, :], ACT.Copy).then_inc(S["y_ready"], 1)

            def exp_table():
                act.preload_act_table_set("natural_log_exp_and_others")

            xnT_read(banks[0], 0)
            for j in range(3):
                for ck in range(CK):
                    round_mix(0, j, ck)
                if j == KJ:
                    k_read(banks[1], 0, 0)
                if j == VJ:
                    for c in range(CK):
                        v_read(banks[0], 0, c)
            for c in range(CK):
                r_read(banks[1], 0, c)
            xnT_read(banks[0], 1)
            exp_table()

            def period(tau, par):
                g = 1 if back(tau) else 0
                if back(tau):
                    y_read(group(par - 1, 4), tau - 1)
                exps(tau, 0)
                if has(tau, 1):
                    for ck in range(CK):
                        round_mix(tau + 1, KJ, ck)
                recip(tau, 0)
                exps(tau, 1)
                if has(tau, 1):
                    for ck in range(CK):
                        round_mix(tau + 1, VJ, ck)
                    k_read(group(par, 0), tau + 1, 1 - par)
                rw_round(tau, 0)
                recip(tau, 1)
                exps(tau, 2)
                if has(tau, 1):
                    for c in range(2):
                        v_read(group(par, 1), tau + 1, c)
                    for ck in range(CK):
                        round_mix(tau + 1, RJ, ck)
                rw_round(tau, 1)
                recip(tau, 2)
                exps(tau, 3)
                if has(tau, 1):
                    for c in range(2, 4):
                        v_read(group(par, 1), tau + 1, c)
                rw_round(tau, 2)
                recip(tau, 3)
                if has(tau, 2):
                    xnT_read(group(par, 3), tau + 2)
                rw_round(tau, 3)
                if has(tau, 1):
                    for c in range(CK):
                        r_read(group(par, 2), tau + 1, c)
                    exp_table()

            periods(act, period)
            y_read(group(1, 4), NT - 1)

            raw = [flat(xin), flat(xnd)]
            act.wait_ge(S["out_used"], CK * NT)
            for q in range(4):
                act.wait_ge(S[f"raw_loaded{q % 2}"], 16 * (q // 2 + 1))
                act.activation((su_hi if q < 2 else sd_hi)[:, (q % 2) * 2048:(q % 2 + 1) * 2048], raw[q % 2], ACT.Copy).then_inc(S["ffn_hi"], 1)
            act.wait_ge(S["gate_loaded"], 16)
            act.activation(gate_w[:, 0, :], flat(k_sb[:, 0, :, :])[:, 0:CK * E], ACT.Copy).then_inc(S["gate_hi"], 1)

            y_bank, (up_bank, turn_bank, route_bank) = banks[0], (banks[1][:, 0:2, :], banks[1][:, 2, :], banks[1][:, 3, :])

            def h_hi(k, c):
                if not first(k):
                    act.wait_ge(S["up_done"], SJ * k)
                    act.wait_ge(S["logits_done"], ST * k)
                act.wait_ge(S["h_turned"], CK * k + c + 1)
                act.activation(hT_hi[:, c, :], turn_bank, ACT.Copy).then_inc(S["h_hi_ready"], 1)

            def scores(k, s):
                act.wait_ge(S["logits_done"], ST * k + s + 1)
                if not (first(k) and s < 2):
                    act.wait_ge(S["slots_ready"], ST * k + s - 1)
                act.activation(score[:, s % 2, :], turn_bank[:, 0:E], ACT.Sigmoid).then_inc(S["score_ready"], 1)

            def hidden(k, j):
                act.wait_ge(S["up_done"], SJ * k + j + 1)
                if not (first(k) and j < 2):
                    act.wait_ge(S["square_ready"], SJ * k + j - 1)
                act.activation(relu[:, j % 2, :], up_bank[:, j % 2, :], ACT.Relu).then_inc(S["relu_ready"], 1)
                act.wait_ge(S["relu_ready"], SJ * k + j + 1)
                if not (first(k) and j < 3):
                    act.wait_ge(S["down_done"], SJ * k + j - (2 if j < 2 else 3) + 1)
                act.activation(s_hi[:, j % 3, :], relu[:, j % 2, :], ACT.Square).then_inc(S["s_hi_ready"], 1)

            def yout_read(k):
                act.wait_ge(S["down_done"], SJ * (k + 1))
                if not first(k):
                    act.wait_ge(S["ysh_stored"], 16 * k)
                for s in range(ST):
                    act.activation(yout[:, s, :], y_bank[:, s, :], ACT.Copy).then_inc(S["yout_ready"], 1)

            for c in range(CK):
                h_hi(0, c)
            act.wait_ge(S["gate_split"], 1)

            def tile(k):
                for j in range(SJ):
                    if j % 2 == 0:
                        scores(k, j // 2)
                    hidden(k, j)
                if has(k, 1):
                    for c in range(CK):
                        h_hi(k + 1, c)
                yout_read(k)

            tiles(act, tile)

            def xdT_read(e, q):
                act.wait_ge(S["xd_turned"], e + 1)
                if not (isinstance(e, int) and e < EB):
                    act.wait_ge(S["e_up"], e - EB + 1)
                act.activation(xdT[q].rearrange("p k n -> p (k n)"), banks[0][:, q % 2, :], ACT.Copy).then_inc(S["xdT_ready"], 1)

            def e_relu(e, q):
                act.wait_ge(S["e_up"], e + 1)
                if not (isinstance(e, int) and e < 2):
                    act.wait_ge(S["e_square"], e - 1)
                act.activation(e_hidden[q % 2], banks[0][:, 2 + q % 2, 0:HID], ACT.Relu).then_inc(S["e_relu"], 1)

            def e_gate(e, q):
                act.wait_ge(S["e_down"], e + 1)
                act.wait_ge(S["scatter_index"], 2 * e + 2)
                if not (isinstance(e, int) and e < 2):
                    act.wait_ge(S["added"], 16 * (e - 1))
                act.activation(e_out[q % 2], banks[1][:, q % 2, :], ACT.Copy, scale=e_gates[:, q:q + 1]).then_inc(S["e_gated"], 1)

            for e in range(2):
                xdT_read(e, e)
            e_relu(0, 0)

            def expert(e, q, m):
                if within(e, 2):
                    xdT_read(e + 2, (q + 2) % EB)
                if within(e, 1):
                    e_relu(e + 1, (q + 1) % EB)
                e_gate(e, q)

            experts(act, expert)

        @block.gpsimd
        def _(pool):
            pool.memset(ident[:, :], 0.0).then_inc(S["ident_ready"], 1)
            pool.memset(neg_half[:, :], -0.5).then_inc(S["half_ready"], 1)
            pool.wait_ge(S["ident_ready"], 1)
            pool.affine_select(out=ident[:, :], in_=ident[:, :], compare_op=ALU.not_equal, fill=1.0, base=0,
                               pattern=[[-1, P]], channel_multiplier=1).then_inc(S["ident_ready"], 1)
            pool.wait_ge(S["half_ready"], 1)

            def inv_std(ln, tau):
                pool.wait_ge(S[f"ln{ln}_moments"], ST * (tau + 1))
                pool.sem_inc(S["pool_step"], 1)
                pool.tensor_scalar(rstd[:, ln - 1, :], mv[:, ln - 1, :, 1], EPS, None, ALU.add).then_inc(S[f"ln{ln}_rstd"], 1)
                pool.wait_ge(S[f"ln{ln}_rstd"], 2 * tau + 1)
                pool.tensor_tensor(rstd[:, ln - 1, :], rstd[:, ln - 1, :], neg_half[:, :], ALU.pow).then_inc(S[f"ln{ln}_rstd"], 1)

            def mix_rest(tau, j, ck):
                n = 4 * j + ck
                pool.wait_ge(S["mix_hi_ready"], 12 * tau + n + 1)
                pool.tensor_tensor(mix_lo[:, n % 3, :], mixf[:, n % 2, :], mix_hi[:, n % 3, :].bitcast(F32),
                                   ALU.subtract).then_inc(S["mix_lo_ready"], 1)

            def times_v(tau, c):
                pool.wait_ge(S["exped"], 8 * tau + 2 * c + 2)
                pool.wait_ge(S["v_ready"], 4 * tau + c + 1)
                for e in range(2):
                    ins = pool.tensor_tensor(vexp[:, c % 2, e, :], below[:, c % 2, e, :], v_sb[:, c, :], ALU.mult)
                ins.then_inc(S["vexped"], 1)

            def gated_num(tau, c):
                pool.wait_ge(S["nd_ready"], 8 * tau + 2 * c + 2)
                pool.wait_ge(S["r_ready"], 4 * tau + c + 1)
                pool.tensor_tensor(vexp[:, c % 2, 1, :], above[:, c % 2, 1, :], sr[:, c, :], ALU.mult).then_inc(S["ns_ready"], 1)
                pool.wait_ge(S["ns_ready"], 4 * tau + c + 1)
                pool.wait_ge(S["recip_ready"], 4 * tau + c + 1)
                pool.tensor_tensor(vexp[:, c % 2, 1, :], vexp[:, c % 2, 1, :], vexp[:, c % 2, 0, :], ALU.mult).then_inc(S["a_ready"], 1)

            def rw_rest(tau, c):
                pool.wait_ge(S["rw_hi_ready"], 4 * tau + c + 1)
                pool.tensor_tensor(rw_lo[:, c, :], above[:, c % 2, 1, :], rw_hi[:, c, :].bitcast(F32),
                                   ALU.subtract).then_inc(S["rw_lo_ready"], 1)

            def residual(tau):
                pool.wait_ge(S["xres_loaded"], 16 * (tau + 1))
                for s in range(ST):
                    pool.wait_ge(S["yn_ready"], ST * tau + s + 1)
                    pool.tensor_tensor(xres[:, s, :], xres[:, s, :], hb[:, s, :], ALU.add).then_inc(S["x1_ready"], 1)

            inv_std(1, 0)
            pool.wait_ge(S["w_split"], 3)
            pool.memset(hb[:, 0:2, :], 0.0).then_inc(S["blank_ready"], 1)
            pool.wait_ge(S["blank_ready"], 1)
            pool.iota(blank_slots[:, :, TOKEN], pattern=[[0, E]], base=N, channel_multiplier=1,
                      allow_small_or_imprecise_dtypes=True).then_inc(S["blank_ready"], 1)
            for j in range(3):
                for ck in range(CK):
                    mix_rest(0, j, ck)
            inv_std(1, 1)

            def period(tau, par):
                times_v(tau, 0)
                if has(tau, 1):
                    for ck in range(CK):
                        mix_rest(tau + 1, KJ, ck)
                gated_num(tau, 0)
                times_v(tau, 1)
                if has(tau, 1):
                    for ck in range(CK):
                        mix_rest(tau + 1, VJ, ck)
                rw_rest(tau, 0)
                gated_num(tau, 1)
                times_v(tau, 2)
                if back(tau):
                    inv_std(2, tau - 1)
                    residual(tau - 1)
                if has(tau, 1):
                    for ck in range(CK):
                        mix_rest(tau + 1, RJ, ck)
                rw_rest(tau, 1)
                gated_num(tau, 2)
                times_v(tau, 3)
                if has(tau, 2):
                    inv_std(1, tau + 2)
                rw_rest(tau, 2)
                if back(tau):
                    inv_std(3, tau - 1)
                gated_num(tau, 3)
                rw_rest(tau, 3)

            periods(pool, period)
            inv_std(2, NT - 1)
            residual(NT - 1)
            inv_std(3, NT - 1)

            pool.wait_ge(S["carried"], 2 * CK * NT)
            pool.iota(number_i, pattern=[[1, E]], base=0, channel_multiplier=0).then_inc(S["number_made"], 1)
            pool.iota(token_i, pattern=[[0, 1]], base=0, channel_multiplier=1).then_inc(S["number_made"], 1)
            pool.memset(ones, 1.0).then_inc(S["ones_ready"], 1)
            pool.memset(causal, 1.0).then_inc(S["causal_ready"], 1)
            pool.memset(seen, 0.0).then_inc(S["seen_ready"], 1)
            pool.wait_ge(S["causal_ready"], 1)
            pool.affine_select(out=causal, in_=causal, compare_op=ALU.is_gt, fill=0.0, base=0,
                               pattern=[[1, P]], channel_multiplier=-1).then_inc(S["causal_ready"], 1)
            pool.wait_ge(S["slots_blank"], 16)

            def tile(k):
                for s in range(ST):
                    pool.wait_ge(S["slots_ready"], ST * k + s + 1)
                    pool.sem_inc(S["pool_step"], 1)
                    for c in range(TOPK):
                        pool.indirect_dma_start(t["slots"], bass.IndirectOffsetOnAxis(ap=slot[:, s % 2, c:c + 1], axis=0), choice[:, s % 2, c, :], None,
                                                bounds_check=E * CAP - 1, oob_is_err=False).then_inc(S[f"scattered{s % 2}"], 16)

            tiles(pool, tile)
            pool.wait_ge(S["ysh_stored"], 16 * NT)

            def gather(e, q):
                pool.wait_ge(S["gather_index"], e + 1)
                if not (isinstance(e, int) and e < EB):
                    pool.wait_ge(S["xd_turned"], e - EB + 1)
                pool.sem_inc(S["pool_step"], 1)
                pool.indirect_dma_start(xd_sb[q], None, t["h"], bass.IndirectOffsetOnAxis(ap=gather_token[:, q:q + 1], axis=0)).then_inc(S[f"xd_loaded{q}"], 16)

            for e in range(EB):
                gather(e, e)

            def expert(e, q, m):
                if within(e, EB):
                    gather(e + EB, q)
                pool.wait_ge(S["e_gated"], e + 1)
                pool.wait_ge(S["scatter_index"], 2 * e + 2)
                if not first(e):
                    pool.wait_ge(S["added"], 16 * e)
                pool.sem_inc(S["pool_step"], 1)
                pool.indirect_dma_start(t["ysh"], bass.IndirectOffsetOnAxis(ap=scatter_token[:, q:q + 1], axis=0), e_out[q % 2], None,
                                        compute_op=ALU.add).then_inc(S["added"], 16)

            experts(pool, expert)

            def final(k, q, m):
                inv_std(4, k)
                pool.wait_ge(S[f"x1_loaded{q}"], 16 * (m + 1))
                for s in range(ST):
                    pool.wait_ge(S["o_normed"], ST * k + s + 1)
                    pool.tensor_tensor(o_y[q][:, s, :], o_y[q][:, s, :], o_x[q][:, s, :], ALU.add).then_inc(S["o_ready"], 1)

            finals(pool, final)

        @block.vector
        def _(dve):
            dve_engine[0] = dve
            for j in range(4):
                dve.wait_ge(S["w_hi"], j + 1)
                hi = W(j, 0).bitcast(F32)
                if j == 3:
                    dve.scalar_tensor_tensor(out=W(j, 1), in0=stage[j % 2][:, :, :], scalar=-1.0, in1=hi,
                                             op0=ALU.mult, op1=ALU.subtract).then_inc(S["w_split"], 1)
                else:
                    dve.tensor_tensor(W(j, 1), stage[j % 2][:, :, :], hi, ALU.subtract).then_inc(S["w_split"], 1)
                if j == 0:
                    dve.wait_ge(S["decay_ready"], 1)
                    dve.tensor_scalar(vecs[:, NEGW, :], vecs[:, DECAY, :], -1.0, None, ALU.mult).then_inc(S["decay_ready"], 1)

            def moments(ln, src, tau):
                for s in range(ST):
                    dve.bn_stats(stats[:, s, :], src[:, s, :]).then_inc(S[f"ln{ln}_stats"], 1)
                after(dve, f"ln{ln}_stats", ST * (tau + 1))
                for s in range(ST):
                    dve.bn_aggr(mv[:, ln - 1, s, :], stats[:, s, :]).then_inc(S[f"ln{ln}_moments"], 1)

            def normalise(ln, dst, src, tau, done):
                dve.wait_ge(S[f"ln{ln}_rstd"], 2 * tau + 2)
                for s in range(ST):
                    dve.tensor_scalar(dst[:, s, :], src[:, s, :], mv[:, ln - 1, s, 0:1], rstd[:, ln - 1, s:s + 1],
                                      ALU.subtract, ALU.mult).then_inc(S[done], 1)

            def ln1_moments(tau):
                dve.wait_ge(S["x_loaded"], 16 * (tau + 1))
                moments(1, xin, tau)

            def ln1_normalise(tau):
                if not (isinstance(tau, int) and tau < 1):
                    dve.wait_ge(S["mixed"], 12 * tau)
                normalise(1, xnd, xin, tau, "xn_ready")

            def shift(tau, par):
                if par == 0:
                    if not (isinstance(tau, int) and tau < 1):
                        dve.wait_ge(S["mixed"], 12 * tau)
                    dve.memset(xnT[:, :, 0:1], 0.0).then_inc(S["shift_ready"], 1)
                else:
                    dve.wait_ge(S["xnT_ready"], 4 * tau)
                    dve.tensor_copy(xnT[:, :, 0:1], xnT[:, :, TT:TT + 1]).then_inc(S["shift_ready"], 1)

            def diff(tau, ck):
                dve.wait_ge(S["xnT_ready"], 4 * tau + ck + 1)
                if ck == 0:
                    dve.wait_ge(S["turned"], 4 * tau + 4)
                dve.tensor_tensor(xnd[:, ck, :], xnT[:, ck, 1:TT + 1], xnT[:, ck, 0:TT],
                                  ALU.subtract).then_inc(S["diff_ready"], 1)

            def mix(tau, j, ck):
                n = 4 * j + ck
                if j == KJ:
                    dve.wait_ge(S["diff_ready"], 4 * tau + ck + 1)
                if not (isinstance(tau, int) and 12 * tau + n < 2):
                    dve.wait_ge(S["mix_lo_ready"], 12 * tau + n - 1)
                dve.scalar_tensor_tensor(out=mixf[:, n % 2, :], in0=xnd[:, ck, :], scalar=vecs[:, MK + j, ck:ck + 1],
                                         in1=xnT[:, ck, 0:TT], op0=ALU.mult, op1=ALU.add).then_inc(S["mixed"], 1)

            def gaps(tau, par, c):
                b = c % 2
                u = 4 * tau + c
                if par == 0:
                    dve.memset(run_max[:, b, 0:1], NEG_BIG).then_inc(S["seeded"], 1)
                    dve.memset(state[:, b, :, 0:1], 0.0).then_inc(S["seeded"], 1)
                else:
                    dve.wait_ge(S["carried"], 2 * (u - CK) + 2)
                    dve.tensor_copy(run_max[:, b, 0:1], carry[:, c, 0:1]).then_inc(S["seeded"], 1)
                    dve.tensor_copy(state[:, b, :, 0:1], carry[:, c, 1:3].rearrange("p (a o) -> p a o", o=1)).then_inc(S["seeded"], 1)
                dve.wait_ge(S["seeded"], 2 * u + 2)
                dve.wait_ge(S["k_ready"], u + 1)
                dve.tensor_tensor_scan(run_max[:, b, 1:TT + 1], vecs[:, NEGW, c:c + 1].to_broadcast([P, TT]), k_sb[:, par, c, :],
                                       run_max[:, b, 0:1], ALU.add, ALU.max).then_inc(S["max_scanned"], 1)
                dve.wait_ge(S["max_scanned"], u + 1)
                if not (isinstance(tau, int) and 4 * tau + c < 2):
                    dve.wait_ge(S["rw_lo_ready"], u - 1)
                dve.tensor_tensor(below[:, b, 1, :], k_sb[:, par, c, :], run_max[:, b, 0:TT], ALU.subtract).then_inc(S["gap_ready"], 1)
                dve.tensor_copy(carry[:, c, 0:1], run_max[:, b, TT:TT + 1]).then_inc(S["carried"], 1)
                dve.wait_ge(S["gap_ready"], u + 1)
                for dst, op in ((above, ALU.max), (below, ALU.min)):
                    for e, shift_by in enumerate((TF, DECAY)):
                        dve.tensor_scalar(dst[:, b, e, :], below[:, b, 1, :], vecs[:, shift_by, c:c + 1], 0.0,
                                          ALU.add, op).then_inc(S["clamped"], 1)

            def scans(tau, c):
                b = c % 2
                u = 4 * tau + c
                dve.wait_ge(S["vexped"], u + 1)
                for e, add in ((0, vexp[:, b, 1, :]), (1, below[:, b, 1, :])):
                    dve.tensor_tensor_scan(state[:, b, e, 1:TT + 1], above[:, b, 1, :], add, state[:, b, e, 0:1],
                                           ALU.mult, ALU.add).then_inc(S["scanned"], 1)
                dve.wait_ge(S["scanned"], 2 * u + 2)
                dve.tensor_tensor(above[:, b, 1, :], above[:, b, 0, :], state[:, b, 0, 0:TT], ALU.mult).then_inc(S["scaled"], 1)
                dve.tensor_copy(carry[:, c, 1:3].rearrange("p (a o) -> p a o", o=1), state[:, b, :, TT:TT + 1]).then_inc(S["carried"], 1)
                dve.wait_ge(S["scaled"], 2 * u + 1)
                dve.tensor_tensor(above[:, b, 0, :], above[:, b, 0, :], state[:, b, 1, 0:TT], ALU.mult).then_inc(S["scaled"], 1)
                dve.tensor_tensor(above[:, b, 1, :], above[:, b, 1, :], vexp[:, b, 0, :], ALU.add).then_inc(S["nd_ready"], 1)
                dve.wait_ge(S["scaled"], 2 * u + 2)
                dve.tensor_tensor(above[:, b, 0, :], above[:, b, 0, :], below[:, b, 0, :], ALU.add).then_inc(S["nd_ready"], 1)

            def refine(tau, c):
                b = c % 2
                u = 4 * tau + c
                dve.wait_ge(S["recip_ready"], u + 1)
                dve.tensor_tensor(above[:, b, 0, :], above[:, b, 0, :], vexp[:, b, 0, :], ALU.mult).then_inc(S["resid_ready"], 1)
                dve.wait_ge(S["resid_ready"], u + 1)
                dve.wait_ge(S["a_ready"], u + 1)
                dve.scalar_tensor_tensor(out=above[:, b, 1, :], in0=above[:, b, 0, :], scalar=2.0, in1=vexp[:, b, 1, :],
                                         op0=ALU.subtract, op1=ALU.mult).then_inc(S["rw_ready"], 1)

            def ln2(tau):
                dve.wait_ge(S["y_ready"], ST * (tau + 1))
                moments(2, hb, tau)

            def ln2_normalise(tau):
                normalise(2, hb, hb, tau, "yn_ready")

            def ln3(tau):
                dve.wait_ge(S["x1_ready"], ST * (tau + 1))
                moments(3, xres, tau)

            def ln3_normalise(tau):
                normalise(3, hb, xres, tau, "h_ready")

            ln1_moments(0)
            ln1_normalise(0)
            shift(0, 0)
            for j in range(3):
                for ck in range(CK):
                    if j == KJ:
                        diff(0, ck)
                    mix(0, j, ck)
            ln1_moments(1)
            ln1_normalise(1)
            shift(1, 1)

            def period(tau, par):
                gaps(tau, par, 0)
                if has(tau, 1):
                    for ck in range(CK):
                        diff(tau + 1, ck)
                        mix(tau + 1, KJ, ck)
                scans(tau, 0)
                gaps(tau, par, 1)
                if has(tau, 1):
                    for ck in range(CK):
                        mix(tau + 1, VJ, ck)
                refine(tau, 0)
                scans(tau, 1)
                if back(tau):
                    ln2(tau - 1)
                gaps(tau, par, 2)
                if back(tau):
                    ln2_normalise(tau - 1)
                if has(tau, 1):
                    for ck in range(CK):
                        mix(tau + 1, RJ, ck)
                refine(tau, 1)
                scans(tau, 2)
                if has(tau, 2):
                    ln1_moments(tau + 2)
                gaps(tau, par, 3)
                if has(tau, 2):
                    ln1_normalise(tau + 2)
                    shift(tau + 2, par)
                refine(tau, 2)
                if back(tau):
                    ln3(tau - 1)
                scans(tau, 3)
                if back(tau):
                    ln3_normalise(tau - 1)
                refine(tau, 3)

            periods(dve, period)
            ln2(NT - 1)
            ln2_normalise(NT - 1)
            ln3(NT - 1)
            ln3_normalise(NT - 1)

            raw = [flat(xin), flat(xnd)]
            for q in range(4):
                dve.wait_ge(S["ffn_hi"], q + 1)
                part = slice((q % 2) * 2048, (q % 2 + 1) * 2048)
                hi, lo = (su_hi, su_lo) if q < 2 else (sd_hi, sd_lo)
                dve.tensor_tensor(lo[:, part], raw[q % 2], hi[:, part].bitcast(F32), ALU.subtract).then_inc(S["ffn_split"], 1)
            dve.wait_ge(S["gate_hi"], 1)
            dve.tensor_tensor(gate_w[:, 1, :], flat(k_sb[:, 0, :, :])[:, 0:CK * E], gate_w[:, 0, :].bitcast(F32),
                              ALU.subtract).then_inc(S["gate_split"], 1)
            dve.wait_ge(S["number_made"], 2)
            dve.tensor_copy(number, number_i).then_inc(S["number_ready"], 1)
            dve.tensor_copy(token, token_i).then_inc(S["token_ready"], 1)
            dve.wait_ge(S["ffn_split"], 4)
            dve.wait_ge(S["number_ready"], 1)
            dve.wait_ge(S["token_ready"], 1)
            dve.wait_ge(S["bias_loaded"], 16)

            turn_bank, route_bank = banks[1][:, 2, :], banks[1][:, 3, :]

            def h_rest(k, c):
                dve.wait_ge(S["h_hi_ready"], CK * k + c + 1)
                dve.tensor_tensor(hT_lo[:, c, :], turn_bank, hT_hi[:, c, :].bitcast(F32), ALU.subtract).then_inc(S["h_lo_ready"], 1)

            def split(k, j):
                dve.wait_ge(S["relu_ready"], SJ * k + j + 1)
                dve.tensor_tensor(square[:, j % 2, :], relu[:, j % 2, :], relu[:, j % 2, :], ALU.mult).then_inc(S["square_ready"], 1)
                dve.wait_ge(S["square_ready"], SJ * k + j + 1)
                dve.wait_ge(S["s_hi_ready"], SJ * k + j + 1)
                dve.tensor_tensor(s_lo[:, j % 3, :], square[:, j % 2, :], s_hi[:, j % 3, :].bitcast(F32), ALU.subtract).then_inc(S["s_lo_ready"], 1)

            STEPS = 34
            count = [0]

            def route(k, s):
                base = STEPS * (ST * k + s)

                def step(ins):
                    ins.then_inc(S["route_step"], 1)
                    count[0] += 1

                def settled(own=False):
                    dve.wait_ge(S["route_step"], base + count[0])
                    if own:
                        dve.sem_inc(S["dve_step"], 1)

                return step, settled

            def choose(k, s):
                count[0] = 0
                step, settled = route(k, s)
                by_group = biased.rearrange("p (g e) -> p g e", g=GROUPS)
                sc = score[:, s % 2, :]
                dve.wait_ge(S["score_ready"], ST * k + s + 1)
                step(dve.tensor_tensor(biased, sc, bias_row, ALU.add))
                settled(own=True)
                for g in range(GROUPS):
                    step(dve.max(group_top[:, g, :], by_group[:, g, :]))
                settled()
                step(dve.tensor_tensor(group_score, group_top[:, :, 0], group_top[:, :, 1], ALU.add))
                settled(own=True)
                step(dve.max(group_best, group_score))
                settled(own=True)
                step(dve.max_index(group_index, group_best, group_score))
                settled()
                step(dve.tensor_copy(group_number, group_index))
                settled()
                step(dve.tensor_tensor(group_hot, number[:, 0:GROUPS].rearrange("p (o g) -> p o g", o=1).to_broadcast([P, TOPG, GROUPS]),
                                       group_number[:, 0:TOPG].rearrange("p (g o) -> p g o", o=1).to_broadcast([P, TOPG, GROUPS]), ALU.is_equal))
                settled()
                step(dve.tensor_reduce(group_mask, group_hot.rearrange("p k g -> p g k"), AX.X, ALU.add))
                settled()
                step(dve.tensor_scalar(group_floor, group_mask, 1.0, LOWEST, ALU.subtract, ALU.mult))
                over_experts = [m.rearrange("p (g o) -> p g o", o=1).to_broadcast([P, GROUPS, EG]) for m in (group_mask, group_floor)]
                masked_g = masked.rearrange("p (g e) -> p g e", g=GROUPS)
                step(dve.tensor_tensor(masked_g, by_group, over_experts[0], ALU.mult))
                settled()
                step(dve.tensor_tensor(masked_g, masked_g, over_experts[1], ALU.add))
                settled(own=True)
                step(dve.max(expert_best, masked))
                settled(own=True)
                step(dve.max_index(expert_index, expert_best, masked))
                settled()
                step(dve.tensor_copy(expert_number, expert_index))
                settled()
                step(dve.tensor_tensor(hot, number.rearrange("p (o e) -> p o e", o=1).to_broadcast([P, TOPK, E]),
                                       expert_number[:, 0:TOPK].rearrange("p (k o) -> p k o", o=1).to_broadcast([P, TOPK, E]), ALU.is_equal))
                settled()
                step(dve.tensor_reduce(sel_f, hot.rearrange("p k e -> p e k"), AX.X, ALU.add))
                settled()
                dve.tensor_copy(sel, sel_f).then_inc(S["sel_ready"], 1)
                step(dve.tensor_tensor(product, hot, sc.rearrange("p (o e) -> p o e", o=1).to_broadcast([P, TOPK, E]), ALU.mult))
                settled()
                step(dve.tensor_reduce(weight, product, AX.X, ALU.add))
                settled()
                step(dve.tensor_reduce(weight_sum, weight, AX.X, ALU.add))
                settled()
                step(dve.tensor_scalar(weight_sum, weight_sum, 1e-20, None, ALU.add))
                settled()
                step(dve.reciprocal(weight_sum, weight_sum))
                settled()
                if not (first(k) and s < 2):
                    dve.wait_ge(S[f"scattered{s % 2}"], 16 * TOPK * (2 * k + s // 2))
                step(dve.tensor_scalar(choice[:, s % 2, :, GATE], weight, weight_sum, ROUTE_SCALE, ALU.mult, ALU.mult))
                step(dve.tensor_copy(choice[:, s % 2, :, TOKEN], token.to_broadcast([P, TOPK])))

            def dispatch(k, s):
                step, settled = route(k, s)
                dve.wait_ge(S["pos_ready"], ST * k + s + 1)
                pos = route_bank[:, 0:E].rearrange("p (o e) -> p o e", o=1).to_broadcast([P, TOPK, E])
                settled()
                step(dve.tensor_tensor(product, hot, pos, ALU.mult))
                settled()
                step(dve.tensor_reduce(place, product, AX.X, ALU.add))
                dve.wait_ge(S["sel_ready"], ST * k + s + 1)
                dve.tensor_tensor(seen, seen, sel, ALU.add).then_inc(S["seen_ready"], 1)
                settled()
                step(dve.scalar_tensor_tensor(out=slot_f, in0=place, scalar=float(E), in1=expert_number[:, 0:TOPK], op0=ALU.mult, op1=ALU.add))
                settled()
                dve.tensor_copy(slot[:, s % 2, :], slot_f).then_inc(S["slots_ready"], 1)
                step(dve.tensor_scalar(token, token, float(P), None, ALU.add))
                assert count[0] == STEPS, count[0]

            for c in range(CK):
                h_rest(0, c)

            def tile(k):
                for j in range(SJ):
                    split(k, j)
                    if j == 1 and not first(k):
                        dispatch(k - 1, 3)
                    if j in (3, 5):
                        dispatch(k, j // 2 - 1)
                    if j in (1, 3, 5):
                        choose(k, j // 2)
                if has(k, 1):
                    for c in range(CK):
                        h_rest(k + 1, c)
                dispatch(k, 2)
                choose(k, 3)

            tiles(dve, tile)
            dispatch(NT - 1, 3)

            def index_gather(e, q):
                if not (isinstance(e, int) and e < EB):
                    dve.wait_ge(S["xd_turned"], e - EB + 1)
                    dve.sem_inc(S["dve_step"], 1)
                dve.tensor_copy(gather_token[:, q:q + 1], column(e, TOKEN)).then_inc(S["gather_index"], 1)

            def index_scatter(e, q):
                if not (isinstance(e, int) and e < EB):
                    dve.wait_ge(S["added"], 16 * (e - EB + 1))
                    dve.sem_inc(S["dve_step"], 1)
                dve.tensor_copy(scatter_token[:, q:q + 1], column(e, TOKEN)).then_inc(S["scatter_index"], 1)
                dve.tensor_copy(e_gates[:, q:q + 1], column(e, GATE)).then_inc(S["scatter_index"], 1)

            def column(e, which):
                return table[:, bass.ds(e, 1), which]

            def e_square(e, q):
                dve.wait_ge(S["e_relu"], e + 1)
                if not (isinstance(e, int) and e < 2):
                    dve.wait_ge(S["e_down"], e - 1)
                dve.tensor_tensor(e_act[q % 2].rearrange("p k n -> p (k n)"), e_hidden[q % 2], e_hidden[q % 2], ALU.mult).then_inc(S["e_square"], 1)

            dve.wait_ge(S["table_loaded"], 16)
            for e in range(EB):
                index_gather(e, e)
            index_scatter(0, 0)
            e_square(0, 0)

            def expert(e, q, m):
                if within(e, 1):
                    e_square(e + 1, (q + 1) % EB)
                    index_scatter(e + 1, (q + 1) % EB)
                if within(e, EB):
                    index_gather(e + EB, q)

            experts(dve, expert)

            def final(k, q, m):
                dve.wait_ge(S[f"ysh_loaded{q}"], 16 * (m + 1))
                moments(4, o_y[q], k)
                normalise(4, o_y[q], o_y[q], k, "o_normed")

            finals(dve, final)


def kernel(**inputs):
    import numpy as _np
    import concourse.bacc as _bacc
    from concourse import mybir as _mybir
    from concourse.bass_utils import run_bass_kernel_spmd as _run

    def by_partition(w, chunks):
        return _np.ascontiguousarray(w.reshape(chunks, P, -1).transpose(1, 0, 2))

    g = {n: _np.asarray(a) for n, a in inputs.items()}
    vecs = [g["L0_attn_time_decay"], g["L0_attn_time_first"], g["L0_attn_time_mix_k"], g["L0_attn_time_mix_v"], g["L0_attn_time_mix_r"]]
    arrays = {
        "x": _np.ascontiguousarray(g["L0_attn_x"].reshape(N, C)),
        "vecs": _np.ascontiguousarray(_np.stack([v.reshape(CK, P).T for v in vecs], axis=1)),
        "Wk": by_partition(g["L0_attn_Wk"].T, CK),
        "Wv": by_partition(g["L0_attn_Wv"].T, CK),
        "Wr": by_partition(g["L0_attn_Wr"].T, CK),
        "Wo": by_partition(g["L0_attn_Wo"].T, CK),
        "gate": by_partition(g["L0_ffn_gate_w"].T, CK).reshape(P, CK * E),
        "e_bias": g["L0_ffn_e_bias"].reshape(1, E),
        "su": by_partition(g["L0_ffn_shared_up_w"].T, CK).reshape(P, 2, -1),
        "sd": by_partition(g["L0_ffn_shared_down_w"].T, SJ).reshape(P, 2, -1),
        "w1": _np.ascontiguousarray(g["L0_ffn_w1"].transpose(0, 2, 1).reshape(E, CK, P, HID).transpose(0, 2, 1, 3)).reshape(E, P, CK * HID),
        "w2": _np.ascontiguousarray(g["L0_ffn_w2"].transpose(0, 2, 1).reshape(E, IK, P, C).transpose(0, 2, 1, 3)).reshape(E, P, IK * C),
    }
    nc = _bacc.Bacc("TRN2", target_bir_lowering=False, num_devices=1)
    aps = {n: nc.dram_tensor(f"in_{n}", a.shape, _mybir.dt.from_np(a.dtype), kind="ExternalInput").ap() for n, a in arrays.items()}
    scratch = {"x1": (N, C), "h": (N + P, C), "ysh": (N + P, C), "slots": (E * CAP, 2)}
    aps.update({n: nc.dram_tensor(n, shape, F32, kind="Internal").ap() for n, shape in scratch.items()})
    aps["out"] = nc.dram_tensor("out", (N, C), F32, kind="ExternalOutput").ap()
    sandwich(nc, aps)
    r = _run(nc, [{f"in_{n}": a for n, a in arrays.items()}], core_ids=[0])
    return r.results[0]["out"].reshape(B, T, C)
```

```python
import concourse.bass as bass
from concourse import mybir
from contextlib import ExitStack

F32 = mybir.dt.float32
F32R = mybir.dt.float32r
BF16 = mybir.dt.bfloat16
I32 = mybir.dt.int32
U32 = mybir.dt.uint32
ALU = mybir.AluOpType
ACT = mybir.ActivationFunctionType
AX = mybir.AxisListType

P = 128
C = 512
CK = C // P
B, T = 4, 1024
N = B * T
TT = 512
ST = TT // P
NT = N // TT
EPS = 1e-5
NEG_BIG = -1e38
E, GROUPS, TOPG, TOPK = 64, 8, 4, 6
EG = E // GROUPS
CAP = 128
HID = 256
SH = 1024
SJ = SH // P
IK = HID // P
ROUTE_SCALE = 2.5
GATE, TOKEN = range(2)
EB, WB = 4, 8
LOWEST = 3e38
EARLY = NT // 2
KJ, VJ, RJ = range(3)


def sandwich(nc, t):
    ctx = ExitStack()
    with ctx:
        def sb(name, shape, dt=F32):
            return ctx.enter_context(nc.sbuf_tensor(name, shape, dt))

        def sem(name):
            return ctx.enter_context(nc.semaphore(name))

        weights = sb("weights", [P, 8, CK * C], F32R)
        mix_hi = sb("mix_hi", [P, 3, TT], F32R)
        mix_lo = sb("mix_lo", [P, 3, TT], F32R)
        rw_hi = sb("rw_hi", [P, CK, TT], F32R)
        rw_lo = sb("rw_lo", [P, CK, TT], F32R)
        xin = sb("xin", [P, ST, C])
        xres = sb("xres", [P, ST, C])
        xnd = sb("xnd", [P, CK, TT])
        xnT = sb("xnT", [P, CK, TT + 1])
        mixf = sb("mixf", [P, 2, TT])
        k_sb = sb("k_sb", [P, 2, CK, TT])
        v_sb = sb("v_sb", [P, CK, TT])
        sr = sb("sr", [P, CK, TT])
        hb = sb("hb", [P, ST, C])
        run_max = sb("run_max", [P, 2, TT + 1])
        state = sb("state", [P, 2, 2, TT + 1])
        wkv = sb("wkv", [P, 12 * TT])

        def unit_pairs(at):
            return at.rearrange("p b (e t) -> p b e t", e=2)

        exponents = wkv[:, 0:8 * TT].rearrange("p (b w) -> p b w", b=2)
        above = unit_pairs(exponents[:, :, 0:2 * TT])
        below = unit_pairs(exponents[:, :, 2 * TT:4 * TT])
        vexp = unit_pairs(wkv[:, 8 * TT:12 * TT].rearrange("p (b w) -> p b w", b=2))
        gate_w = sb("gate_w", [P, CK, E])
        carry = sb("carry", [P, CK, 3])
        vecs = sb("vecs", [P, 8, CK])
        stats = sb("stats", [P, ST, 6])
        mv = sb("mv", [P, 4, ST, 2])
        rstd = sb("rstd", [P, 4, ST])
        y_sum = sb("y_sum", [P, 2, ST])
        neg_mean = sb("neg_mean", [P, ST])
        offset = sb("offset", [P, 4, ST])
        neg_half = sb("neg_half", [P, ST])
        ident = sb("ident", [P, P])
        TD, TF, MK, MV, MR, DECAY, NEGW, _ = range(8)

        banks = [ctx.enter_context(nc.psum_tensor(f"bank{g}", [P, 4, 512], F32)) for g in range(2)]
        y_bank, (up_bank, turn_bank, route_bank) = banks[1], (banks[0][:, 0:2, :], banks[0][:, 2, :], banks[0][:, 3, :])

        names = """w_loaded0 w_loaded1 vec_loaded x_loaded xres_loaded x1_stored h_stored
        w_hi w_split decay_ready ident_ready half_ready
        ln1_stats ln1_moments ln1_rstd xn_ready turned xnT_ready shift_ready diff_ready mixed mix_hi_ready mix_lo_ready mix_used
        k_ready v_ready r_ready out_used y_ready
        seeded max_scanned gap_ready lifted clamped carried exped vexped scanned scaled nd_ready recip_ln recip_ready ns_ready a_ready
        resid_ready rw_ready rw_hi_ready rw_lo_ready
        y_mean y_squared ln2_rstd yn_ready x1_ready ln3_stats ln3_moments ln3_rstd h_ready
        dve_step pool_step
        blank_ready slots_blank h_blank ysh_blank
        raw_loaded0 raw_loaded1 raw_loaded2 raw_loaded3 ffn_hi ffn_split gate_loaded bias_loaded
        number_made number_ready causal_ready ones_ready seen_ready token_ready
        h_loaded h_chunk_turned h_copied h_hi_ready h_lo_ready up_done relu_ready square_ready s_hi_ready s_lo_ready down_done
        yout_ready ysh_stored logits_done score_ready sel_ready pos_ready placed route_step
        slots_ready scattered
        table_loaded gather_index scatter_index xd_turned xdT_ready e_up e_relu e_square e_down e_gated added
        out_stored ln4_stats ln4_moments ln4_rstd o_normed o_ready o_added""".split()
        names += [f"{n}{q}" for n, b in (("w1_loaded", WB), ("w2_loaded", WB), ("xd_loaded", EB)) for q in range(b)]
        names += [f"{n}{k}" for n in ("ysh_loaded", "x1_loaded") for k in range(NT)]
        S = {n: sem(n) for n in names}

        def W(j, part):
            return weights[:, 2 * j + part, :].rearrange("p (k d) -> p k d", k=CK)

        def flat(tile):
            return tile[:, :, :].rearrange("p a b -> p (a b)")

        stage = [hb, sr]
        raw = [flat(xnd), flat(k_sb[:, 0, :, :]), flat(k_sb[:, 0, :, :]), flat(v_sb)]
        blank_slots = hb[:, 0, 0:2 * E].rearrange("p (e w) -> p e w", w=2)

        su_hi, su_lo, sd_hi, sd_lo = (weights[:, 2 * n:2 * n + 2, :].rearrange("p a b -> p (a b)") for n in range(4))
        su = [w.rearrange("p (k d) -> p k d", k=CK) for w in (su_hi, su_lo)]
        sd = [w.rearrange("p (j c) -> p j c", j=SJ) for w in (sd_hi, sd_lo)]
        hT_hi, hT_lo, s_hi, s_lo = rw_hi, rw_lo, mix_hi, mix_lo
        hT = flat(xnT)[:, 0:CK * TT].rearrange("p (k t) -> p k t", k=CK)
        relu = k_sb[:, 0, 0:2, :]
        square = k_sb[:, 1, 0:2, :]
        yout = v_sb
        consts = flat(mixf)
        bias_row = consts[:, 0:E]
        number = consts[:, E:2 * E]
        causal = consts[:, 128:192].bitcast(BF16)
        ones = consts[:, 192:256].bitcast(BF16)
        sel = consts[:, 256:384].bitcast(BF16).rearrange("p (s e) -> p s e", s=ST)
        seen = consts[:, 384:416].bitcast(BF16)
        token = consts[:, 416:416 + ST]
        number_i = consts[:, 420:484].bitcast(I32)
        token_i = consts[:, 484:484 + ST].bitcast(I32)
        gather_token = consts[:, 488:488 + EB].bitcast(U32)
        scatter_token = consts[:, 492:492 + EB].bitcast(U32)
        e_gates = consts[:, 496:496 + EB]
        scratch = flat(xnd)
        at = [0]

        def carve(*shape, dt=F32):
            n = 1
            for k in shape:
                n *= k
            v = scratch[:, at[0]:at[0] + n]
            at[0] += n
            if dt is not F32:
                v = v.bitcast(dt)
            return {1: lambda: v, 2: lambda: v.rearrange("p (a b) -> p a b", a=shape[0]),
                    3: lambda: v.rearrange("p (a b c) -> p a b c", a=shape[0], b=shape[1])}[len(shape)]()

        score = carve(ST, E)
        biased = carve(ST, E)
        group_top = carve(ST * GROUPS, 8)
        group_score = carve(ST, GROUPS)
        group_best = carve(ST, 8)
        group_index = carve(ST, 8, dt=U32)
        group_number = carve(ST, 8)
        group_hot = carve(ST, TOPG, GROUPS)
        group_mask = carve(ST, GROUPS)
        group_floor = carve(ST, GROUPS)
        expert_best = carve(ST, 8)
        expert_index = carve(ST, 8, dt=U32)
        expert_number = carve(ST, 8)
        sel_sum = carve(E)
        weight = carve(ST, TOPK)
        weight_sum = carve(ST)
        place = carve(ST, TOPK)
        slot_f = carve(ST, TOPK)
        slot = carve(ST, TOPK, dt=U32)
        choice = carve(ST, TOPK, 2)
        table = carve(E, 2)
        flat_run_max = run_max[:, :, :].rearrange("p a b -> p (a b)")
        state_flat = state[:, :, :, :].rearrange("p a b c -> p (a b c)")
        hot = state_flat[:, 0:ST * TOPK * E].rearrange("p (s k e) -> p s k e", s=ST, k=TOPK)
        product = wkv[:, 8 * TT:8 * TT + ST * TOPK * E].rearrange("p (s k e) -> p s k e", s=ST, k=TOPK)

        halves = [flat(m)[:, b * CK * HID:(b + 1) * CK * HID] for m in (hb, sr) for b in range(2)] + \
                 [wkv[:, b * CK * HID:(b + 1) * CK * HID] for b in range(4)] + \
                 [k_sb[:, b, CK // 2:CK, :].rearrange("p a b -> p (a b)") for b in range(2)] + \
                 [flat(xin)[:, b * CK * HID:(b + 1) * CK * HID] for b in range(2)] + \
                 [wkv[:, b * CK * HID:(b + 1) * CK * HID] for b in range(4, 6)] + \
                 [flat_run_max[:, 0:CK * HID], state_flat[:, CK * HID:2 * CK * HID]]
        w1_sb = [w.rearrange("p (k i) -> p k i", k=CK) for w in halves[0::2]]
        w2_sb = [w.rearrange("p (k c) -> p k c", k=IK) for w in halves[1::2]]
        xd_sb = [xres[:, q, :] for q in range(EB)]
        xdT = [flat(xnT)[:, q * C:(q + 1) * C].rearrange("p (k n) -> p k n", k=CK) for q in range(EB)]
        e_hidden = [state_flat[:, b * HID:(b + 1) * HID] for b in range(2)]
        e_act = [state_flat[:, (2 + b) * HID:(3 + b) * HID].rearrange("p (k n) -> p k n", k=IK) for b in range(2)]
        e_out = [k_sb[:, q // 2, q % 2, :] for q in range(EB)]
        o_y = [m[:, :, :] for m in (xin, v_sb, k_sb[:, 0], k_sb[:, 1], xnd, hb, sr)] + [hT]
        o_x = [weights[:, k, :].bitcast(F32).rearrange("p (s c) -> p s c", s=ST) for k in range(NT)]
        x_by_tile = t["x"].rearrange("(t s p) c -> t p s c", s=ST, p=P)
        x1_by_tile = t["x1"].rearrange("(t s p) c -> t p s c", s=ST, p=P)
        h_by_tile = t["h"][0:N, :].rearrange("(t s p) c -> t p s c", s=ST, p=P)

        ysh_by_tile = t["ysh"][0:N, :].rearrange("(t s p) c -> t p s c", s=ST, p=P)
        out_by_tile = t["out"].rearrange("(t s p) c -> t p s c", s=ST, p=P)
        slots_by_place = t["slots"].rearrange("(c e) w -> c e w", e=E)

        def o_slot(k):
            return 3 if k % 2 == 0 else 0

        def y_of(tau):
            return sr if last(tau) else hb

        def tile_of(ap, tau):
            return ap[bass.ds(tau, 1)].rearrange("o p s c -> p (o s) c")

        def periods(eng, period):
            for tau in range(2):
                period(tau, tau)
            with eng.Fori(0, (NT - 4) // 2) as i:
                for par in range(2):
                    period(2 * i + 2 + par, par)
            for tau in range(NT - 2, NT + 1):
                period(tau, tau % 2)

        def tiles(eng, tile):
            for k in range(2):
                tile(k)
            with eng.Fori(0, NT - 4) as i:
                tile(i + 2)
            for k in range(NT - 2, NT):
                tile(k)

        def experts(eng, expert):
            for e in range(WB):
                expert(e, e, 0)
            with eng.Fori(0, E // WB - 3) as i:
                for r in range(WB):
                    expert(WB * i + WB + r, r, i + 1)
            for e in range(E - 2 * WB, E):
                expert(e, e % WB, e // WB)

        def last(tau):
            return isinstance(tau, int) and tau == NT - 1

        def behind_all(tau):
            return isinstance(tau, int) and tau == NT

        def within(e, ahead):
            return not (isinstance(e, int) and e + ahead >= E)

        def second(k):
            return isinstance(k, int) and k == 1

        def last_but_one(k):
            return isinstance(k, int) and k == NT - 2

        def first(n):
            return isinstance(n, int) and n == 0

        def has(tau, ahead):
            return not isinstance(tau, int) or 0 <= tau + ahead < NT

        def load_x1(eng, k, half):
            part = slice(half * ST // 2, (half + 1) * ST // 2)
            eng.dma_start(o_x[k][:, part, :], x1_by_tile[k][:, part, :]).then_inc(S[f"x1_loaded{k}"], 16)

        block = ctx.enter_context(nc.Block())

        @block.sync
        def _(sp):
            sp.dma_start(xin[:, :, :], x_by_tile[0]).then_inc(S["x_loaded"], 16)
            for j, name in enumerate(("Wk", "Wv", "Wr", "Wo")):
                if j >= 2:
                    sp.wait_ge(S["w_split"], j - 1)
                sp.dma_start(stage[j % 2][:, :, :], t[name]).then_inc(S[f"w_loaded{j % 2}"], 16)
                if j == 0:
                    sp.dma_start(flat(gate_w), t["gate"]).then_inc(S["gate_loaded"], 16)
                    sp.dma_start(vecs[:, 0:5, :], t["vecs"]).then_inc(S["vec_loaded"], 16)
            sp.wait_ge(S["turned"], CK)
            sp.dma_start(xin[:, :, :], x_by_tile[1]).then_inc(S["x_loaded"], 16)

            def period(tau, par):
                if has(tau, 2):
                    sp.wait_ge(S["turned"], CK * (tau + 2))
                    sp.dma_start(xin[:, :, :], tile_of(x_by_tile, tau + 2)).then_inc(S["x_loaded"], 16)
                if last(tau):
                    sp.wait_ge(S["mixed"], 12 * NT)
                    load_raw(0)
                    sp.wait_ge(S["mix_lo_ready"], 12 * NT)
                    sp.dma_start(bias_row, t["e_bias"].to_broadcast([P, E])).then_inc(S["bias_loaded"], 16)
                    sp.wait_ge(S["gap_ready"], CK * (NT - 1))
                    load_raw(1)
                    sp.wait_ge(S["turned"], CK * NT)
                    sp.dma_start(xin[:, :, :], h_by_tile[0]).then_inc(S["h_loaded"], 16)
                if has(tau, -2):
                    store_tail(tau - 2)
                if has(tau, -1):
                    if has(tau, -2):
                        sp.wait_ge(S["x1_stored"], 16 * (tau - 1))
                    sp.dma_start(xres[:, :, :], tile_of(x_by_tile, tau - 1)).then_inc(S["xres_loaded"], 16)
                if last(tau):
                    sp.wait_ge(S["ffn_split"], 2)
                    load_raw(2)
                    sp.wait_ge(S["h_chunk_turned"], CK)
                    sp.dma_start(xin[:, :, :], h_by_tile[1]).then_inc(S["h_loaded"], 16)
                    sp.wait_ge(S["vexped"], CK * NT)
                    load_raw(3)

            def load_raw(q):
                src = t["su"] if q < 2 else t["sd"]
                sp.dma_start(raw[q], src[:, q % 2, :]).then_inc(S[f"raw_loaded{q}"], 16)

            def load_expert(name, dst, e, q):
                src = t[name][e] if isinstance(e, int) else t[name][bass.ds(e, 1)].rearrange("o p k -> p (o k)")
                sp.dma_start(dst[q].rearrange("p k i -> p (k i)"), src).then_inc(S[f"{name}_loaded{q}"], 16)

            def store_tail(tau):
                sp.wait_ge(S["h_ready"], ST * (tau + 1))
                sp.dma_start(tile_of(h_by_tile, tau), y_of(tau)[:, :, :]).then_inc(S["h_stored"], 16)
                sp.dma_start(tile_of(x1_by_tile, tau), xres[:, :, :]).then_inc(S["x1_stored"], 16)

            sp.wait_ge(S["blank_ready"], 2)
            sp.dma_start(slots_by_place, blank_slots).then_inc(S["slots_blank"], 16)
            sp.dma_start(t["h"][N:N + P, :], hb[:, 1, :]).then_inc(S["h_blank"], 16)
            sp.dma_start(t["ysh"][N:N + P, :], hb[:, 1, :]).then_inc(S["ysh_blank"], 16)

            periods(sp, period)

            def tile(k):
                if has(k, 2):
                    sp.wait_ge(S["h_chunk_turned"], CK * (k + 2))
                    sp.dma_start(xin[:, :, :], tile_of(h_by_tile, k + 2)).then_inc(S["h_loaded"], 16)
                if last(k):
                    sp.wait_ge(S["h_chunk_turned"], CK * NT)
                    sp.wait_ge(S["slots_ready"], NT)
                    for r in range(EB, WB):
                        load_expert("w1", w1_sb, r, r)
                        load_expert("w2", w2_sb, r, r)
                    sp.wait_ge(S["scattered"], 16 * TOPK * ST * NT)
                    sp.dma_start(table, slots_by_place).then_inc(S["table_loaded"], 16)
                sp.wait_ge(S["yout_ready"], ST * (k + 1))
                sp.dma_start(tile_of(ysh_by_tile, k), yout[:, :, :]).then_inc(S["ysh_stored"], 16)
                if second(k):
                    store_tail(NT - 1)
                    sp.wait_ge(S["x1_stored"], 16 * NT)
                    sp.wait_ge(S["h_stored"], 16 * NT)
                    sp.wait_ge(S["rw_lo_ready"], CK * NT)
                    sp.wait_ge(S["h_blank"], 16)
                    sp.wait_ge(S["ysh_blank"], 16)
                    for q in range(EB):
                        load_expert("w1", w1_sb, q, q)
                        load_expert("w2", w2_sb, q, q)

            tiles(sp, tile)

            sp.wait_ge(S["down_done"], SJ * NT)
            sp.wait_ge(S["ysh_stored"], 16 * NT)

            sp.wait_ge(S["e_up"], 1)
            load_expert("w1", w1_sb, WB, 0)

            def expert(e, r, n):
                if within(e, WB + 1):
                    sp.wait_ge(S["e_up"], e + 2)
                    load_expert("w1", w1_sb, e + WB + 1, (r + 1) % WB)
                if within(e, WB):
                    sp.wait_ge(S["e_down"], e + 1)
                    load_expert("w2", w2_sb, e + WB, r)

            experts(sp, expert)

            for n in range(2 * EARLY):
                sp.wait_ge(S["added"], 16 * (E - 2 * EARLY + n))
                load_x1(sp, n // 2, n % 2)
            sp.wait_ge(S["added"], 16 * E)
            for k in range(NT):
                sp.dma_start(o_y[k], ysh_by_tile[k]).then_inc(S[f"ysh_loaded{k}"], 16)
            for k in range(NT):
                sp.wait_ge(S["o_ready"], ST // 2 * (k + 1))
                sp.wait_ge(S["o_added"], ST // 2 * (k + 1))
                sp.dma_start(out_by_tile[k], o_y[k]).then_inc(S["out_stored"], 16)
            sp.wait_ge(S["out_stored"], 16 * NT)

        @block.tensor
        def _(pe):
            even, odd = banks

            def h_transpose(bank, c):
                for s in range(ST):
                    mm = pe.transpose(bank[:, s * P:(s + 1) * P], xin[:, s, c * P:(c + 1) * P], ident[:, :])
                mm.then_inc(S["h_chunk_turned"], 1)

            def logits(bank, k):
                pe.wait_ge(S["h_copied"], CK * (k + 1))
                for s in range(ST):
                    for ck in range(CK):
                        mm = pe.matmul(bank[:, s * E:(s + 1) * E], hT[:, ck, s * P:(s + 1) * P], gate_w[:, ck, :],
                                       start=(ck == 0), stop=(ck == CK - 1))
                mm.then_inc(S["logits_done"], 1)

            def places(bank, k):
                pe.wait_ge(S["sel_ready"], k + 1)
                pe.wait_ge(S["seen_ready"], k + 1)
                if first(k):
                    pe.wait_ge(S["causal_ready"], 2)
                    pe.wait_ge(S["ones_ready"], 1)
                for s in range(ST):
                    out = bank[:, s * E:(s + 1) * E]
                    pe.matmul(out, causal, sel[:, s, :], start=True, stop=False)
                    for before in range(s):
                        pe.matmul(out, ones, sel[:, before, :], start=False, stop=False)
                    mm = pe.matmul(out, ones, seen, start=False, stop=True)
                mm.then_inc(S["pos_ready"], 1)

            def transposes(bank, tau, *chunks):
                pe.wait_ge(S["xn_ready"], ST * (tau + 1))
                for c in chunks:
                    if not first(tau):
                        pe.wait_ge(S["v_ready"], 4 * (tau - 1) + c + 1)
                    for s in range(ST):
                        mm = pe.transpose(bank[:, c, s * P:(s + 1) * P], xin[:, s, c * P:(c + 1) * P], ident[:, :])
                    mm.then_inc(S["turned"], 1)

            def project(bank, tau, j, ck):
                pe.wait_ge(S["mix_lo_ready"], 12 * tau + 4 * j + ck + 1)
                slot = (4 * j + ck) % 3
                for d in range(CK):
                    hi = W(j, 0)[:, ck, d * P:(d + 1) * P]
                    lo = W(j, 1)[:, ck, d * P:(d + 1) * P]
                    pe.matmul(bank[:, d, :], hi, mix_hi[:, slot, :], start=(ck == 0), stop=False)
                    pe.matmul(bank[:, d, :], hi, mix_lo[:, slot, :], start=False, stop=False)
                    mm = pe.matmul(bank[:, d, :], lo, mix_hi[:, slot, :], start=False, stop=(ck == CK - 1))
                mm.then_inc(S["mix_used"], 1)

            def output(bank, tau, ck):
                pe.wait_ge(S["rw_lo_ready"], 4 * tau + ck + 1)
                for s in range(ST):
                    hi = rw_hi[:, ck, s * P:(s + 1) * P]
                    lo = rw_lo[:, ck, s * P:(s + 1) * P]
                    pe.matmul(bank[:, s, :], hi, W(3, 0)[:, ck, :], start=(ck == 0), stop=False)
                    pe.matmul(bank[:, s, :], hi, W(3, 1)[:, ck, :], start=False, stop=False)
                    mm = pe.matmul(bank[:, s, :], lo, W(3, 0)[:, ck, :], start=False, stop=(ck == CK - 1))
                mm.then_inc(S["out_used"], 1)

            pe.wait_ge(S["ident_ready"], 2)
            transposes(even, 0, *range(CK))
            for j, bank in ((KJ, odd), (VJ, even)):
                pe.wait_ge(S["w_split"], j + 1)
                if j == VJ:
                    pe.wait_ge(S["xnT_ready"], 4)
                for ck in range(CK):
                    project(bank, 0, j, ck)
            pe.wait_ge(S["w_split"], 3)
            pe.wait_ge(S["k_ready"], 4)
            for ck in range(2):
                project(odd, 0, RJ, ck)
            transposes(even, 1, *range(CK))
            for ck in range(2, CK):
                project(odd, 0, RJ, ck)
            pe.wait_ge(S["xnT_ready"], 8)
            for ck in range(CK - 1):
                project(even, 1, KJ, ck)
            pe.wait_ge(S["w_split"], 4)

            def period(tau, par):
                ahead, behind = has(tau, 1), has(tau, -1)
                if behind:
                    if has(tau, 0):
                        pe.wait_ge(S["r_ready"], 4 * (tau + 1))
                    else:
                        pe.wait_ge(S["y_squared"], 4 * (tau - 1))
                    for ck in range(2):
                        output(odd, tau - 1, ck)
                if ahead:
                    project(even, tau + 1, KJ, CK - 1)
                if behind:
                    for ck in range(2, CK):
                        output(odd, tau - 1, ck)
                if ahead:
                    pe.wait_ge(S["k_ready"], 4 * (tau + 2))
                    for ck in range(CK):
                        project(even, tau + 1, VJ, ck)
                    if behind:
                        pe.wait_ge(S["y_squared"], 4 * tau)
                    else:
                        pe.wait_ge(S["r_ready"], 4)
                    for ck in range(CK - 1):
                        project(odd, tau + 1, RJ, ck)
                    if has(tau, 2):
                        transposes(even, tau + 2, *range(CK - 1))
                    project(odd, tau + 1, RJ, CK - 1)
                if has(tau, 2):
                    transposes(even, tau + 2, CK - 1)
                    pe.wait_ge(S["xnT_ready"], 4 * (tau + 3))
                    for ck in range(CK - 1):
                        project(even, tau + 2, KJ, ck)
                if last(tau):
                    pe.wait_ge(S["h_loaded"], 16)
                    pe.wait_ge(S["v_ready"], CK * NT)
                    for c in range(CK):
                        h_transpose(even[:, c, :], c)
                    pe.wait_ge(S["gate_loaded"], 16)
                    logits(turn_bank, 0)

            periods(pe, period)

            def up(k, j):
                if not (first(k) and j < 2):
                    pe.wait_ge(S["relu_ready"], SJ * k + j - 1)
                for ck in range(CK):
                    if j == 0:
                        pe.wait_ge(S["h_lo_ready"], CK * k + ck + 1)
                    hi, lo = (x[:, ck, j * P:(j + 1) * P] for x in su)
                    pe.matmul(up_bank[:, j % 2, :], hi, hT_hi[:, ck, :], start=(ck == 0), stop=False)
                    pe.matmul(up_bank[:, j % 2, :], hi, hT_lo[:, ck, :], start=False, stop=False)
                    mm = pe.matmul(up_bank[:, j % 2, :], lo, hT_hi[:, ck, :], start=False, stop=(ck == CK - 1))
                mm.then_inc(S["up_done"], 1)

            def down(k, j):
                pe.wait_ge(S["s_lo_ready"], SJ * k + j + 1)
                if j == 0:
                    if first(k):
                        pe.wait_ge(S["ffn_split"], 3)
                        pe.wait_ge(S["y_squared"], ST * NT)
                    else:
                        pe.wait_ge(S["yout_ready"], ST * k)
                if first(k) and j == SJ // 2:
                    pe.wait_ge(S["ffn_split"], 4)
                for s in range(ST):
                    hi, lo = (x[:, j % 3, s * P:(s + 1) * P] for x in (s_hi, s_lo))
                    pe.matmul(y_bank[:, s, :], hi, sd[0][:, j, :], start=(j == 0), stop=False)
                    pe.matmul(y_bank[:, s, :], hi, sd[1][:, j, :], start=False, stop=False)
                    mm = pe.matmul(y_bank[:, s, :], lo, sd[0][:, j, :], start=False, stop=(j == SJ - 1))
                mm.then_inc(S["down_done"], 1)

            pe.wait_ge(S["ffn_split"], 2)

            def xd_transpose(e, r, n):
                q, b = r % EB, r % 2
                pe.wait_ge(S[f"xd_loaded{q}"], 16 * (n * (WB // EB) + r // EB + 1))
                if not (isinstance(e, int) and e < 2):
                    pe.wait_ge(S["xdT_ready"], e - 1)
                for c in range(CK):
                    mm = pe.transpose(banks[0][:, 2 + b, c * P:(c + 1) * P], xd_sb[q][:, c * P:(c + 1) * P], ident[:, :])
                mm.then_inc(S["xd_turned"], 1)

            def e_first(e, r, n):
                q, b = r % EB, r % 2
                pe.wait_ge(S[f"w1_loaded{r}"], 16 * (n + 1))
                pe.wait_ge(S["xdT_ready"], e + 1)
                if not (isinstance(e, int) and e < 2):
                    pe.wait_ge(S["e_relu"], e - 1)
                for i in range(IK):
                    for ck in range(CK):
                        mm = pe.matmul(banks[0][:, b, i * CAP:(i + 1) * CAP], w1_sb[r][:, ck, i * P:(i + 1) * P], xdT[q][:, ck, :],
                                       start=(ck == 0), stop=(ck == CK - 1))
                mm.then_inc(S["e_up"], 1)

            def e_second(e, r, n):
                b = r % 2
                pe.wait_ge(S[f"w2_loaded{r}"], 16 * (n + 1))
                pe.wait_ge(S["e_square"], e + 1)
                if not (isinstance(e, int) and e < 2):
                    pe.wait_ge(S["e_gated"], e - 1)
                for i in range(IK):
                    mm = pe.matmul(banks[1][:, b, :], e_act[b][:, i, :], w2_sb[r][:, i, :], start=(i == 0), stop=(i == IK - 1))
                mm.then_inc(S["e_down"], 1)

            def tile(k):
                for j in range(SJ):
                    if j == 3 and has(k, 1):
                        pe.wait_ge(S["placed"], k + 1)
                        h_transpose(turn_bank, 1)
                        pe.wait_ge(S["h_copied"], CK * (k + 1) + 1)
                        h_transpose(route_bank, 2)
                    up(k, j)
                    if j == 1 and has(k, 1):
                        places(turn_bank, k)
                    if has(k, 1):
                        if j == 2:
                            pe.wait_ge(S["h_loaded"], 16 * (k + 2))
                            h_transpose(route_bank, 0)
                        if j == 3:
                            pe.wait_ge(S["h_copied"], CK * (k + 1) + 2)
                            h_transpose(turn_bank, 3)
                        if j == 4:
                            logits(turn_bank, k + 1)
                    if j >= 2:
                        down(k, j - 2)
                if last_but_one(k):
                    places(turn_bank, k + 1)
                down(k, SJ - 2)
                if last(k):
                    pe.wait_ge(S["placed"], NT)
                    for e in range(2):
                        xd_transpose(e, e, 0)
                down(k, SJ - 1)

            tiles(pe, tile)
            pe.wait_ge(S["relu_ready"], SJ * NT)
            e_first(0, 0, 0)
            pe.wait_ge(S["yout_ready"], ST * NT)

            def expert(e, r, n):
                if within(e, 2):
                    xd_transpose(e + 2, (r + 2) % WB, n + (r + 2) // WB)
                if within(e, 1):
                    e_first(e + 1, (r + 1) % WB, n + (r + 1) // WB)
                e_second(e, r, n)

            experts(pe, expert)

        @block.scalar
        def _(act):
            even, odd = banks

            def round_weight(j):
                act.wait_ge(S[f"w_loaded{j % 2}"], 16 * (j // 2 + 1))
                act.activation(W(j, 0), stage[j % 2][:, :, :], ACT.Copy, scale=-1.0 if j == 3 else 1.0).then_inc(S["w_hi"], 1)

            def xnT_read(bank, tau, *chunks):
                act.wait_ge(S["shift_ready"], tau + 1)
                for c in chunks:
                    act.wait_ge(S["turned"], 4 * tau + c + 1)
                    act.activation(xnT[:, c, 1:TT + 1], bank[:, c, :], ACT.Copy).then_inc(S["xnT_ready"], 1)

            def round_mix(tau, j, ck):
                n = 4 * j + ck
                act.wait_ge(S["mixed"], 12 * tau + n + 1)
                if not (isinstance(tau, int) and 12 * tau + n < 3):
                    act.wait_ge(S["mix_used"], 12 * tau + n - 2)
                act.activation(mix_hi[:, n % 3, :], mixf[:, n % 2, :], ACT.Copy).then_inc(S["mix_hi_ready"], 1)

            def k_read(bank, tau, par):
                for c in range(CK):
                    act.wait_ge(S["mix_used"], 12 * tau + 4 * KJ + 4)
                    if not (isinstance(tau, int) and tau < 2):
                        act.wait_ge(S["gap_ready"], 4 * (tau - 2) + c + 1)
                    act.activation(k_sb[:, par, c, :], bank[:, c, :], ACT.Copy).then_inc(S["k_ready"], 1)

            def v_read(bank, tau, c):
                act.wait_ge(S["mix_used"], 12 * tau + 4 * VJ + 4)
                if not (isinstance(tau, int) and tau < 1):
                    act.wait_ge(S["vexped"], 4 * (tau - 1) + c + 1)
                act.activation(v_sb[:, c, :], bank[:, c, :], ACT.Copy).then_inc(S["v_ready"], 1)

            def r_read(bank, tau, c):
                act.wait_ge(S["mix_used"], 12 * tau + 4 * RJ + 4)
                if not (isinstance(tau, int) and tau < 1):
                    act.wait_ge(S["ns_ready"], 4 * (tau - 1) + c + 1)
                else:
                    act.wait_ge(S["w_split"], 4)
                act.activation(sr[:, c, :], bank[:, c, :], ACT.Sigmoid).then_inc(S["r_ready"], 1)

            def exps(tau, c):
                b = c % 2
                act.wait_ge(S["gap_ready"], 4 * tau + c + 1)
                for e, shift_by in enumerate((TF, DECAY)):
                    act.activation(above[:, b, e, :], vexp[:, b, 0, :], ACT.Relu, bias=vecs[:, shift_by, c:c + 1]).then_inc(S["lifted"], 1)
                act.wait_ge(S["clamped"], 8 * tau + 2 * c + 2)
                act.activation(below[:, b, :, :], below[:, b, :, :], ACT.Exp).then_inc(S["exped"], 1)
                act.wait_ge(S["lifted"], 8 * tau + 2 * c + 2)
                act.activation(above[:, b, :, :], above[:, b, :, :], ACT.Exp, scale=-1.0).then_inc(S["exped"], 1)

            def recip(tau, c):
                act.wait_ge(S["nd_ready"], 8 * tau + 2 * c + 2)
                act.activation(vexp[:, c % 2, 0, :], above[:, c % 2, 0, :], ACT.Ln).then_inc(S["recip_ln"], 1)
                act.wait_ge(S["recip_ln"], 4 * tau + c + 1)
                act.activation(vexp[:, c % 2, 0, :], vexp[:, c % 2, 0, :], ACT.Exp, scale=-1.0).then_inc(S["recip_ready"], 1)

            def rw_round(tau, c):
                act.wait_ge(S["rw_ready"], 4 * tau + c + 1)
                if has(tau, -1):
                    act.wait_ge(S["out_used"], 4 * (tau - 1) + c + 1)
                act.activation(rw_hi[:, c, :], above[:, c % 2, 1, :], ACT.Copy).then_inc(S["rw_hi_ready"], 1)

            def y_read(bank, tau):
                if last(tau):
                    act.wait_ge(S["ns_ready"], CK * NT)
                elif not (isinstance(tau, int) and tau < 1):
                    act.wait_ge(S["h_stored"], 16 * tau)
                for s in range(ST):
                    act.wait_ge(S["out_used"], 4 * tau + 4)
                    act.activation(y_of(tau)[:, s, :], bank[:, s, :], ACT.Copy, accum_out=y_sum[:, 0, s:s + 1]).then_inc(S["y_ready"], 1)

            def y_squares(bank, tau):
                act.wait_ge(S["y_ready"], ST * (tau + 1))
                act.activation(neg_mean[:, :], y_sum[:, 0, :], ACT.Copy, scale=-1.0 / C).then_inc(S["y_mean"], 1)
                act.wait_ge(S["y_mean"], tau + 1)
                for s in range(ST):
                    act.activation(bank[:, s, :], bank[:, s, :], ACT.Square, bias=neg_mean[:, s:s + 1],
                                   accum_out=y_sum[:, 1, s:s + 1]).then_inc(S["y_squared"], 1)

            def ln3_normalise(tau):
                act.wait_ge(S["ln3_rstd"], 4 * tau + 4)
                for s in range(ST):
                    act.activation(y_of(tau)[:, s, :], xres[:, s, :], ACT.Identity, scale=rstd[:, 2, s:s + 1],
                                   bias=offset[:, 2, s:s + 1]).then_inc(S["h_ready"], 1)

            def exp_table():
                act.preload_act_table_set("natural_log_exp_and_others")

            def ffn_round(q):
                act.wait_ge(S[f"raw_loaded{q}"], 16)
                act.activation((su_hi if q < 2 else sd_hi)[:, (q % 2) * 2048:(q % 2 + 1) * 2048], raw[q], ACT.Copy).then_inc(S["ffn_hi"], 1)

            def h_copy(bank, k, c):
                if not first(k):
                    act.wait_ge(S["logits_done"], k)
                    act.wait_ge(S["h_lo_ready"], CK * k)
                act.wait_ge(S["h_chunk_turned"], CK * k + c + 1)
                act.activation(hT[:, c, :], bank, ACT.Copy).then_inc(S["h_copied"], 1)

            def h_hi(k, c):
                if first(k):
                    act.wait_ge(S["out_used"], CK * (NT - 1) + c + 1)
                else:
                    act.wait_ge(S["up_done"], SJ * k)
                act.wait_ge(S["h_copied"], CK * k + c + 1)
                act.activation(hT_hi[:, c, :], hT[:, c, :], ACT.Copy).then_inc(S["h_hi_ready"], 1)

            def scores(bank, k):
                act.wait_ge(S["logits_done"], k + 1)
                if first(k):
                    act.wait_ge(S["ffn_split"], 1)
                else:
                    act.wait_ge(S["slots_ready"], k)
                act.activation(score, bank[:, 0:ST * E].rearrange("p (s e) -> p s e", s=ST), ACT.Sigmoid).then_inc(S["score_ready"], 1)

            round_weight(0)
            act.wait_ge(S["vec_loaded"], 16)
            act.activation(vecs[:, DECAY, :], vecs[:, TD, :], ACT.Exp).then_inc(S["decay_ready"], 1)
            round_weight(1)
            xnT_read(even, 0, *range(CK))
            for ck in range(CK):
                round_mix(0, KJ, ck)
                if ck == 1:
                    round_weight(2)
            for ck in range(2):
                round_mix(0, VJ, ck)
            round_weight(3)
            k_read(odd, 0, 0)
            for ck in range(2, CK):
                round_mix(0, VJ, ck)
            for ck in range(2):
                round_mix(0, RJ, ck)
            exps(0, 0)
            for c in range(CK):
                v_read(even, 0, c)
            for ck in range(2, CK):
                round_mix(0, RJ, ck)
            xnT_read(even, 1, *range(CK))
            round_mix(1, KJ, 0)
            for c in range(CK):
                r_read(odd, 0, c)
            exp_table()
            for ck in range(1, CK - 1):
                round_mix(1, KJ, ck)

            def period(tau, par):
                here, ahead, behind = has(tau, 0), has(tau, 1), has(tau, -1)

                def rounds(j, *chunks):
                    if ahead:
                        for ck in chunks:
                            round_mix(tau + 1, j, ck)

                if behind:
                    rw_round(tau - 1, 3)
                if last(tau):
                    act.wait_ge(S["mix_used"], 12 * NT)
                    ffn_round(0)
                if here:
                    rounds(KJ, 3)
                    if has(tau, -2) and ahead:
                        ln3_normalise(tau - 2)
                    recip(tau, 0)
                    rounds(VJ, 0)
                    exps(tau, 1)
                    if last(tau):
                        ffn_round(1)
                        ln3_normalise(tau - 2)
                    if ahead:
                        k_read(even, tau + 1, 1 - par)
                    rounds(VJ, 1)
                    rw_round(tau, 0)
                    rounds(VJ, 2)
                else:
                    for c in range(CK):
                        h_hi(0, c)
                        if c == CK - 2:
                            ffn_round(3)
                    y_read(odd, tau - 1)
                if behind and ahead:
                    y_read(odd, tau - 1)
                if here:
                    recip(tau, 1)
                    rounds(VJ, 3)
                    exps(tau, 2)
                    rounds(RJ, 0)
                    if behind and ahead:
                        y_squares(odd, tau - 1)
                    if last(tau):
                        y_read(odd, tau - 1)
                        for c in range(CK):
                            h_copy(even[:, c, :], 0, c)
                    rw_round(tau, 1)
                    rounds(RJ, 1)
                    if ahead:
                        for c in range(2):
                            v_read(even, tau + 1, c)
                    recip(tau, 2)
                    if last(tau):
                        y_squares(odd, tau - 1)
                    rounds(RJ, 2)
                    exps(tau, 3)
                    if ahead:
                        v_read(even, tau + 1, 2)
                    rounds(RJ, 3)
                    if last(tau):
                        scores(turn_bank, 0)
                        exp_table()
                        ffn_round(2)
                    rw_round(tau, 2)
                    if ahead:
                        v_read(even, tau + 1, CK - 1)
                    if has(tau, 2):
                        xnT_read(even, tau + 2, *range(CK - 1))
                    recip(tau, 3)
                if has(tau, 2):
                    xnT_read(even, tau + 2, CK - 1)
                    round_mix(tau + 2, KJ, 0)
                if ahead:
                    exps(tau + 1, 0)
                if has(tau, 2):
                    round_mix(tau + 2, KJ, 1)
                if ahead:
                    for c in range(CK):
                        r_read(odd, tau + 1, c)
                    exp_table()
                if has(tau, 2):
                    round_mix(tau + 2, KJ, 2)

            periods(act, period)

            def hidden(k, j):
                act.wait_ge(S["up_done"], SJ * k + j + 1)
                if first(k) and j == 0:
                    act.wait_ge(S["ffn_split"], 3)
                if not (first(k) and j < 2):
                    act.wait_ge(S["square_ready"], SJ * k + j - 1)
                act.activation(relu[:, j % 2, :], up_bank[:, j % 2, :], ACT.Relu).then_inc(S["relu_ready"], 1)
                act.wait_ge(S["relu_ready"], SJ * k + j + 1)
                if not (first(k) and j < 3):
                    act.wait_ge(S["down_done"], SJ * k + j - (2 if j < 2 else 3) + 1)
                act.activation(s_hi[:, j % 3, :], relu[:, j % 2, :], ACT.Square).then_inc(S["s_hi_ready"], 1)

            def yout_read(k):
                act.wait_ge(S["down_done"], SJ * (k + 1))
                if not first(k):
                    act.wait_ge(S["ysh_stored"], 16 * k)
                for s in range(ST):
                    act.activation(yout[:, s, :], y_bank[:, s, :], ACT.Copy).then_inc(S["yout_ready"], 1)

            def xdT_read(e, q):
                act.wait_ge(S["xd_turned"], e + 1)
                if not (isinstance(e, int) and e < EB):
                    act.wait_ge(S["e_up"], e - EB + 1)
                act.activation(xdT[q].rearrange("p k n -> p (k n)"), banks[0][:, 2 + q % 2, :], ACT.Copy).then_inc(S["xdT_ready"], 1)

            def tile(k):
                for j in range(SJ):
                    if j == 3 and has(k, 1):
                        h_copy(turn_bank, k + 1, 1)
                        h_copy(route_bank, k + 1, 2)
                    hidden(k, j)
                    if first(k) and j == 0:
                        y_squares(y_bank, NT - 1)
                    if j == 4 and (first(k) or second(k)):
                        ln3_normalise(NT - 2 + k)
                    if has(k, 1):
                        if j == 2:
                            h_copy(route_bank, k + 1, 0)
                        if j == 3:
                            h_copy(turn_bank, k + 1, 3)
                        if j == 4:
                            scores(turn_bank, k + 1)
                if has(k, 1):
                    for c in range(CK):
                        h_hi(k + 1, c)
                if last(k):
                    act.wait_ge(S["h_lo_ready"], CK * NT)
                    for e in range(2):
                        xdT_read(e, e)
                yout_read(k)

            tiles(act, tile)

            def e_relu(e, q):
                act.wait_ge(S["e_up"], e + 1)
                if not (isinstance(e, int) and e < 2):
                    act.wait_ge(S["e_square"], e - 1)
                act.activation(e_hidden[q % 2], banks[0][:, q % 2, 0:HID], ACT.Relu).then_inc(S["e_relu"], 1)

            def e_gate(e, q):
                act.wait_ge(S["e_down"], e + 1)
                act.wait_ge(S["scatter_index"], 2 * e + 2)
                if not (isinstance(e, int) and e < EB):
                    act.wait_ge(S["added"], 16 * (e - EB + 1))
                act.activation(e_out[q], banks[1][:, q % 2, :], ACT.Copy, scale=e_gates[:, q:q + 1]).then_inc(S["e_gated"], 1)

            e_relu(0, 0)

            def expert(e, r, n):
                q = r % EB
                if within(e, 2):
                    xdT_read(e + 2, (q + 2) % EB)
                if within(e, 1):
                    e_relu(e + 1, (q + 1) % EB)
                e_gate(e, q)

            experts(act, expert)

            for k in range(NT):
                act.wait_ge(S["ln4_rstd"], 4 * (k + 1))
                for s in range(ST):
                    act.activation(o_y[k][:, s, :], o_y[k][:, s, :], ACT.Identity, scale=rstd[:, o_slot(k), s:s + 1],
                                   bias=offset[:, o_slot(k), s:s + 1]).then_inc(S["o_normed"], 1)

        @block.gpsimd
        def _(pool):
            pool.memset(ident[:, :], 0.0).then_inc(S["ident_ready"], 1)
            pool.memset(neg_half[:, :], -0.5).then_inc(S["half_ready"], 1)
            pool.wait_ge(S["ident_ready"], 1)
            pool.affine_select(out=ident[:, :], in_=ident[:, :], compare_op=ALU.not_equal, fill=1.0, base=0,
                               pattern=[[-1, P]], channel_multiplier=1).then_inc(S["ident_ready"], 1)
            pool.wait_ge(S["half_ready"], 1)

            def ln1_inv_std(tau):
                pool.wait_ge(S["ln1_moments"], ST * (tau + 1))
                pool.sem_inc(S["pool_step"], 1)
                pool.tensor_scalar(rstd[:, 0, :], mv[:, 0, :, 1], EPS, None, ALU.add).then_inc(S["ln1_rstd"], 1)
                pool.wait_ge(S["ln1_rstd"], 2 * tau + 1)
                pool.tensor_tensor(rstd[:, 0, :], rstd[:, 0, :], neg_half[:, :], ALU.pow).then_inc(S["ln1_rstd"], 1)

            def ln3_scale_and_offset(tau):
                pool.wait_ge(S["ln3_moments"], ST * (tau + 1))
                pool.sem_inc(S["pool_step"], 1)
                pool.tensor_scalar(rstd[:, 2, :], mv[:, 2, :, 1], EPS, None, ALU.add).then_inc(S["ln3_rstd"], 1)
                pool.tensor_scalar(offset[:, 2, :], mv[:, 2, :, 0], -1.0, None, ALU.mult).then_inc(S["ln3_rstd"], 1)
                pool.wait_ge(S["ln3_rstd"], 4 * tau + 2)
                pool.tensor_tensor(rstd[:, 2, :], rstd[:, 2, :], neg_half[:, :], ALU.pow).then_inc(S["ln3_rstd"], 1)
                pool.wait_ge(S["ln3_rstd"], 4 * tau + 3)
                pool.tensor_tensor(offset[:, 2, :], offset[:, 2, :], rstd[:, 2, :], ALU.mult).then_inc(S["ln3_rstd"], 1)

            def ln2_inv_std(tau):
                pool.wait_ge(S["y_squared"], ST * (tau + 1))
                pool.sem_inc(S["pool_step"], 1)
                pool.tensor_scalar(rstd[:, 1, :], y_sum[:, 1, :], 1.0 / C, EPS, ALU.mult, ALU.add).then_inc(S["ln2_rstd"], 1)
                pool.wait_ge(S["ln2_rstd"], 2 * tau + 1)
                pool.tensor_tensor(rstd[:, 1, :], rstd[:, 1, :], neg_half[:, :], ALU.pow).then_inc(S["ln2_rstd"], 1)

            def mix_rest(tau, j, ck):
                n = 4 * j + ck
                pool.wait_ge(S["mix_hi_ready"], 12 * tau + n + 1)
                pool.tensor_tensor(mix_lo[:, n % 3, :], mixf[:, n % 2, :], mix_hi[:, n % 3, :].bitcast(F32),
                                   ALU.subtract).then_inc(S["mix_lo_ready"], 1)

            def times_v(tau, c):
                pool.wait_ge(S["exped"], 8 * tau + 2 * c + 1)
                pool.wait_ge(S["v_ready"], 4 * tau + c + 1)
                for e in range(2):
                    ins = pool.tensor_tensor(vexp[:, c % 2, e, :], below[:, c % 2, e, :], v_sb[:, c, :], ALU.mult)
                ins.then_inc(S["vexped"], 1)

            def gated_num(tau, c):
                pool.wait_ge(S["nd_ready"], 8 * tau + 2 * c + 2)
                pool.wait_ge(S["r_ready"], 4 * tau + c + 1)
                pool.tensor_tensor(vexp[:, c % 2, 1, :], above[:, c % 2, 1, :], sr[:, c, :], ALU.mult).then_inc(S["ns_ready"], 1)
                pool.wait_ge(S["ns_ready"], 4 * tau + c + 1)
                pool.wait_ge(S["recip_ready"], 4 * tau + c + 1)
                pool.tensor_tensor(vexp[:, c % 2, 1, :], vexp[:, c % 2, 1, :], vexp[:, c % 2, 0, :], ALU.mult).then_inc(S["a_ready"], 1)

            def rw_rest(tau, c):
                pool.wait_ge(S["rw_hi_ready"], 4 * tau + c + 1)
                pool.tensor_tensor(rw_lo[:, c, :], above[:, c % 2, 1, :], rw_hi[:, c, :].bitcast(F32),
                                   ALU.subtract).then_inc(S["rw_lo_ready"], 1)

            def residual(tau, first_s, last_s):
                pool.wait_ge(S["xres_loaded"], 16 * (tau + 1))
                for s in range(first_s, last_s):
                    pool.wait_ge(S["yn_ready"], ST * tau + s + 1)
                    pool.tensor_tensor(xres[:, s, :], xres[:, s, :], y_of(tau)[:, s, :], ALU.add).then_inc(S["x1_ready"], 1)

            def ffn_rest(q):
                pool.wait_ge(S["ffn_hi"], q + 1)
                pool.wait_ge(S["out_used"], CK * NT)
                part = slice((q - 2) * 2048, (q - 1) * 2048)
                pool.tensor_tensor(sd_lo[:, part], raw[q], sd_hi[:, part].bitcast(F32), ALU.subtract).then_inc(S["ffn_split"], 1)

            def routing_constants():
                pool.wait_ge(S["mix_lo_ready"], 12 * NT)
                pool.sem_inc(S["pool_step"], 1)
                pool.iota(number_i, pattern=[[1, E]], base=0, channel_multiplier=0).then_inc(S["number_made"], 1)
                pool.iota(token_i, pattern=[[P, ST]], base=0, channel_multiplier=1).then_inc(S["number_made"], 1)
                pool.memset(ones, 1.0).then_inc(S["ones_ready"], 1)
                pool.memset(causal, 1.0).then_inc(S["causal_ready"], 1)
                pool.memset(seen, 0.0).then_inc(S["seen_ready"], 1)
                pool.wait_ge(S["causal_ready"], 1)
                pool.affine_select(out=causal, in_=causal, compare_op=ALU.is_gt, fill=0.0, base=0,
                                   pattern=[[1, P]], channel_multiplier=-1).then_inc(S["causal_ready"], 1)

            ln1_inv_std(0)
            for j in (KJ, VJ):
                for ck in range(CK):
                    mix_rest(0, j, ck)
            ln1_inv_std(1)
            for ck in range(CK):
                mix_rest(0, RJ, ck)
            times_v(0, 0)
            pool.wait_ge(S["w_split"], 3)
            pool.memset(hb[:, 0:2, :], 0.0).then_inc(S["blank_ready"], 1)
            pool.wait_ge(S["blank_ready"], 1)
            pool.iota(blank_slots[:, :, TOKEN], pattern=[[0, E]], base=N, channel_multiplier=1,
                      allow_small_or_imprecise_dtypes=True).then_inc(S["blank_ready"], 1)
            mix_rest(1, KJ, 0)
            for ck in range(1, CK - 1):
                mix_rest(1, KJ, ck)

            def period(tau, par):
                here, ahead, behind = has(tau, 0), has(tau, 1), has(tau, -1)

                def rests(j, *chunks):
                    if ahead:
                        for ck in chunks:
                            mix_rest(tau + 1, j, ck)

                if behind:
                    rw_rest(tau - 1, 3)
                if last(tau):
                    routing_constants()
                if here:
                    rests(KJ, 3)
                    gated_num(tau, 0)
                    rests(VJ, 0)
                    times_v(tau, 1)
                    if last(tau):
                        ln3_scale_and_offset(tau - 2)
                    if has(tau, 2):
                        ln1_inv_std(tau + 2)
                    rests(VJ, 1)
                    rw_rest(tau, 0)
                    rests(VJ, 2)
                if behind_all(tau):
                    ffn_rest(2)
                if here:
                    gated_num(tau, 1)
                    rests(VJ, 3)
                    times_v(tau, 2)
                    rests(RJ, 0)
                    rw_rest(tau, 1)
                    rests(RJ, 1)
                if behind and not last(tau):
                    ln2_inv_std(tau - 1)
                if here:
                    gated_num(tau, 2)
                    rests(RJ, 2)
                    if last(tau):
                        ln2_inv_std(tau - 1)
                    times_v(tau, 3)
                    rests(RJ, 3)
                    if last(tau):
                        residual(tau - 1, 0, ST)
                    rw_rest(tau, 2)
                if behind_all(tau):
                    ln3_scale_and_offset(tau - 2)
                    ffn_rest(3)
                if behind and ahead:
                    residual(tau - 1, 0, 1)
                if here:
                    gated_num(tau, 3)
                if last_but_one(tau):
                    times_v(tau + 1, 0)
                if behind and ahead:
                    residual(tau - 1, 1, ST)
                if has(tau, 2):
                    mix_rest(tau + 2, KJ, 0)
                    times_v(tau + 1, 0)
                    mix_rest(tau + 2, KJ, 1)
                    if behind:
                        ln3_scale_and_offset(tau - 1)
                    mix_rest(tau + 2, KJ, 2)

            periods(pool, period)
            pool.wait_ge(S["slots_blank"], 16)

            def tile(k):
                pool.wait_ge(S["slots_ready"], k + 1)
                pool.sem_inc(S["pool_step"], 1)
                for s in range(ST):
                    for c in range(TOPK):
                        pool.indirect_dma_start(t["slots"], bass.IndirectOffsetOnAxis(ap=slot[:, s, c:c + 1], axis=0), choice[:, s, c, :], None,
                                                bounds_check=E * CAP - 1, oob_is_err=False).then_inc(S["scattered"], 16)
                if first(k):
                    residual(NT - 1, 0, ST)
                    ln3_scale_and_offset(NT - 1)

            tiles(pool, tile)

            def gather(e, q):
                pool.wait_ge(S["gather_index"], e + 1)
                if not (isinstance(e, int) and e < EB):
                    pool.wait_ge(S["xd_turned"], e - EB + 1)
                pool.sem_inc(S["pool_step"], 1)
                pool.indirect_dma_start(xd_sb[q], None, t["h"], bass.IndirectOffsetOnAxis(ap=gather_token[:, q:q + 1], axis=0)).then_inc(S[f"xd_loaded{q}"], 16)

            for e in range(EB):
                gather(e, e)

            def expert(e, r, n):
                q = r % EB
                if within(e, EB):
                    gather(e + EB, q)
                pool.wait_ge(S["e_gated"], e + 1)
                pool.wait_ge(S["scatter_index"], 2 * e + 2)
                if first(e):
                    pool.wait_ge(S["ysh_stored"], 16 * NT)
                else:
                    pool.wait_ge(S["added"], 16 * e)
                pool.sem_inc(S["pool_step"], 1)
                pool.indirect_dma_start(t["ysh"], bass.IndirectOffsetOnAxis(ap=scatter_token[:, q:q + 1], axis=0), e_out[q], None,
                                        compute_op=ALU.add).then_inc(S["added"], 16)
                n = e - (E - 2 * (NT - EARLY)) if isinstance(e, int) else -1
                if n >= 0:
                    load_x1(pool, EARLY + n // 2, n % 2)

            experts(pool, expert)

            def o_scale(k):
                w = o_slot(k)
                pool.wait_ge(S["ln4_moments"], ST * (k + 1))
                if k >= 2:
                    pool.wait_ge(S["o_normed"], ST * (k - 1))
                pool.sem_inc(S["pool_step"], 1)
                pool.tensor_scalar(rstd[:, w, :], mv[:, w, :, 1], EPS, None, ALU.add).then_inc(S["ln4_rstd"], 1)
                pool.tensor_scalar(offset[:, w, :], mv[:, w, :, 0], -1.0, None, ALU.mult).then_inc(S["ln4_rstd"], 1)
                pool.wait_ge(S["ln4_rstd"], 4 * k + 2)
                pool.tensor_tensor(rstd[:, w, :], rstd[:, w, :], neg_half[:, :], ALU.pow).then_inc(S["ln4_rstd"], 1)
                pool.wait_ge(S["ln4_rstd"], 4 * k + 3)
                pool.tensor_tensor(offset[:, w, :], offset[:, w, :], rstd[:, w, :], ALU.mult).then_inc(S["ln4_rstd"], 1)

            def o_add(k):
                pool.wait_ge(S[f"x1_loaded{k}"], 32)
                for s in range(ST // 2):
                    pool.wait_ge(S["o_normed"], ST * k + s + 1)
                    pool.tensor_tensor(o_y[k][:, s, :], o_y[k][:, s, :], o_x[k][:, s, :], ALU.add).then_inc(S["o_ready"], 1)

            for k in range(NT):
                o_scale(k)
                if k >= 1:
                    o_add(k - 1)
            o_add(NT - 1)

        @block.vector
        def _(dve):
            def split_weight(j):
                dve.wait_ge(S["w_hi"], j + 1)
                hi = W(j, 0).bitcast(F32)
                if j == 3:
                    dve.scalar_tensor_tensor(out=W(j, 1), in0=stage[j % 2][:, :, :], scalar=-1.0, in1=hi,
                                             op0=ALU.mult, op1=ALU.subtract).then_inc(S["w_split"], 1)
                else:
                    dve.tensor_tensor(W(j, 1), stage[j % 2][:, :, :], hi, ALU.subtract).then_inc(S["w_split"], 1)
                if j == 0:
                    dve.wait_ge(S["decay_ready"], 1)
                    dve.tensor_scalar(vecs[:, NEGW, :], vecs[:, DECAY, :], -1.0, None, ALU.mult).then_inc(S["decay_ready"], 1)

            def moments(ln, src, tau):
                for s in range(ST):
                    dve.bn_stats(stats[:, s, :], src[:, s, :]).then_inc(S[f"ln{ln}_stats"], 1)
                dve.wait_ge(S[f"ln{ln}_stats"], ST * (tau + 1))
                dve.sem_inc(S["dve_step"], 1)
                for s in range(ST):
                    dve.bn_aggr(mv[:, ln - 1, s, :], stats[:, s, :]).then_inc(S[f"ln{ln}_moments"], 1)

            def ln1_moments(tau):
                dve.wait_ge(S["x_loaded"], 16 * (tau + 1))
                moments(1, xin, tau)

            def ln1_normalise(tau):
                dve.wait_ge(S["ln1_rstd"], 2 * tau + 2)
                for s in range(ST):
                    dve.tensor_scalar(xin[:, s, :], xin[:, s, :], mv[:, 0, s, 0:1], rstd[:, 0, s:s + 1],
                                      ALU.subtract, ALU.mult).then_inc(S["xn_ready"], 1)

            def shift(tau, par):
                if par == 0:
                    if not (isinstance(tau, int) and tau < 1):
                        dve.wait_ge(S["mixed"], 12 * tau)
                    dve.memset(xnT[:, :, 0:1], 0.0).then_inc(S["shift_ready"], 1)
                else:
                    dve.wait_ge(S["xnT_ready"], 4 * tau)
                    dve.wait_ge(S["mixed"], 12 * tau)
                    dve.tensor_copy(xnT[:, :, 0:1], xnT[:, :, TT:TT + 1]).then_inc(S["shift_ready"], 1)

            def diff(tau, ck):
                dve.wait_ge(S["xnT_ready"], 4 * tau + ck + 1)
                dve.tensor_tensor(xnd[:, ck, :], xnT[:, ck, 1:TT + 1], xnT[:, ck, 0:TT],
                                  ALU.subtract).then_inc(S["diff_ready"], 1)

            def mix(tau, j, ck):
                n = 4 * j + ck
                if j == KJ:
                    dve.wait_ge(S["diff_ready"], 4 * tau + ck + 1)
                if not (isinstance(tau, int) and 12 * tau + n < 2):
                    dve.wait_ge(S["mix_lo_ready"], 12 * tau + n - 1)
                dve.scalar_tensor_tensor(out=mixf[:, n % 2, :], in0=xnd[:, ck, :], scalar=vecs[:, MK + j, ck:ck + 1],
                                         in1=xnT[:, ck, 0:TT], op0=ALU.mult, op1=ALU.add).then_inc(S["mixed"], 1)

            def gaps(tau, par, c):
                b = c % 2
                u = 4 * tau + c
                if par == 0:
                    dve.memset(run_max[:, b, 0:1], NEG_BIG).then_inc(S["seeded"], 1)
                    dve.memset(state[:, b, :, 0:1], 0.0).then_inc(S["seeded"], 1)
                else:
                    dve.wait_ge(S["carried"], 2 * (u - CK) + 2)
                    dve.tensor_copy(run_max[:, b, 0:1], carry[:, c, 0:1]).then_inc(S["seeded"], 1)
                    dve.tensor_copy(state[:, b, :, 0:1], carry[:, c, 1:3].rearrange("p (a o) -> p a o", o=1)).then_inc(S["seeded"], 1)
                dve.wait_ge(S["seeded"], 2 * u + 2)
                dve.wait_ge(S["k_ready"], u + 1)
                dve.tensor_tensor_scan(run_max[:, b, 1:TT + 1], vecs[:, NEGW, c:c + 1].to_broadcast([P, TT]), k_sb[:, par, c, :],
                                       run_max[:, b, 0:1], ALU.add, ALU.max).then_inc(S["max_scanned"], 1)
                dve.wait_ge(S["max_scanned"], u + 1)
                if not (isinstance(tau, int) and 4 * tau + c < 2):
                    dve.wait_ge(S["rw_lo_ready"], u - 1)
                dve.tensor_tensor(vexp[:, b, 0, :], k_sb[:, par, c, :], run_max[:, b, 0:TT], ALU.subtract).then_inc(S["gap_ready"], 1)
                dve.tensor_copy(carry[:, c, 0:1], run_max[:, b, TT:TT + 1]).then_inc(S["carried"], 1)
                dve.wait_ge(S["gap_ready"], u + 1)
                for e, shift_by in enumerate((TF, DECAY)):
                    dve.tensor_scalar(below[:, b, e, :], vexp[:, b, 0, :], vecs[:, shift_by, c:c + 1], 0.0,
                                      ALU.add, ALU.min).then_inc(S["clamped"], 1)

            def scans(tau, c):
                b = c % 2
                u = 4 * tau + c
                dve.wait_ge(S["vexped"], u + 1)
                dve.wait_ge(S["exped"], 2 * u + 2)
                for e, add in ((0, vexp[:, b, 1, :]), (1, below[:, b, 1, :])):
                    dve.tensor_tensor_scan(state[:, b, e, 1:TT + 1], above[:, b, 1, :], add, state[:, b, e, 0:1],
                                           ALU.mult, ALU.add).then_inc(S["scanned"], 1)
                dve.wait_ge(S["scanned"], 2 * u + 2)
                dve.tensor_tensor(above[:, b, 1, :], above[:, b, 0, :], state[:, b, 0, 0:TT], ALU.mult).then_inc(S["scaled"], 1)
                dve.tensor_copy(carry[:, c, 1:3].rearrange("p (a o) -> p a o", o=1), state[:, b, :, TT:TT + 1]).then_inc(S["carried"], 1)
                dve.wait_ge(S["scaled"], 2 * u + 1)
                dve.tensor_tensor(above[:, b, 0, :], above[:, b, 0, :], state[:, b, 1, 0:TT], ALU.mult).then_inc(S["scaled"], 1)
                dve.tensor_tensor(above[:, b, 1, :], above[:, b, 1, :], vexp[:, b, 0, :], ALU.add).then_inc(S["nd_ready"], 1)
                dve.wait_ge(S["scaled"], 2 * u + 2)
                dve.tensor_tensor(above[:, b, 0, :], above[:, b, 0, :], below[:, b, 0, :], ALU.add).then_inc(S["nd_ready"], 1)

            def refine(tau, c):
                b = c % 2
                u = 4 * tau + c
                dve.wait_ge(S["recip_ready"], u + 1)
                dve.tensor_tensor(above[:, b, 0, :], above[:, b, 0, :], vexp[:, b, 0, :], ALU.mult).then_inc(S["resid_ready"], 1)
                dve.wait_ge(S["resid_ready"], u + 1)
                dve.wait_ge(S["a_ready"], u + 1)
                dve.scalar_tensor_tensor(out=above[:, b, 1, :], in0=above[:, b, 0, :], scalar=2.0, in1=vexp[:, b, 1, :],
                                         op0=ALU.subtract, op1=ALU.mult).then_inc(S["rw_ready"], 1)

            def ln2_normalise(tau):
                dve.wait_ge(S["ln2_rstd"], 2 * tau + 2)
                for s in range(ST):
                    dve.tensor_scalar(y_of(tau)[:, s, :], y_of(tau)[:, s, :], neg_mean[:, s:s + 1], rstd[:, 1, s:s + 1],
                                      ALU.add, ALU.mult).then_inc(S["yn_ready"], 1)

            def ln3(tau):
                dve.wait_ge(S["x1_ready"], ST * (tau + 1))
                if last(tau):
                    dve.wait_ge(S["h_ready"], ST * (NT - 1))
                moments(3, xres, tau)

            def ffn_rest(q):
                dve.wait_ge(S["ffn_hi"], q + 1)
                part = slice(q * 2048, (q + 1) * 2048)
                dve.tensor_tensor(su_lo[:, part], raw[q], su_hi[:, part].bitcast(F32), ALU.subtract).then_inc(S["ffn_split"], 1)

            def h_rest(k, c):
                dve.wait_ge(S["h_hi_ready"], CK * k + c + 1)
                dve.tensor_tensor(hT_lo[:, c, :], hT[:, c, :], hT_hi[:, c, :].bitcast(F32), ALU.subtract).then_inc(S["h_lo_ready"], 1)

            PICKED, CHOSEN, STEPS = 57, 58, 69
            steps = {"base": 0, "done": 0}

            def step(ins):
                ins.then_inc(S["route_step"], 1)
                steps["done"] += 1

            def settled(own=False):
                dve.wait_ge(S["route_step"], steps["base"] + steps["done"])
                if own:
                    dve.sem_inc(S["dve_step"], 1)

            def over(x, shape):
                return x.to_broadcast([P] + shape)

            def groups(k):
                steps.update(base=STEPS * k, done=0)
                dve.wait_ge(S["score_ready"], k + 1)
                if first(k):
                    dve.wait_ge(S["bias_loaded"], 16)
                step(dve.tensor_tensor(biased, score, over(bias_row.rearrange("p (o e) -> p o e", o=1), [ST, E]), ALU.add))
                settled(own=True)
                for s in range(ST):
                    for g in range(GROUPS):
                        step(dve.max(group_top[:, s * GROUPS + g, :], biased[:, s, g * EG:(g + 1) * EG]))
                settled()
                step(dve.tensor_tensor(group_score.rearrange("p s g -> p (s g)"), group_top[:, :, 0], group_top[:, :, 1], ALU.add))
                settled(own=True)
                for s in range(ST):
                    step(dve.max(group_best[:, s, :], group_score[:, s, :]))
                settled(own=True)
                for s in range(ST):
                    step(dve.max_index(group_index[:, s, :], group_best[:, s, :], group_score[:, s, :]))

            def group_experts(k):
                settled()
                step(dve.tensor_copy(group_number, group_index))
                settled()
                step(dve.tensor_tensor(group_hot, over(number[:, 0:GROUPS].rearrange("p (o q g) -> p o q g", o=1, q=1), [ST, TOPG, GROUPS]),
                                       over(group_number[:, :, 0:TOPG].rearrange("p s (k o) -> p s k o", o=1), [ST, TOPG, GROUPS]), ALU.is_equal))
                settled()
                step(dve.tensor_reduce(group_mask, group_hot.rearrange("p s k g -> p s g k"), AX.X, ALU.add))
                settled()
                step(dve.tensor_scalar(group_floor, group_mask, 1.0, LOWEST, ALU.subtract, ALU.mult))
                over_experts = [over(m.rearrange("p s g -> p (s g)").rearrange("p (n o) -> p n o", o=1), [ST * GROUPS, EG]) for m in (group_mask, group_floor)]
                by_group = biased.rearrange("p s (g e) -> p (s g) e", g=GROUPS)
                step(dve.tensor_tensor(by_group, by_group, over_experts[0], ALU.mult))
                settled()
                step(dve.tensor_tensor(by_group, by_group, over_experts[1], ALU.add))
                settled(own=True)
                for s in range(ST):
                    step(dve.max(expert_best[:, s, :], biased[:, s, :]))
                settled(own=True)
                for s in range(ST):
                    step(dve.max_index(expert_index[:, s, :], expert_best[:, s, :], biased[:, s, :]))
                settled()
                step(dve.tensor_copy(expert_number, expert_index))
                assert steps["done"] == PICKED, steps

            def experts_chosen(k):
                steps.update(base=STEPS * k, done=PICKED)
                settled()
                step(dve.tensor_tensor(hot, over(number.rearrange("p (o q e) -> p o q e", o=1, q=1), [ST, TOPK, E]),
                                       over(expert_number[:, :, 0:TOPK].rearrange("p s (k o) -> p s k o", o=1), [ST, TOPK, E]), ALU.is_equal))
                settled()
                if not first(k):
                    dve.wait_ge(S["pos_ready"], k)
                with nc.allow_low_precision(reason="a sum of one-hots that differ: 0 or 1"):
                    dve.tensor_reduce(sel, hot.rearrange("p s k e -> p s e k"), AX.X, ALU.add).then_inc(S["sel_ready"], 1)
                assert steps["done"] == CHOSEN, steps

            def counted(k, bank):
                steps.update(base=STEPS * k, done=CHOSEN)
                dve.wait_ge(S["pos_ready"], k + 1)
                if first(k):
                    dve.wait_ge(S["rw_lo_ready"], CK * NT)
                pos = bank[:, 0:ST * E].rearrange("p (s o e) -> p s o e", s=ST, o=1)
                dve.tensor_tensor(product, hot, over(pos, [ST, TOPK, E]), ALU.mult).then_inc(S["placed"], 1)
                dve.wait_ge(S["sel_ready"], k + 1)
                step(dve.tensor_reduce(sel_sum, sel.rearrange("p s e -> p e s"), AX.X, ALU.add))
                dve.wait_ge(S["placed"], k + 1)
                step(dve.tensor_reduce(place, product, AX.X, ALU.add))
                settled()
                dve.tensor_tensor(seen, seen, sel_sum, ALU.add).then_inc(S["seen_ready"], 1)

            def gates_and_slots(k):
                step(dve.tensor_tensor(product, hot, over(score.rearrange("p s (o e) -> p s o e", o=1), [ST, TOPK, E]), ALU.mult))
                settled()
                step(dve.tensor_reduce(weight, product, AX.X, ALU.add))
                settled()
                step(dve.tensor_reduce(weight_sum, weight, AX.X, ALU.add))
                settled()
                step(dve.tensor_scalar(weight_sum, weight_sum, 1e-20, None, ALU.add))
                settled()
                step(dve.reciprocal(weight_sum, weight_sum))
                settled()
                if not first(k):
                    dve.wait_ge(S["scattered"], 16 * TOPK * ST * k)
                step(dve.scalar_tensor_tensor(out=choice[:, :, :, GATE], in0=weight, scalar=ROUTE_SCALE,
                                              in1=over(weight_sum.rearrange("p (s o) -> p s o", o=1), [ST, TOPK]), op0=ALU.mult, op1=ALU.mult))
                step(dve.tensor_copy(choice[:, :, :, TOKEN], over(token.rearrange("p (s o) -> p s o", o=1), [ST, TOPK])))
                step(dve.scalar_tensor_tensor(out=slot_f, in0=place, scalar=float(E), in1=expert_number[:, :, 0:TOPK], op0=ALU.mult, op1=ALU.add))
                settled()
                dve.tensor_copy(slot, slot_f).then_inc(S["slots_ready"], 1)
                step(dve.tensor_scalar(token, token, float(TT), None, ALU.add))
                assert steps["done"] == STEPS, steps

            ln1_moments(0)
            ln1_normalise(0)
            shift(0, 0)
            for j in range(2):
                split_weight(j)
            for ck in range(CK):
                diff(0, ck)
                mix(0, KJ, ck)
                if ck == 2:
                    split_weight(2)
            for ck in range(CK):
                mix(0, VJ, ck)
                if ck == 1:
                    split_weight(3)
            ln1_moments(1)
            mix(0, RJ, 0)
            gaps(0, 0, 0)
            mix(0, RJ, 1)
            ln1_normalise(1)
            for ck in range(2, CK):
                mix(0, RJ, ck)
            shift(1, 1)
            for ck in range(CK - 1):
                diff(1, ck)
                mix(1, KJ, ck)
            diff(1, CK - 1)

            def period(tau, par):
                here, ahead, behind = has(tau, 0), has(tau, 1), has(tau, -1)

                def mixes(j, *chunks):
                    if ahead:
                        for ck in chunks:
                            mix(tau + 1, j, ck)

                if behind:
                    refine(tau - 1, 3)
                if behind_all(tau):
                    for c in range(CK - 1):
                        h_rest(0, c)
                if here:
                    mixes(KJ, 3)
                    scans(tau, 0)
                    mixes(VJ, 0)
                    gaps(tau, par, 1)
                    if last(tau):
                        ln3(tau - 2)
                    if has(tau, 2):
                        ln1_moments(tau + 2)
                    mixes(VJ, 1)
                    refine(tau, 0)
                    if last(tau):
                        ffn_rest(0)
                    mixes(VJ, 2)
                    scans(tau, 1)
                    mixes(VJ, 3)
                    gaps(tau, par, 2)
                    mixes(RJ, 0)
                else:
                    group_experts(0)
                    h_rest(0, CK - 1)
                    experts_chosen(0)
                if here:
                    refine(tau, 1)
                    if last(tau):
                        ffn_rest(1)
                    mixes(RJ, 1)
                    if has(tau, 2):
                        ln1_normalise(tau + 2)
                    scans(tau, 2)
                    mixes(RJ, 2)
                    gaps(tau, par, 3)
                    mixes(RJ, 3)
                    if has(tau, 2):
                        shift(tau + 2, par)
                    refine(tau, 2)
                    if behind:
                        ln2_normalise(tau - 1)
                    if last(tau):
                        dve.wait_ge(S["number_made"], 2)
                        dve.tensor_copy(number, number_i).then_inc(S["number_ready"], 1)
                        dve.tensor_copy(token, token_i).then_inc(S["token_ready"], 1)
                        dve.wait_ge(S["number_ready"], 1)
                        dve.wait_ge(S["token_ready"], 1)
                    scans(tau, 3)
                    if last(tau):
                        groups(0)
                    if has(tau, 2):
                        diff(tau + 2, 0)
                        mix(tau + 2, KJ, 0)
                    if ahead:
                        gaps(tau + 1, 1 - par, 0)
                    if has(tau, 2):
                        for ck in range(1, CK - 1):
                            diff(tau + 2, ck)
                            mix(tau + 2, KJ, ck)
                        diff(tau + 2, CK - 1)
                    if behind and has(tau, 2):
                        ln3(tau - 1)

            periods(dve, period)

            def split(k, j):
                dve.wait_ge(S["relu_ready"], SJ * k + j + 1)
                dve.tensor_tensor(square[:, j % 2, :], relu[:, j % 2, :], relu[:, j % 2, :], ALU.mult).then_inc(S["square_ready"], 1)
                dve.wait_ge(S["square_ready"], SJ * k + j + 1)
                dve.wait_ge(S["s_hi_ready"], SJ * k + j + 1)
                dve.tensor_tensor(s_lo[:, j % 3, :], square[:, j % 2, :], s_hi[:, j % 3, :].bitcast(F32), ALU.subtract).then_inc(S["s_lo_ready"], 1)

            def index_gather(e, q):
                if not (isinstance(e, int) and e < EB):
                    dve.wait_ge(S["xd_turned"], e - EB + 1)
                    dve.sem_inc(S["dve_step"], 1)
                dve.tensor_copy(gather_token[:, q:q + 1], column(e, TOKEN)).then_inc(S["gather_index"], 1)

            def index_scatter(e, q):
                if not (isinstance(e, int) and e < EB):
                    dve.wait_ge(S["added"], 16 * (e - EB + 1))
                    dve.sem_inc(S["dve_step"], 1)
                dve.tensor_copy(scatter_token[:, q:q + 1], column(e, TOKEN)).then_inc(S["scatter_index"], 1)
                dve.tensor_copy(e_gates[:, q:q + 1], column(e, GATE)).then_inc(S["scatter_index"], 1)

            def column(e, which):
                return table[:, bass.ds(e, 1), which]

            def e_square(e, q):
                dve.wait_ge(S["e_relu"], e + 1)
                if not (isinstance(e, int) and e < 2):
                    dve.wait_ge(S["e_down"], e - 1)
                dve.tensor_tensor(e_act[q % 2].rearrange("p k n -> p (k n)"), e_hidden[q % 2], e_hidden[q % 2], ALU.mult).then_inc(S["e_square"], 1)

            def tile(k):
                for j in range(SJ):
                    if first(k) and j == 1:
                        counted(0, turn_bank)
                        ln3(NT - 2)
                    split(k, j)
                    if first(k):
                        if j == 2:
                            ln2_normalise(NT - 1)
                    if second(k) and j == 2:
                        ln3(NT - 1)
                    if has(k, 1):
                        if j == 1:
                            if not first(k):
                                counted(k, turn_bank)
                            gates_and_slots(k)
                        if j == 5:
                            groups(k + 1)
                        if j == 6:
                            group_experts(k + 1)
                        if j == 7:
                            experts_chosen(k + 1)
                    if last(k) and j == SJ - 2:
                        dve.wait_ge(S["table_loaded"], 16)
                        for e in range(EB):
                            index_gather(e, e)
                if has(k, 1):
                    for c in range(CK):
                        h_rest(k + 1, c)
                if last_but_one(k):
                    counted(k + 1, turn_bank)
                    gates_and_slots(k + 1)

            tiles(dve, tile)

            index_scatter(0, 0)
            e_square(0, 0)

            def expert(e, r, n):
                q = r % EB
                if within(e, 1):
                    e_square(e + 1, (q + 1) % EB)
                    index_scatter(e + 1, (q + 1) % EB)
                if within(e, EB):
                    index_gather(e + EB, q)

            experts(dve, expert)

            def o_moments(k):
                dve.wait_ge(S[f"ysh_loaded{k}"], 16)
                if k >= 1:
                    dve.wait_ge(S["ln4_moments"], ST * k)
                if k >= 2:
                    dve.wait_ge(S["ln4_rstd"], 4 * (k - 1))
                for s in range(ST):
                    dve.bn_stats(stats[:, s, :], o_y[k][:, s, :]).then_inc(S["ln4_stats"], 1)
                dve.wait_ge(S["ln4_stats"], ST * (k + 1))
                for s in range(ST):
                    dve.bn_aggr(mv[:, o_slot(k), s, :], stats[:, s, :]).then_inc(S["ln4_moments"], 1)

            def o_add(k):
                dve.wait_ge(S[f"x1_loaded{k}"], 32)
                for s in range(ST // 2, ST):
                    dve.wait_ge(S["o_normed"], ST * k + s + 1)
                    dve.tensor_tensor(o_y[k][:, s, :], o_y[k][:, s, :], o_x[k][:, s, :], ALU.add).then_inc(S["o_added"], 1)

            for k in range(NT):
                o_moments(k)
                if k >= 1:
                    o_add(k - 1)
            o_add(NT - 1)


def kernel(**inputs):
    import numpy as _np
    import concourse.bacc as _bacc
    from concourse import mybir as _mybir
    from concourse.bass_utils import run_bass_kernel_spmd as _run

    def by_partition(w, chunks):
        return _np.ascontiguousarray(w.reshape(chunks, P, -1).transpose(1, 0, 2))

    g = {n: _np.asarray(a) for n, a in inputs.items()}
    vecs = [g["L0_attn_time_decay"], g["L0_attn_time_first"], g["L0_attn_time_mix_k"], g["L0_attn_time_mix_v"], g["L0_attn_time_mix_r"]]
    arrays = {
        "x": _np.ascontiguousarray(g["L0_attn_x"].reshape(N, C)),
        "vecs": _np.ascontiguousarray(_np.stack([v.reshape(CK, P).T for v in vecs], axis=1)),
        "Wk": by_partition(g["L0_attn_Wk"].T, CK),
        "Wv": by_partition(g["L0_attn_Wv"].T, CK),
        "Wr": by_partition(g["L0_attn_Wr"].T, CK),
        "Wo": by_partition(g["L0_attn_Wo"].T, CK),
        "gate": by_partition(g["L0_ffn_gate_w"].T, CK).reshape(P, CK * E),
        "e_bias": g["L0_ffn_e_bias"].reshape(1, E),
        "su": by_partition(g["L0_ffn_shared_up_w"].T, CK).reshape(P, 2, -1),
        "sd": by_partition(g["L0_ffn_shared_down_w"].T, SJ).reshape(P, 2, -1),
        "w1": _np.ascontiguousarray(g["L0_ffn_w1"].transpose(0, 2, 1).reshape(E, CK, P, HID).transpose(0, 2, 1, 3)).reshape(E, P, CK * HID),
        "w2": _np.ascontiguousarray(g["L0_ffn_w2"].transpose(0, 2, 1).reshape(E, IK, P, C).transpose(0, 2, 1, 3)).reshape(E, P, IK * C),
    }
    nc = _bacc.Bacc("TRN2", target_bir_lowering=False, num_devices=1)
    aps = {n: nc.dram_tensor(f"in_{n}", a.shape, _mybir.dt.from_np(a.dtype), kind="ExternalInput").ap() for n, a in arrays.items()}
    scratch = {"x1": (N, C), "h": (N + P, C), "ysh": (N + P, C), "slots": (E * CAP, 2)}
    aps.update({n: nc.dram_tensor(n, shape, F32, kind="Internal").ap() for n, shape in scratch.items()})
    aps["out"] = nc.dram_tensor("out", (N, C), F32, kind="ExternalOutput").ap()
    sandwich(nc, aps)
    r = _run(nc, [{f"in_{n}": a for n, a in arrays.items()}], core_ids=[0])
    return r.results[0]["out"].reshape(B, T, C)
```
